# Optimizing a Trainium2 kernel written in Bass

```python
import numpy as np
import jax
import jax.numpy as jnp

def _softmax(x, axis=-1):
    return jax.nn.softmax(x, axis=axis)

def _gelu(x):
    return jax.nn.gelu(x, approximate=True)

def _silu(x):
    return jax.nn.silu(x)

def _sigmoid(x):
    return jax.nn.sigmoid(x)

def _layernorm(x, axis=-1, eps=1e-05):
    m = jnp.mean(x, axis=axis, keepdims=True)
    v = jnp.var(x, axis=axis, keepdims=True)
    return (x - m) / jnp.sqrt(v + eps)

def _scatter_add(tgt, idx, src, axis=0):
    return tgt.at[idx].add(src)

def _segment_sum(src, seg, n):
    return jax.ops.segment_sum(src, seg, n)
kernel_name = 'mk_gnn_preln_d4_gnn_r32_d20f0c'

def setup_inputs(seed: int=0):
    np.random.seed(seed)
    _w = jnp.asarray

    def _rec_inputs():
        import jax
        import jax.numpy as jnp
        _gk = jax.random.key(seed)
        x = -0.000202 + 1 * jax.random.normal(jax.random.fold_in(_gk, 1), (3125, 64), jnp.float32)
        _s = jax.random.randint(jax.random.fold_in(_gk, 2), (25000,), 0, 3125, jnp.int32)
        _d = jax.random.randint(jax.random.fold_in(_gk, 3), (25000,), 0, 3125, jnp.int32)
        _loop = jnp.arange(3125, dtype=jnp.int32)
        src = jnp.concatenate([_s, _d, _loop])
        dst = jnp.concatenate([_d, _s, _loop])
        _o = jnp.argsort(dst, stable=True)
        src = src[_o]
        dst = dst[_o]
        edge_attr_16 = 0.000254156 + 0.999948 * jax.random.normal(jax.random.fold_in(_gk, 11), (53125, 16), jnp.float32)
        edge_attr_64 = 1.36993e-05 + 0.999972 * jax.random.normal(jax.random.fold_in(_gk, 12), (53125, 64), jnp.float32)
        edge_attr_9 = 0.000739051 + 0.999958 * jax.random.normal(jax.random.fold_in(_gk, 13), (53125, 9), jnp.float32)
        edge_type_8 = jax.random.randint(jax.random.fold_in(_gk, 15), (53125,), 0, 8, jnp.int32)
        return (x, src, dst, edge_attr_16, edge_attr_64, edge_attr_9, edge_type_8)
    x, src, dst, edge_attr_16, edge_attr_64, edge_attr_9, edge_type_8 = _rec_inputs()

    def _L0_gnn_setup():
        import jax, jax.numpy as jnp
        import numpy as np
        N_NODES = 3125
        N_EDGES = 31250
        DIM = 64
        NUM_REL = 8
        HIDDEN = 64
        key = jax.random.key(seed)
        k_v, k_e, k_r, k_w1, k_w2 = jax.random.split(key, 5)
        V = jax.random.normal(k_v, (N_NODES, DIM), dtype=jnp.float32)
        edge_index = jax.random.randint(k_e, (2, N_EDGES), 0, N_NODES, dtype=jnp.int64)
        rel_ids = jax.random.randint(k_r, (N_EDGES,), 0, NUM_REL, dtype=jnp.int64)
        W1 = jax.random.normal(k_w1, (2 * DIM + NUM_REL, HIDDEN), dtype=jnp.float32) * 0.05
        b1 = jnp.zeros((HIDDEN,), dtype=jnp.float32)
        W2 = jax.random.normal(k_w2, (HIDDEN, DIM), dtype=jnp.float32) * 0.05
        b2 = jnp.zeros((DIM,), dtype=jnp.float32)
        return {'V': V, 'edge_index': edge_index, 'rel_ids': rel_ids, 'W1': W1, 'b1': b1, 'W2': W2, 'b2': b2}
    _L0_gnn_all = _L0_gnn_setup()
    _L0_gnn_in = {k: v for k, v in _L0_gnn_all.items() if k in ('W1', 'b1', 'W2', 'b2')}
    del _L0_gnn_all

    def _L1_gnn_setup():
        import jax, jax.numpy as jnp
        import numpy as np
        N, E = (50000, 25000)
        EMB, HEADS, EDGE_DIM = (64, 4, 16)
        NEG_SLOPE = 0.2
        LN_EPS = 1e-05
        key = jax.random.key(seed)
        ks = jax.random.split(key, 12)
        HC = HEADS * EMB
        inp = {'x': jax.random.normal(ks[0], (N, EMB), jnp.float32), 'edge_index': jax.random.randint(ks[1], (2, E), 0, N, jnp.int32), 'edge_attr': jax.random.normal(ks[2], (E, EDGE_DIM), jnp.float32), 'W': jax.random.normal(ks[3], (EMB, HC), jnp.float32) * 0.1, 'W_edge': jax.random.normal(ks[4], (EDGE_DIM, HC), jnp.float32) * 0.1, 'att_src': jax.random.normal(ks[5], (HEADS, EMB), jnp.float32) * 0.1, 'att_dst': jax.random.normal(ks[6], (HEADS, EMB), jnp.float32) * 0.1, 'att_edge': jax.random.normal(ks[7], (HEADS, EMB), jnp.float32) * 0.1, 'bias': jnp.zeros((HC,), jnp.float32), 'Wp': jax.random.normal(ks[8], (HC, EMB), jnp.float32) * 0.05, 'bp': jnp.zeros((EMB,), jnp.float32), 'gamma': jnp.ones((EMB,), jnp.float32), 'beta': jnp.zeros((EMB,), jnp.float32)}
        return inp
    _L1_gnn_all = _L1_gnn_setup()
    _L1_gnn_in = {k: v for k, v in _L1_gnn_all.items() if k in ('W', 'W_edge', 'att_src', 'att_dst', 'att_edge', 'bias', 'Wp', 'bp', 'gamma', 'beta')}
    del _L1_gnn_all

    def _L2_gnn_setup():
        import jax, jax.numpy as jnp
        import numpy as np
        N = 3125
        E = 50000
        IN_C = 64
        HID_C = 64
        key = jax.random.key(seed)
        k1, k2, k3, k4 = jax.random.split(key, 4)
        x = jax.random.normal(k1, (N, IN_C), dtype=jnp.float32)
        edge_index = jax.random.randint(k2, (2, E), 0, N, dtype=jnp.int64)
        W = jax.random.normal(k3, (HID_C, IN_C), dtype=jnp.float32) / np.sqrt(IN_C)
        b = jax.random.normal(k4, (HID_C,), dtype=jnp.float32) * 0.01
        return {'x': x, 'edge_index': edge_index, 'W': W, 'b': b}
    _L2_gnn_all = _L2_gnn_setup()
    _L2_gnn_in = {k: v for k, v in _L2_gnn_all.items() if k in ('W', 'b')}
    del _L2_gnn_all

    def _L3_gnn_setup():
        import jax, jax.numpy as jnp
        import numpy as np
        N, E = (10000, 10000)
        D, S, HE = (64, 9, 64)
        H, DQK, DV = (8, 16, 16)
        OK, OV = (H * DQK, H * DV)
        EPS_BN = 1e-05

        def tensor_product(x_e, sh, w, C):
            acc = sh[:, 0:1] * (x_e @ C[:, 0, :])
            for s in range(1, S):
                acc = acc + sh[:, s:s + 1] * (x_e @ C[:, s, :])
            return acc * w

        def mlp2(x, w1, b1, w2, b2):
            return jax.nn.relu(x @ w1 + b1) @ w2 + b2
        key = jax.random.key(seed)
        ks = jax.random.split(key, 20)
        g = lambda k, shape, fan: jax.random.normal(k, shape, jnp.float32) / np.float32(np.sqrt(fan))
        return {'tfn_features': jax.random.normal(ks[0], (N, D), jnp.float32), 'edge_features': jax.random.normal(ks[1], (E, HE), jnp.float32), 'edge_sh': jax.random.normal(ks[2], (E, S), jnp.float32), 'Wq': g(ks[3], (D, OK), D), 'Cqk': g(ks[4], (D, S, OK), D * S), 'Cv': g(ks[5], (D, S, OV), D * S), 'k_w1': g(ks[6], (HE, HE), HE), 'k_b1': jnp.zeros((HE,), jnp.float32), 'k_w2': g(ks[7], (HE, OK), HE), 'k_b2': jnp.zeros((OK,), jnp.float32), 'v_w1': g(ks[8], (HE, HE), HE), 'v_b1': jnp.zeros((HE,), jnp.float32), 'v_w2': g(ks[9], (HE, OV), HE), 'v_b2': jnp.zeros((OV,), jnp.float32), 'W_out': g(ks[10], (OV, D), OV), 'W_self': g(ks[11], (D, D), D), 'gamma': jnp.ones((D,), jnp.float32), 'beta': jnp.zeros((D,), jnp.float32), 'edge_index': jax.random.randint(ks[12], (2, E), 0, N, dtype=jnp.int32)}
    _L3_gnn_all = _L3_gnn_setup()
    _L3_gnn_in = {k: v for k, v in _L3_gnn_all.items() if k in ('Wq', 'Cqk', 'Cv', 'k_w1', 'k_b1', 'k_w2', 'k_b2', 'v_w1', 'v_b1', 'v_w2', 'v_b2', 'W_out', 'W_self', 'gamma', 'beta')}
    del _L3_gnn_all
    return {'x': x, 'src': src, 'dst': dst, 'edge_attr_16': edge_attr_16, 'edge_attr_64': edge_attr_64, 'edge_attr_9': edge_attr_9, 'edge_type_8': edge_type_8, 'L0_gnn_W1': _L0_gnn_in['W1'], 'L0_gnn_b1': _L0_gnn_in['b1'], 'L0_gnn_W2': _L0_gnn_in['W2'], 'L0_gnn_b2': _L0_gnn_in['b2'], 'L1_gnn_W': _L1_gnn_in['W'], 'L1_gnn_W_edge': _L1_gnn_in['W_edge'], 'L1_gnn_att_src': _L1_gnn_in['att_src'], 'L1_gnn_att_dst': _L1_gnn_in['att_dst'], 'L1_gnn_att_edge': _L1_gnn_in['att_edge'], 'L1_gnn_bias': _L1_gnn_in['bias'], 'L1_gnn_Wp': _L1_gnn_in['Wp'], 'L1_gnn_bp': _L1_gnn_in['bp'], 'L1_gnn_gamma': _L1_gnn_in['gamma'], 'L1_gnn_beta': _L1_gnn_in['beta'], 'L2_gnn_W': _L2_gnn_in['W'], 'L2_gnn_b': _L2_gnn_in['b'], 'L3_gnn_Wq': _L3_gnn_in['Wq'], 'L3_gnn_Cqk': _L3_gnn_in['Cqk'], 'L3_gnn_Cv': _L3_gnn_in['Cv'], 'L3_gnn_k_w1': _L3_gnn_in['k_w1'], 'L3_gnn_k_b1': _L3_gnn_in['k_b1'], 'L3_gnn_k_w2': _L3_gnn_in['k_w2'], 'L3_gnn_k_b2': _L3_gnn_in['k_b2'], 'L3_gnn_v_w1': _L3_gnn_in['v_w1'], 'L3_gnn_v_b1': _L3_gnn_in['v_b1'], 'L3_gnn_v_w2': _L3_gnn_in['v_w2'], 'L3_gnn_v_b2': _L3_gnn_in['v_b2'], 'L3_gnn_W_out': _L3_gnn_in['W_out'], 'L3_gnn_W_self': _L3_gnn_in['W_self'], 'L3_gnn_gamma': _L3_gnn_in['gamma'], 'L3_gnn_beta': _L3_gnn_in['beta']}

def reference(x, src, dst, edge_attr_16, edge_attr_64, edge_attr_9, edge_type_8, L0_gnn_W1, L0_gnn_b1, L0_gnn_W2, L0_gnn_b2, L1_gnn_W, L1_gnn_W_edge, L1_gnn_att_src, L1_gnn_att_dst, L1_gnn_att_edge, L1_gnn_bias, L1_gnn_Wp, L1_gnn_bp, L1_gnn_gamma, L1_gnn_beta, L2_gnn_W, L2_gnn_b, L3_gnn_Wq, L3_gnn_Cqk, L3_gnn_Cv, L3_gnn_k_w1, L3_gnn_k_b1, L3_gnn_k_w2, L3_gnn_k_b2, L3_gnn_v_w1, L3_gnn_v_b1, L3_gnn_v_w2, L3_gnn_v_b2, L3_gnn_W_out, L3_gnn_W_self, L3_gnn_gamma, L3_gnn_beta):
    import jax
    import jax.numpy as jnp

    def _L0_gnn_ref(V, edge_index, rel_ids, W1, b1, W2, b2):
        import jax, jax.numpy as jnp
        import numpy as np
        N_NODES = 3125
        N_EDGES = 31250
        DIM = 64
        NUM_REL = 8
        HIDDEN = 64
        src = edge_index[0]
        dst = edge_index[1]
        src_h = V[src]
        dst_h = V[dst]
        rel_onehot = jax.nn.one_hot(rel_ids, NUM_REL, dtype=V.dtype)
        edge_feat = jnp.concatenate([src_h, dst_h, rel_onehot], axis=-1)
        h = jax.nn.relu(edge_feat @ W1 + b1)
        msg = h @ W2 + b2
        out = jax.ops.segment_sum(msg, dst, num_segments=V.shape[0])
        return V + out

    def _L1_gnn_ref(x, edge_index, edge_attr, W, W_edge, att_src, att_dst, att_edge, bias, Wp, bp, gamma, beta):
        import jax, jax.numpy as jnp
        import numpy as np
        N, E = (50000, 25000)
        EMB, HEADS, EDGE_DIM = (64, 4, 16)
        NEG_SLOPE = 0.2
        LN_EPS = 1e-05
        n = x.shape[0]
        H, C = att_src.shape
        xw = (x @ W).reshape(n, H, C)
        a_src_n = jnp.einsum('nhc,hc->nh', xw, att_src)
        a_dst_n = jnp.einsum('nhc,hc->nh', xw, att_dst)
        src, dst = (edge_index[0], edge_index[1])
        loop = jnp.arange(n, dtype=edge_index.dtype)
        cnt = jax.ops.segment_sum(jnp.ones_like(dst, jnp.float32), dst, num_segments=n)
        loop_attr = jax.ops.segment_sum(edge_attr, dst, num_segments=n) / jnp.maximum(cnt, 1.0)[:, None]
        src2 = jnp.concatenate([src, loop])
        dst2 = jnp.concatenate([dst, loop])
        ea = jnp.concatenate([edge_attr, loop_attr], axis=0)
        ew = (ea @ W_edge).reshape(-1, H, C)
        a_edge = jnp.einsum('ehc,hc->eh', ew, att_edge)
        alpha = a_src_n[src2] + a_dst_n[dst2] + a_edge
        alpha = jnp.where(alpha >= 0, alpha, NEG_SLOPE * alpha)
        amax = jax.ops.segment_max(alpha, dst2, num_segments=n)
        ae = jnp.exp(alpha - amax[dst2])
        denom = jax.ops.segment_sum(ae, dst2, num_segments=n)
        attn = ae / denom[dst2]
        msg = xw[src2] * attn[:, :, None]
        agg = jax.ops.segment_sum(msg, dst2, num_segments=n)
        gat_out = agg.reshape(n, H * C) + bias
        proj = gat_out @ Wp + bp
        h = x + jax.nn.elu(proj)
        mu = jnp.mean(h, axis=-1, keepdims=True)
        var = jnp.mean((h - mu) ** 2, axis=-1, keepdims=True)
        out = (h - mu) * jax.lax.rsqrt(var + LN_EPS) * gamma + beta
        return out

    def _L2_gnn_ref(x, edge_index, W, b):
        import jax, jax.numpy as jnp
        import numpy as np
        N = 3125
        E = 50000
        IN_C = 64
        HID_C = 64
        n = x.shape[0]
        loop = jnp.arange(n, dtype=edge_index.dtype)
        row = jnp.concatenate([edge_index[0], loop])
        col = jnp.concatenate([edge_index[1], loop])
        ones = jnp.ones(col.shape[0], dtype=x.dtype)
        deg = jax.ops.segment_sum(ones, col, num_segments=n)
        dis = jnp.where(deg > 0, jax.lax.rsqrt(deg), 0.0)
        norm = dis[row] * dis[col]
        h = x @ W.T
        msg = norm[:, None] * h[row]
        out = jax.ops.segment_sum(msg, col, num_segments=n) + b
        return jax.nn.relu(out)

    def _L3_gnn_ref(tfn_features, edge_features, edge_sh, Wq, Cqk, Cv, k_w1, k_b1, k_w2, k_b2, v_w1, v_b1, v_w2, v_b2, W_out, W_self, gamma, beta, edge_index):
        import jax, jax.numpy as jnp
        import numpy as np
        N, E = (10000, 10000)
        D, S, HE = (64, 9, 64)
        H, DQK, DV = (8, 16, 16)
        OK, OV = (H * DQK, H * DV)
        EPS_BN = 1e-05

        def tensor_product(x_e, sh, w, C):
            acc = sh[:, 0:1] * (x_e @ C[:, 0, :])
            for s in range(1, S):
                acc = acc + sh[:, s:s + 1] * (x_e @ C[:, s, :])
            return acc * w

        def mlp2(x, w1, b1, w2, b2):
            return jax.nn.relu(x @ w1 + b1) @ w2 + b2
        edge_dst, edge_src = (edge_index[0], edge_index[1])
        n = tfn_features.shape[0]
        q = (tfn_features @ Wq).reshape(n, H, DQK)
        x_dst = tfn_features[edge_dst]
        wk = mlp2(edge_features, k_w1, k_b1, k_w2, k_b2)
        wv = mlp2(edge_features, v_w1, v_b1, v_w2, v_b2)
        k = tensor_product(x_dst, edge_sh, wk, Cqk).reshape(-1, H, DQK)
        v = tensor_product(x_dst, edge_sh, wv, Cv).reshape(-1, H, DV)
        attn = jnp.einsum('ehd,ehd->eh', q[edge_src], k)
        amax = jax.ops.segment_max(attn, edge_src, num_segments=n)
        ex = jnp.exp(attn - amax[edge_src])
        denom = jax.ops.segment_sum(ex, edge_src, num_segments=n)
        alpha = ex / (denom[edge_src] + 1e-16)
        upd = jax.ops.segment_sum(v * alpha[..., None], edge_src, num_segments=n)
        upd = upd.reshape(n, OV) @ W_out
        out = tfn_features @ W_self + upd
        mu = out.mean(axis=0)
        var = out.var(axis=0)
        return (out - mu) * jax.lax.rsqrt(var + EPS_BN) * gamma + beta
    edge_index = jnp.stack([src, dst])
    h = jnp.maximum(_layernorm(x, axis=-1), 0.0)
    x = x + _L0_gnn_ref(h, edge_index, edge_type_8, L0_gnn_W1, L0_gnn_b1, L0_gnn_W2, L0_gnn_b2)
    h = jnp.maximum(_layernorm(x, axis=-1), 0.0)
    x = x + _L1_gnn_ref(h, edge_index, edge_attr_16, L1_gnn_W, L1_gnn_W_edge, L1_gnn_att_src, L1_gnn_att_dst, L1_gnn_att_edge, L1_gnn_bias, L1_gnn_Wp, L1_gnn_bp, L1_gnn_gamma, L1_gnn_beta)
    h = jnp.maximum(_layernorm(x, axis=-1), 0.0)
    x = x + _L2_gnn_ref(h, edge_index, L2_gnn_W, L2_gnn_b)
    h = jnp.maximum(_layernorm(x, axis=-1), 0.0)
    x = x + _L3_gnn_ref(h, edge_attr_64, edge_attr_9, L3_gnn_Wq, L3_gnn_Cqk, L3_gnn_Cv, L3_gnn_k_w1, L3_gnn_k_b1, L3_gnn_k_w2, L3_gnn_k_b2, L3_gnn_v_w1, L3_gnn_v_b1, L3_gnn_v_w2, L3_gnn_v_b2, L3_gnn_W_out, L3_gnn_W_self, L3_gnn_gamma, L3_gnn_beta, edge_index)
    return x

_drawn_inputs = setup_inputs


def setup_inputs(seed=0):
    import zlib

    import numpy as np

    out = dict(_drawn_inputs(seed))
    spreads = {'L0_gnn_b1': (0.0, 0.1),
     'L0_gnn_b2': (0.0, 0.1),
     'L1_gnn_bias': (0.0, 0.1),
     'L1_gnn_bp': (0.0, 0.1),
     'L1_gnn_gamma': (1.0, 0.2),
     'L1_gnn_beta': (0.0, 0.1),
     'L3_gnn_k_b1': (0.0, 0.434),
     'L3_gnn_k_b2': (0.0, 0.365),
     'L3_gnn_v_b1': (0.0, 0.582),
     'L3_gnn_v_b2': (0.0, 0.455),
     'L3_gnn_gamma': (1.0, 0.2),
     'L3_gnn_beta': (0.0, 0.407)}
    factors = {'edge_attr_16': 8.0,
     'L1_gnn_W_edge': 7.877,
     'L1_gnn_att_src': 30.051,
     'L1_gnn_att_dst': 64.0,
     'L1_gnn_att_edge': 8.0,
     'L2_gnn_b': 23.002}
    for name, (base, spread) in spreads.items():
        noise = np.random.default_rng([zlib.crc32(name.encode()), seed]).standard_normal(out[name].shape)
        drawn = base * np.exp(spread * noise) if base else spread * noise
        out[name] = jnp.asarray(drawn.astype(out[name].dtype))
    for name, factor in factors.items():
        out[name] = (out[name] * factor).astype(out[name].dtype)
    return out
```

```python
from contextlib import ExitStack

import concourse.bass as bass
from concourse import mybir

F32 = mybir.dt.float32
BF16 = mybir.dt.bfloat16
I32 = mybir.dt.int32
ALU = mybir.AluOpType
ACT = mybir.ActivationFunctionType
AX = mybir.AxisListType

N = 3125
D = 64
E = 53125
PN = 125
NJ = N // PN
W = 128
NT = -(-E // (32 * W)) * 32
EP = NT * W
GT = 4
UG = 8
UT = GT * UG
NI = NT // UT
NW = N + W
REL = 8
EPS = 1e-5
SLOPE = 0.2
BIG = 1e30
GCOL = 128
LAST = "L3"
STAGES = ["L0", "L1", "L2", "L3"]


def wait(eng, sem, value):
    if not isinstance(value, int) or value > 0:
        eng.wait_ge(sem, value)


class Chain:

    def __init__(self, eng, sem):
        self.eng, self.sem, self.n = eng, sem, 0

    def mark(self, ins):
        self.n += 1
        ins.then_inc(self.sem, 1)

    def link(self, ins):
        self.mark(ins)
        self.eng.wait_ge(self.sem, self.n)


class LoopChain:

    def __init__(self, eng, sem, i, steps):
        self.eng, self.sem, self.at, self.k, self.steps = eng, sem, i * steps, 0, steps

    def link(self, ins):
        self.mark(ins)
        self.eng.wait_ge(self.sem, self.at + self.k)

    def mark(self, ins):
        self.k += 1
        ins.then_inc(self.sem, 1)

    def done(self):
        assert self.k == self.steps, (self.k, self.steps)


def rounds(n, k):
    return [(a, min(k, n - a)) for a in range(0, n, k)]


def build(nc, A, out):
    with ExitStack() as ctx:
        def sb(name, shape, dt=F32):
            return ctx.enter_context(nc.sbuf_tensor(name, shape, dt))

        layer = ExitStack()
        sems = []

        def tmp(name, shape, dt=F32):
            return layer.enter_context(nc.sbuf_tensor(name, shape, dt))

        def sem(name):
            sems.append(nc.alloc_semaphore(name=name))
            return sems[-1]

        def end_of_layer():
            layer.close()
            nc.clear_and_free_semaphores(sems)
            sems.clear()
            nc.all_engine_barrier()

        def dram(name, shape, dt=F32):
            return nc.dram_tensor(name, shape, dt, kind="Internal").ap()

        bank = [ctx.enter_context(nc.psum_tensor(f"bank{b}", [128, 512], F32)) for b in range(8)]

        X = sb("X", [PN, NJ, D])
        H = sb("H", [PN, NJ, D])
        HT = sb("HT", [D, N])
        acc = sb("acc", [128, 3, NW])
        ident = sb("ident", [128, 128])
        iota_row = sb("iota_row", [128, 128])
        iota_i = sb("iota_i", [128, 128], I32)
        iota_p = sb("iota_p", [128, 1])
        iota_pi = sb("iota_pi", [128, 1], I32)
        src_i = sb("src_i", [128, NT], I32)
        dst_i = sb("dst_i", [128, NT], I32)
        base_i = sb("base_i", [128, NT], I32)
        dloc = sb("dloc", [128, NT])
        base_f = sb("base_f", [128, NT])
        edge_a = sb("edge_a", [128, NT, 4])
        st = sb("st", [PN, 8, NJ])
        cnt = sb("cnt", [PN, NJ])
        zero = sb("zero", [128, 256])
        idx = sb("idx", [128, UT], I32)

        loop_a = sb("loop_a", [PN, NJ, 4])

        w1 = sb("w1", [D, 2, D])
        w1r = sb("w1r", [REL, D])
        b1r = sb("b1r", [REL, D])
        w2x = sb("w2x", [D + 5, D + 5])
        wedge = sb("wedge", [16, 4, 64])
        atte = sb("atte", [16, 4, 64])
        v16 = sb("v16", [16, 4])

        s_done = {}

        TA = dram("TA", [N, D])
        TB = dram("TB", [NW, D])

        l_x, l_i, l_w0 = sem("l_x"), sem("l_i"), sem("l_w0")
        c_pool, c_dve, c_zero = sem("c_pool"), sem("c_dve"), sem("c_zero")
        l_zero = sem("l_zero")
        with nc.Block() as block:
            @block.sync
            def _(sp):
                sp.dma_start(X[:], A["x"].rearrange("(j p) f -> p j f", p=PN)).then_inc(l_x, 16)
                sp.dma_start(src_i[:], A["src"]).then_inc(l_i, 16)
                sp.dma_start(dst_i[:], A["dst"]).then_inc(l_i, 16)
                sp.dma_start(base_i[:], A["dst"][0:1, :].partition_broadcast(128)).then_inc(l_i, 16)
                w1d = A["L0_gnn_W1"]
                sp.dma_start(w1[:], w1d[0:2 * D, :].rearrange("(a k) n -> k a n", a=2)).then_inc(l_w0, 16)
                sp.dma_start(w1r[:], w1d[2 * D:2 * D + REL, :]).then_inc(l_w0, 16)
                sp.dma_start(b1r[:], A["L0_gnn_b1"].partition_broadcast(REL)).then_inc(l_w0, 16)
                sp.wait_ge(c_zero, 1)
                sp.dma_start(w2x[0:D, 0:D], A["L0_gnn_W2"]).then_inc(l_w0, 16)
                sp.dma_start(w2x[D:D + 1, 0:D], A["L0_gnn_b2"]).then_inc(l_w0, 16)
                sp.dma_start(wedge[:], A["L1_gnn_W_edge"].rearrange("k (h c) -> k h c", h=4)).then_inc(l_w0, 16)
                sp.dma_start(atte[:], A["L1_gnn_att_edge"].partition_broadcast(16)).then_inc(l_w0, 16)
                sp.wait_ge(c_dve, 2)
                sp.dma_start(TB[N:NW, :], zero[:, 0:D]).then_inc(l_zero, 16)
                sp.wait_ge(l_zero, 16)
                sp.wait_ge(l_x, 16)
                sp.wait_ge(l_i, 48)
                sp.wait_ge(l_w0, 7 * 16)

            @block.gpsimd
            def _(pool):
                pool.memset(w2x[:], 0.0).then_inc(c_pool, 1)
                pool.memset(ident[:], 0.0).then_inc(c_pool, 1)
                pool.iota(iota_i[:], [[1, 128]], 0, 0).then_inc(c_pool, 1)
                pool.iota(iota_pi[:], [[0, 1]], 0, 1).then_inc(c_pool, 1)
                pool.wait_ge(c_pool, 4)
                pool.affine_select(out=ident[:], in_=ident[:], compare_op=ALU.not_equal, fill=1.0, base=0,
                                   pattern=[[-1, 128]], channel_multiplier=1).then_inc(c_pool, 1)
                pool.affine_select(out=w2x[:, D:D + 5], in_=w2x[:, D:D + 5], compare_op=ALU.not_equal, fill=1.0,
                                   base=-D, pattern=[[-1, 5]], channel_multiplier=1).then_inc(c_zero, 1)

            @block.vector
            def _(dve):
                c = Chain(dve, c_dve)
                c.mark(dve.memset(acc[:], 0.0))
                c.mark(dve.memset(zero[:], 0.0))
                dve.wait_ge(c_pool, 4)
                c.mark(dve.tensor_copy(iota_row[:], iota_i[:]))
                c.mark(dve.tensor_copy(iota_p[:], iota_pi[:]))
                dve.wait_ge(l_i, 48)
                c.mark(dve.tensor_copy(dloc[:], dst_i[:]))
                c.link(dve.tensor_copy(base_f[:], base_i[:]))
                c.mark(dve.tensor_tensor(dloc[:], dloc[:], base_f[:], ALU.subtract))
                dve.wait_ge(l_w0, 7 * 16)
                c.mark(dve.tensor_tensor(w1r[:], w1r[:], b1r[:], ALU.add))
                c.link(dve.tensor_tensor(wedge[:], wedge[:], atte[:], ALU.mult))
                c.mark(dve.tensor_reduce(v16[:], wedge[:], AX.X, ALU.add))

        def node_buffers(p):
            return tmp(p + "_XC", [PN, NJ, D]), tmp(p + "_yn", [PN, NJ, D]), tmp(p + "_tab", [PN, NJ, 2 * D])

        def ln_relu_steps(c, s_var, s_std, n, dst=H, src=X, relu=True, XC=None):
            dve = c.eng
            bc = lambda r: st[:, r, :].unsqueeze(2).to_broadcast([PN, NJ, D])
            c.link(dve.tensor_reduce(st[:, 0, :], src[:], AX.X, ALU.add))
            c.link(dve.tensor_scalar(st[:, 1, :], st[:, 0, :], -1.0 / D, None, ALU.mult))
            c.link(dve.tensor_tensor(XC[:], src[:], bc(1), ALU.add))
            c.link(dve.tensor_tensor(dst[:], XC[:], XC[:], ALU.mult))
            c.link(dve.tensor_reduce(st[:, 2, :], dst[:], AX.X, ALU.add))
            dve.tensor_scalar(st[:, 3, :], st[:, 2, :], 1.0 / D, EPS, ALU.mult, ALU.add).then_inc(s_var, 1)
            dve.wait_ge(s_std, n)
            c.link(dve.reciprocal(st[:, 5, :], st[:, 4, :]))
            c.link(dve.tensor_tensor(dst[:], XC[:], bc(5), ALU.mult))
            if relu:
                c.link(dve.tensor_scalar(dst[:], dst[:], 0.0, None, ALU.max))

        def ln_std_step(act, s_var, s_std, n):
            act.wait_ge(s_var, n)
            act.activation(st[:, 4, :], st[:, 3, :], ACT.Sqrt).then_inc(s_std, 1)

        def transpose_steps(pe, s_t, s_free, src=H):
            for r, (j0, n) in enumerate(rounds(NJ, 4)):
                if r >= 2:
                    pe.wait_ge(s_free, r - 1)
                for j in range(n):
                    last = pe.transpose(bank[r % 2][0:D, j * PN:(j + 1) * PN], src[:, j0 + j, :], ident[0:PN, 0:PN])
                last.then_inc(s_t, 1)

        def transposed_copy_steps(act, s_t, s_free, dst=HT):
            for r, (j0, n) in enumerate(rounds(NJ, 4)):
                act.wait_ge(s_t, r + 1)
                act.activation(dst[0:D, j0 * PN:(j0 + n) * PN], bank[r % 2][0:D, 0:n * PN], ACT.Copy).then_inc(s_free, 1)

        def gather_program(ga, pool, table, width, s_g, s_used, s_idx, s_step, ring=UG, per=1):
            def half(i, hh):
                for k in range(hh * 4, hh * 4 + 4):
                    wait(pool, s_g[k], i * 64)
                pool.tensor_copy(idx[:, hh * 16:hh * 16 + 16], src_i[:, bass.ds(i * UT + hh * 16, 16)]).then_inc(s_idx, 1)
                pool.wait_ge(s_idx, i * 2 + (hh + 1))
                pool.sem_inc(s_step, 1)
                for k in range(hh * 4, hh * 4 + 4):
                    if not isinstance(i, int) or k >= ring:
                        pool.wait_ge(s_used, (i * UG + (k - ring + 1)) * per)
                        pool.sem_inc(s_step, 1)
                    for t in range(GT):
                        o = ga[:, (k % ring) * GT + t, 0:width]
                        pool.indirect_dma_start(o, None, table, bass.IndirectOffsetOnAxis(
                            ap=idx[:, k * GT + t:k * GT + t + 1], axis=0)).then_inc(s_g[k], 16)
            for hh in range(2):
                half(0, hh)
            with pool.Fori(1, NI) as i:
                for hh in range(2):
                    half(i, hh)

        def each_group(eng, body):
            for k in range(UG):
                body(0, k)
            with eng.Fori(1, NI) as i:
                for k in range(UG):
                    body(i, k)

        def before(i, k):
            if k:
                return i, k - 1
            return None if isinstance(i, int) and i == 0 else (i - 1, UG - 1)

        def back(i, k, n):
            if k >= n:
                return i, k - n
            return None if isinstance(i, int) and i == 0 else (i - 1, UG + k - n)

        def base_of(eng, i, k, t):
            return eng.value_load(base_i[0:1, bass.ds(i * UT + (k * GT + t), 1)], min_val=0, max_val=N - 1)

        def window_loads(win, sp, i, k, table, width, s_w, s_used):
            if not isinstance(i, int) or i > 0:
                sp.wait_ge(s_used, (i - 1) * UG + (k + 1))
            for t in range(GT):
                b = base_of(sp, i, k, t)
                sp.dma_start(win[:, k * GT + t, 0:width], table[bass.ds(b, W), :]).then_inc(s_w[k], 16)

        def one_hot_step(one, dve, i, k, s_one):
            dve.tensor_tensor(one[:, (k % 2) * GT:(k % 2 + 1) * GT, :], iota_row[:].unsqueeze(1).to_broadcast([128, GT, 128]),
                              dloc[:, bass.ds(i * UT + k * GT, GT)].unsqueeze(2).to_broadcast([128, GT, 128]),
                              ALU.is_equal).then_inc(s_one, 1)

        def one_hot_ring_step(one, dve, i, k, s_one):
            dve.tensor_tensor(one[:, k * GT:(k + 1) * GT, :], iota_row[:].unsqueeze(1).to_broadcast([128, GT, 128]),
                              dloc[:, bass.ds(i * UT + k * GT, GT)].unsqueeze(2).to_broadcast([128, GT, 128]),
                              ALU.is_equal).then_inc(s_one, 1)

        n0_dve, n0_var, n0_std, n0_t, n0_tc, n0_m, n0_mc, n0_o = [sem("n0_" + x) for x in
            ("dve", "var", "std", "t", "tc", "m", "mc", "o")]
        XC, yn, tab = node_buffers("n0")
        with nc.Block() as block:
            @block.vector
            def _(dve):
                c = Chain(dve, n0_dve)
                ln_relu_steps(c, n0_var, n0_std, 1, XC=XC)

            @block.scalar
            def _(act):
                ln_std_step(act, n0_var, n0_std, 1)
                transposed_copy_steps(act, n0_t, n0_tc)
                for r, (j0, n) in enumerate(rounds(NJ, 4)):
                    act.wait_ge(n0_m, r + 1)
                    act.activation(tab[:, j0:j0 + n, :], bank[2 + r % 2][0:PN, 0:n * 128].rearrange("p (j f) -> p j f", j=n),
                                   ACT.Copy).then_inc(n0_mc, 1)

            @block.tensor
            def _(pe):
                pe.wait_ge(n0_dve, 8)
                transpose_steps(pe, n0_t, n0_tc)
                for r, (j0, n) in enumerate(rounds(NJ, 4)):
                    pe.wait_ge(n0_tc, r + 1)
                    if r >= 2:
                        pe.wait_ge(n0_mc, r - 1)
                    for j in range(n):
                        last = pe.matmul(bank[2 + r % 2][0:PN, j * 128:(j + 1) * 128], HT[:, (j0 + j) * PN:(j0 + j + 1) * PN],
                                         w1[:].rearrange("k a n -> k (a n)"), start=True, stop=True)
                    last.then_inc(n0_m, 1)

            @block.sync
            def _(sp):
                sp.wait_ge(n0_mc, len(rounds(NJ, 4)))
                sp.dma_start(TA.rearrange("(j p) f -> p j f", p=PN), tab[:, :, 0:D]).then_inc(n0_o, 16)
                sp.dma_start(TB[0:N, :].rearrange("(j p) f -> p j f", p=PN), tab[:, :, D:2 * D]).then_inc(n0_o, 16)
                sp.wait_ge(n0_o, 32)

        layer.close()

        e0_g = [sem(f"e0_g{k}") for k in range(UG)]
        e0_w = [sem(f"e0_w{k}") for k in range(UG)]
        e0_e = [sem(f"e0_e{k}") for k in range(2)]
        (e0_used, e0_idx, e0_step, e0_one, e0_T, e0_oT, e0_rel, e0_P, e0_pre, e0_ms, e0_S, e0_acc,
         e0_wused) = [sem("e0_" + x) for x in ("used", "idx", "step", "one", "T", "oT", "rel", "P", "pre", "ms", "S", "acc", "wused")]
        ga = tmp("ga0", [128, UT, D])
        win = tmp("win0", [128, UT, D])
        one = tmp("one0", [128, UT, 128])
        oneT = tmp("oneT0", [128, 2, GT, 128])
        rel_i = tmp("rel_i", [REL, 2, GT * W], I32)
        ea = tmp("ea", [16, 2, GT * W])
        relT = tmp("relT", [REL, 2, GT * W])
        pre = tmp("pre", [128, 2, GT, D])
        msg = tmp("msg", [128, 2, GT, D + 5])
        MS = D + 5
        e0_ones = sem("e0_ones")
        with nc.Block() as block:
            @block.gpsimd
            def _(pool):
                pool.memset(msg[:, :, :, D:D + 1], 1.0).then_inc(e0_ones, 1)
                gather_program(ga, pool, TA, D, e0_g, e0_used, e0_idx, e0_step)

            @block.sync
            def _(sp):
                def body(i, k):
                    window_loads(win, sp, i, k, TB, D, e0_w, e0_wused)
                each_group(sp, body)

            @block.scalar
            def _(act):
                def loads(i, k):
                    wait(act, e0_P, i * UG + (k - 1))
                    wait(act, e0_rel, i * UG + (k - 1))
                    cols = bass.ds((i * UG + k) * GT * W, GT * W)
                    act.dma_start(rel_i[:, k % 2, :], A["rel"][:, cols].partition_broadcast(REL)).then_inc(e0_e[k % 2], 16)
                    act.dma_start(ea[:, k % 2, :], A["ea16"][:, cols]).then_inc(e0_e[k % 2], 16)

                def body(i, k):
                    loads(i, k)
                    g = i * UG + k
                    act.wait_ge(e0_T, g + 1)
                    wait(act, e0_P, g - 1)
                    act.activation(oneT[:, k % 2], bank[k % 2][:].rearrange("p (t n) -> p t n", t=GT), ACT.Copy).then_inc(e0_oT, 1)
                    act.wait_ge(e0_pre, g + 1)
                    wait(act, e0_S, g - 1)
                    act.activation(msg[:, k % 2, :, 0:D], pre[:, k % 2], ACT.Relu).then_inc(e0_ms, 1)
                    P = bank[2 + k % 2][:, 0:GT * (D + 4)].rearrange("p (t f) -> p t f", t=GT)
                    act.activation(msg[:, k % 2, :, D + 1:MS], P[:, :, D:D + 4], ACT.Copy).then_inc(e0_ms, 1)
                    act.activation(edge_a[:, bass.ds(g * GT, GT), :], P[:, :, D:D + 4], ACT.Copy).then_inc(e0_ms, 1)
                act.wait_ge(e0_ones, 1)
                each_group(act, body)

            @block.tensor
            def _(pe):
                def sums(i, k):
                    g = i * UG + k
                    pe.wait_ge(e0_ms, g * 3 + 3)
                    wait(pe, e0_acc, (g - 1) * GT)
                    for t in range(GT):
                        last = pe.matmul(bank[4 + k % 2][0:MS, t * 128:(t + 1) * 128], msg[:, k % 2, t, :], one[:, (k % 2) * GT + t, :],
                                         start=True, stop=True)
                    last.then_inc(e0_S, 1)

                def body(i, k):
                    g = i * UG + k
                    pe.wait_ge(e0_one, g + 1)
                    wait(pe, e0_oT, g - 1)
                    for t in range(GT):
                        last = pe.transpose(bank[k % 2][:, t * 128:(t + 1) * 128], one[:, (k % 2) * GT + t, :], ident[:])
                    last.then_inc(e0_T, 1)
                    if before(i, k):
                        sums(*before(i, k))
                    pe.wait_ge(e0_oT, g + 1)
                    pe.wait_ge(e0_rel, g + 1)
                    pe.wait_ge(e0_w[k], i * 64 + 64)
                    wait(pe, e0_ms, (g - 1) * 3)
                    for t in range(GT):
                        o = t * (D + 4)
                        P = bank[2 + k % 2]
                        pe.matmul(P[:, o:o + D], oneT[:, k % 2, t, :], win[:, k * GT + t, 0:D], start=True, stop=False)
                        pe.matmul(P[:, o:o + D], relT[:, k % 2, t * W:(t + 1) * W], w1r[:], start=False, stop=True)
                        last = pe.matmul(P[:, o + D:o + D + 4], ea[:, k % 2, t * W:(t + 1) * W], v16[:], start=True, stop=True)
                    last.then_inc(e0_P, 1)
                each_group(pe, body)
                sums(NI - 1, UG - 1)

            @block.vector
            def _(dve):
                def add_sums(i, k):
                    g = i * UG + k
                    dve.wait_ge(e0_S, g + 1)
                    for t in range(GT):
                        b = base_of(dve, i, k, t)
                        wait(dve, e0_acc, g * GT + t)
                        a = acc[0:MS, 0, bass.ds(b, W)]
                        dve.tensor_tensor(a, a, bank[4 + k % 2][0:MS, t * 128:(t + 1) * 128], ALU.add).then_inc(e0_acc, 1)

                def body(i, k):
                    g = i * UG + k
                    wait(dve, e0_S, g - 1)
                    one_hot_step(one, dve, i, k, e0_one)
                    dve.wait_ge(e0_e[k % 2], i * (UG // 2 * 32) + (k // 2 + 1) * 32)
                    dve.tensor_scalar(relT[:, k % 2, :], rel_i[:, k % 2, :], iota_p[0:REL, 0:1], None, ALU.is_equal).then_inc(e0_rel, 1)
                    if before(i, k):
                        add_sums(*before(i, k))
                    dve.wait_ge(e0_P, g + 1)
                    dve.wait_ge(e0_g[k], i * 64 + 64)
                    wait(dve, e0_ms, (g - 1) * 3)
                    P = bank[2 + k % 2][:, 0:GT * (D + 4)].rearrange("p (t f) -> p t f", t=GT)
                    dve.tensor_tensor(pre[:, k % 2], ga[:, k * GT:(k + 1) * GT, 0:D], P[:, :, 0:D], ALU.add).then_inc(e0_pre, 1)
                    dve.wait_ge(e0_pre, g + 1)
                    dve.sem_inc(e0_used, 1)
                    dve.sem_inc(e0_wused, 1)
                each_group(dve, body)
                add_sums(NI - 1, UG - 1)

        layer.close()
        m0_m, m0_dve, m0_c, m0_f = [sem("m0_" + x) for x in ("m", "dve", "c", "f")]
        with nc.Block() as block:
            @block.tensor
            def _(pe):
                for r, (j0, n) in enumerate(rounds(NJ, 4)):
                    if r >= 2:
                        pe.wait_ge(m0_f, r - 1)
                    for j in range(n):
                        last = pe.matmul(bank[r % 2][0:PN, j * 128:j * 128 + MS], acc[0:MS, 0, (j0 + j) * PN:(j0 + j + 1) * PN],
                                         w2x[:], start=True, stop=True)
                    last.then_inc(m0_m, 1)

            @block.vector
            def _(dve):
                c = Chain(dve, m0_dve)
                c.link(dve.tensor_tensor(X[:], X[:], H[:], ALU.add))
                for r, (j0, n) in enumerate(rounds(NJ, 4)):
                    dve.wait_ge(m0_m, r + 1)
                    P = bank[r % 2][0:PN, 0:n * 128].rearrange("p (j f) -> p j f", j=n)
                    c.mark(dve.tensor_tensor(X[:, j0:j0 + n, :], X[:, j0:j0 + n, :], P[:, :, 0:D], ALU.add))
                    c.mark(dve.tensor_copy(cnt[:, j0:j0 + n], P[:, :, D]))
                    c.mark(dve.tensor_copy(loop_a[:, j0:j0 + n, :], P[:, :, D + 1:MS]))
                    dve.wait_ge(m0_dve, c.n)
                    dve.sem_inc(m0_f, 1)

        def finish(stage):
            if LAST != stage:
                return False
            z_o = sem("z_o")
            with nc.Block() as block:
                @block.sync
                def _(sp):
                    sp.dma_start(out.rearrange("(j p) f -> p j f", p=PN), X[:]).then_inc(z_o, 16)
                    sp.wait_ge(z_o, 16)
            return True
        end_of_layer()
        if finish("L0"):
            return

        SG = 16
        KG = SG // GT
        pl = sb("pl", [1, NT])
        ql = sb("ql", [1, NT])
        first = sb("first", [128, NT])
        sel = sb("sel", [128, 3, 128])
        sel8 = sb("sel8", [128, 2, 128])
        delta_t = sb("delta_t", [128, SG])
        dst_f = sb("dst_f", [128, NT])
        al = sb("al", [128, 2, 128])
        am = sb("am", [128, 128])
        lp = sb("lp", [128, 64])
        dsth = sb("dsth", [128, 128])
        dT = sb("dT", [128, 130])
        pen = sb("pen", [128, 129])
        f1 = sb("f1", [128, 128])
        mx = sb("mx", [128, 128])
        mlast = sb("mlast", [128, 1])
        crow = sb("crow", [1, 8, SG + 1])
        prow = sb("prow", [1, 8, SG + 1])
        lrow = sb("lrow", [1, 8, SG + 1])
        cshift = sb("cshift", [1, 8, SG])
        ccol = sb("ccol", [128, 1])
        cm = sb("cm", [128, 1])
        fdiag = sb("fdiag", [128, SG])
        fac = sb("fac", [128, 2, 3, SG])
        ex = sb("ex", [128, 2, 2, 128])
        s_b = {}

        def softmax_sems(p):
            return {x: sem(f"{p}_{x}") for x in ("al", "T1", "dT", "pen", "f1", "ml", "cr", "cc", "mx", "cm", "pen2", "pe", "fd", "me",
                                                 "fac", "sub", "ex", "bd")}

        def softmax_dve(dve, S, q, c0, s, heads, scores, after):
            R = heads * SG
            c = LoopChain(dve, S["bd"], q, scores(None) + 14)
            scores(c)
            bch = lambda v: v.unsqueeze(1).to_broadcast([v.shape[0], heads, SG])
            c.mark(dve.tensor_copy(dsth[:, 0:R].rearrange("p (h t) -> p h t", h=heads), bch(dst_f[:, bass.ds(c0, SG)])))
            c.link(dve.tensor_copy(prow[:, 0:heads, 1:SG + 1], bch(pl[:, bass.ds(c0, SG)])))
            dve.sem_inc(S["al"], 1)
            dve.wait_ge(S["dT"], q + 1)
            c.link(dve.tensor_tensor(pen[0:R, 1:128], dT[0:R, 1:128], dT[0:R, 0:127], ALU.is_equal))
            c.link(dve.tensor_scalar(pen[0:R, 1:128], pen[0:R, 1:128], -1.0, BIG, ALU.add, ALU.mult))
            amT = bank[3][0:R, 0:128]
            c.mark(dve.tensor_tensor_scan(f1[0:R, :], pen[0:R, 0:128], amT, -BIG, ALU.add, ALU.max))
            dve.wait_ge(S["bd"], c.at + c.k)
            dve.sem_inc(S["f1"], 1)
            dve.wait_ge(S["ml"], q + 1)
            c.link(dve.tensor_copy(crow[:, 0:heads, 1:SG + 1], bank[3][0:1, 256:256 + R].rearrange("p (h t) -> p h t", h=heads)))
            flat = lambda v: v[:, 0:heads, :].rearrange("p h t -> p (h t)")
            c.link(dve.tensor_tensor_scan(flat(lrow), flat(prow), flat(crow), -BIG, ALU.add, ALU.max))
            c.mark(dve.tensor_copy(crow[:, 0:heads, 0:1], lrow[:, 0:heads, SG:SG + 1]))
            c.link(dve.tensor_tensor(cshift[:, 0:heads, :], lrow[:, 0:heads, 0:SG], bch(ql[:, bass.ds(c0, SG)]), ALU.add))
            dve.sem_inc(S["cr"], 1)
            dve.wait_ge(S["cc"], q + 1)
            c.link(dve.tensor_copy(ccol[0:R, :], bank[3][0:R, 384:385]))
            c.link(dve.tensor_tensor_scan(f1[0:R, :], pen[0:R, 0:128], amT, ccol[0:R, 0:1], ALU.add, ALU.max))
            c.link(dve.tensor_tensor_scan(mx[0:R, ::-1], pen[0:R, 128:0:-1], f1[0:R, ::-1], -BIG, ALU.add, ALU.max))
            c.link(dve.tensor_tensor(cm[0:R, :], ccol[0:R, :], mx[0:R, 0:1], ALU.subtract))
            dve.sem_inc(S["mx"], 1)
            dve.wait_ge(S["cm"], q + 1)
            c.mark(dve.tensor_scalar(fdiag[0:R, :], delta_t[0:R, :], cm[0:R, 0:1], None, ALU.mult))
            dve.wait_ge(S["bd"], c.at + c.k)
            dve.sem_inc(S["fd"], 1)
            dve.wait_ge(S["me"], q + 1)
            after(c, bank[3][:, 128:128 + R])
            c.done()

        def softmax_pe(pe, S, q, fb, heads, selm, nr):
            R = heads * SG
            pe.wait_ge(S["al"], q + 1)
            wait(pe, S["ex"], q * 2)
            pe.sem_inc(S["pe"], 1)
            pe.transpose(bank[3][0:R, 0:128], am[:, 0:R], ident[:])
            pe.transpose(bank[3][0:R, 128:256], dsth[:, 0:R], ident[:]).then_inc(S["T1"], 1)
            pe.wait_ge(S["f1"], q + 1)
            pe.sem_inc(S["pe"], 1)
            pe.transpose(bank[3][0:1, 256:256 + R], f1[0:R, 127:128], ident[0:R, 0:R]).then_inc(S["ml"], 1)
            pe.wait_ge(S["cr"], q + 1)
            pe.sem_inc(S["pe"], 1)
            pe.transpose(bank[3][0:R, 384:385], cshift[:, 0:heads, :].rearrange("p h t -> p (h t)"), ident[0:1, 0:1]).then_inc(S["cc"], 1)
            pe.wait_ge(S["mx"], q + 1)
            pe.sem_inc(S["pe"], 1)
            pe.transpose(bank[3][:, 128:128 + R], mx[0:R, :], ident[0:R, 0:R]).then_inc(S["me"], 1)
            pe.wait_ge(S["fd"], q + 1)
            pe.sem_inc(S["pe"], 1)
            for r in range(nr):
                last = pe.matmul(fb[:, r * SG:(r + 1) * SG], selm[0:R, r, :], fdiag[0:R, :], start=True, stop=True)
            last.then_inc(S["fac"], 1)

        def softmax_act(act, S, q, s, fb, heads, nr, nex):
            R = heads * SG
            act.wait_ge(S["T1"], q + 1)
            act.activation(dT[0:R, 0:128], bank[3][0:R, 128:256], ACT.Copy).then_inc(S["dT"], 1)
            act.wait_ge(S["mx"], q + 1)
            act.activation(cm[0:R, :], cm[0:R, :], ACT.Exp).then_inc(S["cm"], 1)
            act.wait_ge(S["sub"], q + 1)
            act.activation(ex[:, s, 0:nex, 0:R], ex[:, s, 0:nex, 0:R], ACT.Exp).then_inc(S["ex"], 1)
            act.wait_ge(S["fac"], q + 1)
            act.activation(fac[:, s, 0:nr, :], fb[:, 0:nr * SG].rearrange("p (r t) -> p r t", r=nr), ACT.Copy).then_inc(S["ex"], 1)

        k_i, k_d, k_l, k_p = sem("k_i"), sem("k_d"), sem("k_l"), sem("k_p")
        dprev = sb("dprev", [128, NT], I32)
        lastr = sb("lastr", [1, NT + 1], I32)
        with nc.Block() as block:
            @block.sync
            def _(sp):
                sp.dma_start(dprev[:], A["dst_before"]).then_inc(k_l, 16)
                sp.wait_ge(k_d, 1)
                sp.dma_start(lastr[:, 1:NT + 1], A["dst"][W - 1:W, :]).then_inc(k_l, 16)

            @block.gpsimd
            def _(pool):
                for m in (sel, sel8, delta_t):
                    pool.memset(m[:], 0.0).then_inc(k_i, 1)
                pool.wait_ge(k_i, 3)
                n = 3
                for h in range(8):
                    pool.affine_select(out=delta_t[:], in_=delta_t[:], compare_op=ALU.not_equal, fill=1.0, base=-h * SG,
                                       pattern=[[-1, SG]], channel_multiplier=1).then_inc(k_i, 1)
                    n += 1
                    pool.wait_ge(k_i, n)
                for m, heads, cw in ((sel, 4, 64), (sel8, 8, 16)):
                    nr = 2 if heads == 4 else 1
                    for r in range(nr):
                        v = m[:, r, :]
                        pool.memset(v, 1.0).then_inc(k_i, 1)
                        n += 1
                        pool.wait_ge(k_i, n)
                        per = 128 // cw
                        vv = v.rearrange("p (a c) -> p a c", a=per)
                        pool.affine_select(out=vv, in_=vv, compare_op=ALU.is_ge, fill=0.0, base=-SG * per * r,
                                           pattern=[[-SG, per], [0, cw]], channel_multiplier=1).then_inc(k_i, 1)
                        n += 1
                        pool.wait_ge(k_i, n)
                        pool.affine_select(out=vv, in_=vv, compare_op=ALU.is_ge, fill=0.0, base=SG * per * r + SG - 1,
                                           pattern=[[SG, per], [0, cw]], channel_multiplier=-1).then_inc(k_i, 1)
                        n += 1
                        pool.wait_ge(k_i, n)
                    reps = 2 if heads == 4 else 1
                    v = m[:, nr, 0:8]
                    pool.memset(v, 1.0).then_inc(k_i, 1)
                    n += 1
                    pool.wait_ge(k_i, n)
                    vv = v.rearrange("p (b h) -> p b h", b=reps)
                    pool.affine_select(out=vv, in_=vv, compare_op=ALU.is_ge, fill=0.0, base=0,
                                       pattern=[[0, reps], [-SG, heads]], channel_multiplier=1).then_inc(k_i, 1)
                    n += 1
                    pool.wait_ge(k_i, n)
                    pool.affine_select(out=vv, in_=vv, compare_op=ALU.is_ge, fill=0.0, base=SG - 1,
                                       pattern=[[0, reps], [SG, heads]], channel_multiplier=-1).then_inc(k_i, 1)
                    n += 1
                    pool.wait_ge(k_i, n)

            @block.vector
            def _(dve):
                c = Chain(dve, k_d)
                c.mark(dve.memset(lastr[:, 0:1], -2))
                c.mark(dve.memset(pen[:], 0.0))
                c.mark(dve.memset(prow[:], -BIG))
                c.mark(dve.tensor_copy(dst_f[:], dst_i[:]))
                dve.wait_ge(k_l, 32)
                c.mark(dve.tensor_tensor(first[:], dst_i[:], dprev[:], ALU.not_equal))
                c.mark(dve.tensor_tensor(pl[:], lastr[:, 1:NT + 1], lastr[:, 0:NT], ALU.is_equal))
                c.link(dve.tensor_tensor(ql[:], base_i[0:1, :], lastr[:, 0:NT], ALU.is_equal))
                c.mark(dve.tensor_scalar(pl[:], pl[:], -1.0, BIG, ALU.add, ALU.mult))
                c.mark(dve.tensor_scalar(ql[:], ql[:], -1.0, BIG, ALU.add, ALU.mult))

        WD = 4 * 64
        w_att = sb("w_att", [D, 4, 64])
        att = sb("att", [D, 2, 4, 64])
        wsd = sb("wsd", [D, 2, 4])
        gw = sb("gw", [D, WD])
        wp = sb("wp", [128, 2, D])
        wT = sb("wT", [128, 2, D])
        ww0 = sb("ww0", [D, 4, D])
        wwbd = sb("wwbd", [128, 2, 2, D])
        biasc = sb("biasc", [128, 2])
        biasb = sb("biasb", [128, 2, PN])
        cb = sb("cb", [PN, D])
        bpb = sb("bpb", [PN, D])
        gamma = sb("gamma", [PN, D])
        beta = sb("beta", [PN, D])
        asd = sb("asd", [PN, NJ, 8])
        dw = sb("dw", [PN, NJ, 8])
        T1 = dram("T1", [N, D + 4])
        T1W = dram("T1W", [NW, 8])
        n1_l, n1_dve, n1_var, n1_std, n1_t, n1_tc, n1_pw, n1_aw, n1_m, n1_o, n1_pp = [sem("n1_" + x) for x in
            ("l", "dve", "var", "std", "t", "tc", "pw", "aw", "m", "o", "pp")]
        XC, yn, tab = node_buffers("n1")
        with nc.Block() as block:
            @block.sync
            def _(sp):
                sp.dma_start(gw[:], A["L1_gnn_W"]).then_inc(n1_l, 16)
                sp.dma_start(att[:, 0], A["L1_gnn_att_src"].rearrange("h c -> (h c)").unsqueeze(0).partition_broadcast(D)).then_inc(n1_l, 16)
                sp.dma_start(att[:, 1], A["L1_gnn_att_dst"].rearrange("h c -> (h c)").unsqueeze(0).partition_broadcast(D)).then_inc(n1_l, 16)
                sp.dma_start(wp[:], A["L1_gnn_Wp"].rearrange("(g p) o -> p g o", g=2)).then_inc(n1_l, 16)
                sp.dma_start(bpb[:], A["L1_gnn_bp"].partition_broadcast(PN)).then_inc(n1_l, 16)
                sp.dma_start(gamma[:], A["L1_gnn_gamma"].partition_broadcast(PN)).then_inc(n1_l, 16)
                sp.dma_start(beta[:], A["L1_gnn_beta"].partition_broadcast(PN)).then_inc(n1_l, 16)
                with nc.allow_non_contiguous_dma(reason="256 floats, a column for each pair of heads"):
                    sp.dma_start(biasc[:], A["L1_gnn_bias"].rearrange("a (g p) -> (a p) g", g=2)).then_inc(n1_l, 16)
                sp.dma_start(T1W[N:NW, :], zero[:, 0:8]).then_inc(n1_o, 16)
                sp.wait_ge(n1_dve, 24)
                sp.dma_start(T1.rearrange("(j p) f -> p j f", p=PN)[:, :, 0:D], H[:]).then_inc(n1_o, 16)
                sp.dma_start(T1.rearrange("(j p) f -> p j f", p=PN)[:, :, D:D + 4], asd[:, :, 0:4]).then_inc(n1_o, 16)
                sp.dma_start(T1W[0:N, :].rearrange("(j p) f -> p j f", p=PN), dw[:]).then_inc(n1_o, 16)
                sp.wait_ge(n1_o, 64)

            @block.vector
            def _(dve):
                c = Chain(dve, n1_dve)
                ln_relu_steps(c, n1_var, n1_std, 1, XC=XC)
                c.mark(dve.memset(acc[:], 0.0))
                c.mark(dve.memset(wwbd[:], 0.0))
                dve.wait_ge(n1_l, 8 * 16)
                for a in range(2):
                    c.link(dve.tensor_tensor(w_att[:], gw[:].rearrange("k (h c) -> k h c", h=4), att[:, a], ALU.mult))
                    c.link(dve.tensor_reduce(wsd[:, a, :], w_att[:], AX.X, ALU.add))
                for g in range(2):
                    c.mark(dve.tensor_scalar(biasb[:, g, :], zero[:, 0:PN], biasc[:, g:g + 1], None, ALU.add))
                dve.wait_ge(n1_pw, 1)
                c.mark(dve.tensor_copy(wT[:], bank[4][:, 0:128].rearrange("p (g k) -> p g k", g=2)))
                dve.wait_ge(n1_pw, 2)
                c.mark(dve.tensor_copy(ww0[:], bank[5][0:D, 0:WD].rearrange("p (h o) -> p h o", h=4)))
                for g in range(2):
                    for hh in range(2):
                        P = slice(64 * hh, 64 * hh + 64)
                        dve.tensor_copy(wwbd[P, g, hh, :], bank[6][P, g * D:(g + 1) * D])
                c.link(dve.tensor_tensor(cb[:], bpb[:], bank[7][0:PN, 0:D], ALU.add))
                dve.wait_ge(n1_m, 1)
                c.link(dve.tensor_copy(asd[:], bank[2][0:PN, 0:NJ * 8].rearrange("p (j f) -> p j f", j=NJ)))
                c.link(dve.tensor_scalar(st[:, 6, :], cnt[:], 1.0, None, ALU.max))
                c.link(dve.reciprocal(st[:, 7, :], st[:, 6, :]))
                c.link(dve.tensor_tensor(loop_a[:], loop_a[:], st[:, 7, :].unsqueeze(2).to_broadcast([PN, NJ, 4]), ALU.mult))
                dve.tensor_copy(dw[:, :, 0:4], asd[:, :, 4:8]).then_inc(n1_aw, 1)
                dve.tensor_tensor(loop_a[:], loop_a[:], asd[:, :, 0:4], ALU.add).then_inc(n1_aw, 1)
                dve.wait_ge(n1_aw, 2)
                dve.tensor_tensor(loop_a[:], loop_a[:], asd[:, :, 4:8], ALU.add).then_inc(n1_aw, 1)
                dve.wait_ge(n1_aw, 3)
                c.mark(dve.scalar_tensor_tensor(dw[:, :, 4:8], loop_a[:], SLOPE, loop_a[:], ALU.mult, ALU.max))

            @block.scalar
            def _(act):
                ln_std_step(act, n1_var, n1_std, 1)
                transposed_copy_steps(act, n1_t, n1_tc)

            @block.tensor
            def _(pe):
                pe.wait_ge(n1_l, 8 * 16)
                for g in range(2):
                    last = pe.transpose(bank[4][:, g * D:(g + 1) * D], gw[:, g * 128:(g + 1) * 128], ident[0:D, 0:D])
                last.then_inc(n1_pw, 1)
                pe.wait_ge(n1_dve, 17)
                c = Chain(pe, n1_pp)
                for h in range(4):
                    P = slice(64 * (h % 2), 64 * (h % 2) + 64)
                    c.link(pe.matmul(bank[5][0:D, h * D:(h + 1) * D], wT[P, h // 2, :], wp[P, h // 2, :], start=True, stop=True))
                    c.link(pe.matmul(bank[6][P, (h // 2) * D:(h // 2 + 1) * D], wT[P, h // 2, :], wp[P, h // 2, :],
                                     start=True, stop=True))
                for g in range(2):
                    last = pe.matmul(bank[7][0:PN, 0:D], biasb[:, g, :], wp[:, g, :], start=(g == 0), stop=(g == 1))
                last.then_inc(n1_pw, 1)
                transpose_steps(pe, n1_t, n1_tc)
                pe.wait_ge(n1_tc, len(rounds(NJ, 4)))
                for j in range(NJ):
                    last = pe.matmul(bank[2][0:PN, j * 8:(j + 1) * 8], HT[:, j * PN:(j + 1) * PN],
                                     wsd[:].rearrange("k a h -> k (a h)"), start=True, stop=True)
                last.then_inc(n1_m, 1)

        layer.close()

        e1_g = [sem(f"e1_g{k}") for k in range(UG)]
        e1_w = [sem(f"e1_w{k}") for k in range(UG)]
        (e1_used, e1_idx, e1_step, e1_one, e1_T, e1_oT, e1_P, e1_M, e1_Mx, e1_S, e1_acc, e1_z, e1_z2) = [sem("e1_" + x) for x in
            ("used", "idx", "step", "one", "T", "oT", "P", "M", "Mx", "S", "acc", "z", "z2")]
        S1 = softmax_sems("b1")
        ga = tmp("ga1", [128, UT, D + 4])
        win = tmp("win1", [128, UT, 8])
        one = tmp("one1", [128, UT, 128])
        oneT = tmp("oneT1", [128, 2, GT, 128])
        M1 = tmp("M1", [128, 2, GT, 3, 128])
        with nc.Block() as block:
            @block.gpsimd
            def _(pool):
                gather_program(ga, pool, T1, D + 4, e1_g, e1_used, e1_idx, e1_step)

            @block.sync
            def _(sp):
                each_group(sp, lambda i, k: window_loads(win, sp, i, k, T1W, 8, e1_w, e1_P))

            @block.scalar
            def _(act):
                def weights(i, k):
                    g = i * UG + k
                    s, kk = k // KG, k % KG
                    wait(act, e1_S, g - 1)
                    act.wait_ge(S1["ex"], (i * 2 + s) * 2 + 1)
                    act.activation(M1[:, k % 2, :, 2, 0:4],
                                   ex[:, s, 0, 0:64].rearrange("p (h t) -> p t h", h=4)[:, kk * GT:(kk + 1) * GT, :],
                                   ACT.Copy).then_inc(e1_Mx, 1)

                def body(i, k):
                    g = i * UG + k
                    act.wait_ge(e1_T, g + 1)
                    wait(act, e1_P, g - 1)
                    act.activation(oneT[:, k % 2], bank[0][:].rearrange("p (t n) -> p t n", t=GT), ACT.Copy).then_inc(e1_oT, 1)
                    if back(i, k, KG):
                        weights(*back(i, k, KG))
                    if k % KG == KG - 1:
                        softmax_act(act, S1, i * 2 + k // KG, k // KG, bank[1 + k // KG][:, 128:176], 4, 3, 2)
                each_group(act, body)
                for k in range(KG, UG):
                    weights(NI - 1, k)

            @block.tensor
            def _(pe):
                def sums(i, k):
                    g = i * UG + k
                    pe.wait_ge(e1_M, g * 2 + 2)
                    pe.wait_ge(e1_Mx, g + 1)
                    for t in range(GT):
                        wait(pe, e1_acc, (g - 1) * 2 * GT + 2 * t + 2)
                        for r in range(3):
                            last = pe.matmul(bank[4 + t][:, r * 128:(r + 1) * 128], M1[:, k % 2, t, r, :], one[:, k * GT + t, :],
                                             start=True, stop=True)
                        last.then_inc(e1_S if t == GT - 1 else e1_z, 1)

                def body(i, k):
                    g = i * UG + k
                    s, kk = k // KG, k % KG
                    pe.wait_ge(e1_one, g + 1)
                    wait(pe, e1_oT, g)
                    for t in range(GT):
                        last = pe.transpose(bank[0][:, t * 128:(t + 1) * 128], one[:, k * GT + t, :], ident[:])
                    last.then_inc(e1_T, 1)
                    if back(i, k, KG):
                        sums(*back(i, k, KG))
                    pe.wait_ge(e1_oT, g + 1)
                    pe.wait_ge(e1_w[k], i * 64 + 64)
                    if kk == 0:
                        wait(pe, S1["ex"], i * 4 + (s * 2 - 2))
                    for t in range(GT):
                        o = (kk * GT + t) * 8
                        last = pe.matmul(bank[1 + s][:, o:o + 8], oneT[:, k % 2, t, :], win[:, k * GT + t, 0:8], start=True, stop=True)
                    last.then_inc(e1_P, 1)
                    if kk == KG - 1:
                        softmax_pe(pe, S1, i * 2 + s, bank[1 + s][:, 128:176], 4, sel, 3)
                each_group(pe, body)
                for k in range(KG, UG):
                    sums(NI - 1, k)

            @block.vector
            def _(dve):
                c = Chain(dve, e1_z2)
                c.mark(dve.memset(M1[:], 0.0))
                c.link(dve.memset(crow[:], -BIG))

                def add_sums(i, k):
                    g = i * UG + k
                    s, kk = k // KG, k % KG
                    wait(dve, e1_S, g - 1)
                    dve.wait_ge(S1["ex"], (i * 2 + s) * 2 + 2)
                    w = lambda x: ex[:, s, x, 0:64].rearrange("p (h t) -> p t h", h=4)[:, kk * GT:(kk + 1) * GT, :]
                    tiles = bass.ds(i * UT + k * GT, GT)
                    dve.tensor_tensor(M1[:, k % 2, :, 0:2, :].rearrange("p t r (b c) -> p t (r b) c", b=2),
                                      ga[:, k * GT:(k + 1) * GT, 0:D].unsqueeze(2).to_broadcast([128, GT, 4, D]),
                                      w(0).unsqueeze(3).to_broadcast([128, GT, 4, D]), ALU.mult).then_inc(e1_M, 1)
                    dve.tensor_tensor(M1[:, k % 2, :, 2, 4:8], w(1), first[:, tiles].unsqueeze(2).to_broadcast([128, GT, 4]),
                                      ALU.mult).then_inc(e1_M, 1)
                    dve.wait_ge(e1_M, g * 2 + 2)
                    dve.sem_inc(e1_used, 1)
                    for t in range(GT):
                        b = base_of(dve, i, k, t)
                        wait(dve, e1_acc, g * 2 * GT + 2 * t)
                        a = acc[:, :, bass.ds(b, 1)]
                        dve.tensor_tensor(a, a, fac[:, s, :, kk * GT + t:kk * GT + t + 1], ALU.mult).then_inc(e1_acc, 1)
                        dve.wait_ge(e1_acc, g * 2 * GT + (2 * t + 1))
                        if t == GT - 1:
                            dve.wait_ge(e1_S, g + 1)
                        else:
                            dve.wait_ge(e1_z, g * (GT - 1) + (t + 1))
                        a = acc[:, :, bass.ds(b, W)]
                        dve.tensor_tensor(a, a, bank[4 + t][:, 0:384].rearrange("p (r n) -> p r n", r=3), ALU.add).then_inc(e1_acc, 1)

                def body(i, k):
                    g = i * UG + k
                    s = k // KG
                    wait(dve, e1_S, g - 7)
                    one_hot_ring_step(one, dve, i, k, e1_one)
                    if back(i, k, KG):
                        add_sums(*back(i, k, KG))
                    if k % KG < KG - 1:
                        return
                    q = i * 2 + s

                    def scores(c):
                        if c is None:
                            return 4
                        for kk in range(KG):
                            dve.wait_ge(e1_g[s * KG + kk], i * 64 + 64)
                        dve.wait_ge(e1_P, g + 1)
                        P = bank[1 + s][:, 0:128].rearrange("p (t f) -> p f t", f=8)
                        v = lambda x: x.rearrange("p (h t) -> p h t", h=4)
                        c.mark(dve.tensor_copy(v(lp[:]), P[:, 4:8, :]))
                        c.link(dve.tensor_tensor(v(al[:, 0, 0:64]), ga[:, s * SG:(s + 1) * SG, D:D + 4].rearrange("p t f -> p f t"),
                                                 P[:, 0:4, :], ALU.add))
                        c.link(dve.tensor_tensor(v(al[:, 0, 0:64]), v(al[:, 0, 0:64]),
                                                 edge_a[:, bass.ds(i * UT + s * SG, SG), :].rearrange("p t f -> p f t"), ALU.add))
                        c.link(dve.scalar_tensor_tensor(al[:, 0, 0:64], al[:, 0, 0:64], SLOPE, al[:, 0, 0:64], ALU.mult, ALU.max))
                        dve.tensor_tensor(am[:, 0:64], al[:, 0, 0:64], lp[:], ALU.max).then_inc(S1["pen"], 1)
                        dve.wait_ge(S1["pen"], q + 1)

                    def after(c, m):
                        dve.tensor_tensor(ex[:, s, 0, 0:64], al[:, 0, 0:64], m, ALU.subtract).then_inc(S1["pen2"], 1)
                        dve.tensor_tensor(ex[:, s, 1, 0:64], lp[:], m, ALU.subtract).then_inc(S1["pen2"], 1)
                        dve.wait_ge(S1["pen2"], q * 2 + 2)
                        dve.sem_inc(S1["sub"], 1)
                    softmax_dve(dve, S1, q, i * UT + s * SG, s, 4, scores, after)
                each_group(dve, body)
                for k in range(KG, UG):
                    add_sums(NI - 1, k)

        layer.close()
        den = sb("den", [PN, NJ, 8])
        yl = sb("yl", [PN, 2, 4, D])
        m1_d, m1_dve, m1_m, m1_act = [sem("m1_" + x) for x in ("d", "dve", "m", "act")]
        m1_var, m1_std = sem("m1_var"), sem("m1_std")
        XC, yn, tab = node_buffers("m1")
        with nc.Block() as block:
            @block.tensor
            def _(pe):
                for j in range(NJ):
                    last = pe.transpose(bank[0][0:PN, j * 8:(j + 1) * 8], acc[0:8, 2, j * PN:(j + 1) * PN], ident[0:8, 0:8])
                last.then_inc(m1_d, 1)
                for j in range(NJ):
                    if j >= 2:
                        pe.wait_ge(m1_dve, 5 + 4 * (j - 1))
                    b = bank[1 + j % 2]
                    for g in range(2):
                        pe.matmul(b[0:PN, g * 128:(g + 1) * 128], acc[:, g, j * PN:(j + 1) * PN],
                                  wwbd[:, g].rearrange("p a o -> p (a o)"), start=True, stop=True)
                    pe.matmul(b[0:PN, 256:512], HT[:, j * PN:(j + 1) * PN], ww0[:].rearrange("p h o -> p (h o)"),
                              start=True, stop=True).then_inc(m1_m, 1)

            @block.vector
            def _(dve):
                c = Chain(dve, m1_dve)
                dve.wait_ge(m1_d, 1)
                c.link(dve.tensor_copy(den[:], bank[0][0:PN, 0:NJ * 8].rearrange("p (j f) -> p j f", j=NJ)))
                c.link(dve.tensor_scalar(st[:, 6, :], cnt[:], 0.0, None, ALU.is_equal))
                c.link(dve.tensor_tensor(den[:, :, 4:8], den[:, :, 4:8], st[:, 6, :].unsqueeze(2).to_broadcast([PN, NJ, 4]), ALU.add))
                c.link(dve.tensor_tensor(den[:, :, 0:4], den[:, :, 0:4], den[:, :, 4:8], ALU.add))
                c.link(dve.reciprocal(den[:, :, 0:4], den[:, :, 0:4]))
                for j in range(NJ):
                    dve.wait_ge(m1_m, j + 1)
                    b = bank[1 + j % 2]
                    y = yl[:, j % 2]
                    wl = den[:, j, 4:8].unsqueeze(2).to_broadcast([PN, 4, D])
                    rd = den[:, j, 0:4].unsqueeze(2).to_broadcast([PN, 4, D])
                    c.link(dve.tensor_tensor(y, b[0:PN, 256:512].rearrange("p (h o) -> p h o", h=4), wl, ALU.mult))
                    c.link(dve.tensor_tensor(y, b[0:PN, 0:256].rearrange("p (h o) -> p h o", h=4), y, ALU.add))
                    c.link(dve.tensor_tensor(y, y, rd, ALU.mult))
                    c.mark(dve.tensor_reduce(XC[:, j, :], y.rearrange("p h o -> p o h"), AX.X, ALU.add))
                dve.wait_ge(m1_dve, c.n)
                bc = lambda v: v[:].unsqueeze(1).to_broadcast([PN, NJ, D])
                c.link(dve.tensor_tensor(XC[:], XC[:], bc(cb), ALU.add))
                c.link(dve.tensor_scalar(tab[:, :, 0:D], XC[:], 0.0, None, ALU.min))
                m1_min = c.n
                c.link(dve.tensor_scalar(XC[:], XC[:], 0.0, -1.0, ALU.max, ALU.add))
                s_done["m1_min"] = m1_min
                c.link(dve.tensor_tensor(H[:], H[:], XC[:], ALU.add))
                dve.wait_ge(m1_act, 1)
                c.link(dve.tensor_tensor(H[:], H[:], tab[:, :, D:2 * D], ALU.add))
                ln_relu_steps(c, m1_var, m1_std, 1, dst=yn, src=H, relu=False, XC=XC)
                c.link(dve.tensor_tensor(yn[:], yn[:], bc(gamma), ALU.mult))
                c.link(dve.tensor_tensor(yn[:], yn[:], bc(beta), ALU.add))
                c.link(dve.tensor_tensor(X[:], X[:], yn[:], ALU.add))

            @block.scalar
            def _(act):
                act.wait_ge(m1_dve, 5 + 4 * NJ + 2)
                act.activation(tab[:, :, D:2 * D], tab[:, :, 0:D], ACT.Exp).then_inc(m1_act, 1)
                ln_std_step(act, m1_var, m1_std, 1)
        end_of_layer()
        if finish("L1"):
            return

        w2t = sb("w2t", [D, D])
        b2b = sb("b2b", [PN, D])
        dis = sb("dis", [PN, NJ])
        T2 = dram("T2", [N, D])
        n2_l, n2_dve, n2_var, n2_std, n2_deg, n2_t, n2_tc, n2_o = [sem("n2_" + x) for x in ("l", "dve", "var", "std", "deg", "t", "tc", "o")]
        XC, yn, tab = node_buffers("n2")
        with nc.Block() as block:
            @block.vector
            def _(dve):
                c = Chain(dve, n2_dve)
                c.link(dve.tensor_scalar(st[:, 6, :], cnt[:], 1.0, None, ALU.add))
                dve.wait_ge(n2_deg, 1)
                c.link(dve.reciprocal(dis[:], st[:, 7, :]))
                c.mark(dve.memset(acc[:], 0.0))
                ln_relu_steps(c, n2_var, n2_std, 1, XC=XC)
                c.mark(dve.tensor_tensor(yn[:], H[:], dis[:].unsqueeze(2).to_broadcast([PN, NJ, D]), ALU.mult))

            @block.scalar
            def _(act):
                act.wait_ge(n2_dve, 1)
                act.activation(st[:, 7, :], st[:, 6, :], ACT.Sqrt).then_inc(n2_deg, 1)
                ln_std_step(act, n2_var, n2_std, 1)
                transposed_copy_steps(act, n2_t, n2_tc)

            @block.tensor
            def _(pe):
                pe.wait_ge(n2_dve, 12)
                transpose_steps(pe, n2_t, n2_tc, src=yn)

            @block.sync
            def _(sp):
                sp.dma_start(w2t[:], A["L2_gnn_WT"]).then_inc(n2_l, 16)
                sp.dma_start(b2b[:], A["L2_gnn_b"].partition_broadcast(PN)).then_inc(n2_l, 16)
                sp.wait_ge(n2_dve, 12)
                sp.dma_start(T2.rearrange("(j p) f -> p j f", p=PN), yn[:]).then_inc(n2_o, 16)
                sp.wait_ge(n2_o, 16)
                sp.wait_ge(n2_l, 32)
        layer.close()

        e2_g = [sem(f"e2_g{k}") for k in range(UG)]
        e2_idx, e2_step, e2_one, e2_S, e2_acc = [sem("e2_" + x) for x in ("idx", "step", "one", "S", "acc")]
        ga = tmp("ga2", [128, UT, D])
        one = tmp("one2", [128, UT, 128])
        with nc.Block() as block:
            @block.gpsimd
            def _(pool):
                gather_program(ga, pool, T2, D, e2_g, e2_S, e2_idx, e2_step)

            @block.tensor
            def _(pe):
                def body(i, k):
                    g = i * UG + k
                    pe.wait_ge(e2_one, g + 1)
                    pe.wait_ge(e2_g[k], i * 64 + 64)
                    wait(pe, e2_acc, (g - 1) * GT)
                    for t in range(GT):
                        last = pe.matmul(bank[k % 2][0:D, t * 128:(t + 1) * 128], ga[:, k * GT + t, :], one[:, k * GT + t, :],
                                         start=True, stop=True)
                    last.then_inc(e2_S, 1)
                each_group(pe, body)

            @block.vector
            def _(dve):
                def add_sums(i, k):
                    g = i * UG + k
                    dve.wait_ge(e2_S, g + 1)
                    for t in range(GT):
                        b = base_of(dve, i, k, t)
                        wait(dve, e2_acc, g * GT + t)
                        a = acc[0:D, 0, bass.ds(b, W)]
                        dve.tensor_tensor(a, a, bank[k % 2][0:D, t * 128:(t + 1) * 128], ALU.add).then_inc(e2_acc, 1)

                def body(i, k):
                    g = i * UG + k
                    wait(dve, e2_S, g - 7)
                    one_hot_ring_step(one, dve, i, k, e2_one)
                    if before(i, k):
                        add_sums(*before(i, k))
                each_group(dve, body)
                add_sums(NI - 1, UG - 1)
        layer.close()

        m2_m, m2_dve = sem("m2_m"), sem("m2_dve")
        XC, yn, tab = node_buffers("m2")
        with nc.Block() as block:
            @block.tensor
            def _(pe):
                for r, (j0, n) in enumerate(rounds(NJ, 4)):
                    if r >= 2:
                        pe.wait_ge(m2_dve, r - 1)
                    for j in range(n):
                        cols = slice((j0 + j) * PN, (j0 + j + 1) * PN)
                        o = bank[r % 2][0:PN, j * D:(j + 1) * D]
                        pe.matmul(o, acc[0:D, 0, cols], w2t[:], start=True, stop=False)
                        last = pe.matmul(o, HT[:, cols], w2t[:], start=False, stop=True)
                    last.then_inc(m2_m, 1)

            @block.vector
            def _(dve):
                c = Chain(dve, m2_dve)
                for r, (j0, n) in enumerate(rounds(NJ, 4)):
                    dve.wait_ge(m2_m, r + 1)
                    c.mark(dve.tensor_tensor(yn[:, j0:j0 + n, :], bank[r % 2][0:PN, 0:n * D].rearrange("p (j f) -> p j f", j=n),
                                             dis[:, j0:j0 + n].unsqueeze(2).to_broadcast([PN, n, D]), ALU.mult))
                dve.wait_ge(m2_dve, c.n)
                c.link(dve.tensor_tensor(yn[:], yn[:], b2b[:].unsqueeze(1).to_broadcast([PN, NJ, D]), ALU.add))
                c.link(dve.scalar_tensor_tensor(X[:], yn[:], 0.0, X[:], ALU.max, ALU.add))
        end_of_layer()
        if finish("L2"):
            return

        F = 128
        NS = 9
        NZ = 5
        wq = sb("wq", [D, F])
        w1kv = sb("w1kv", [D, F])
        b1kv = sb("b1kv", [F, 1])
        w2v = sb("w2v", [D + 1, F])
        w2k = sb("w2k", [128, F])
        b2k = sb("b2k", [F, 1])
        ck = sb("ck", [128, NZ, F])
        cv = sb("cv", [128, NZ, F])
        w_out = sb("w_out", [F, D])
        w_self = sb("w_self", [D, D])
        gcol = sb("gcol", [D, 1])
        bcol = sb("bcol", [D, 1])
        shsel = sb("shsel", [3 * NS, NZ, 128], BF16)
        sel_b = sb("sel_b", [8, 128])
        XX = dram("XX", [N, 2 * D])
        QW = dram("QW", [NW, F])
        SH = dram("SH", [3, NS * EP], BF16)
        n3_l, n3_s, n3_sd, n3_p, n3_dve, n3_var, n3_std, n3_t, n3_tc, n3_q, n3_qc, n3_o, n3_c = [sem("n3_" + x) for x in
            ("l", "s", "sd", "p", "dve", "var", "std", "t", "tc", "q", "qc", "o", "c")]
        NL3 = 17
        SF = NS * EP // 128
        XC, yn, tab = node_buffers("n3")
        shf = tmp("shf", [128, SF])
        shp = tmp("shp", [128, 3, SF], BF16)
        shsel_f = tmp("shsel_f", [3 * NS, NZ, 128])
        with nc.Block() as block:
            @block.sync
            def _(sp):
                sp.dma_start(shf[:], A["ea9"].rearrange("s (a f) -> (s a) f", a=1).rearrange("s f -> (s f)")
                             .rearrange("(p f) -> p f", p=128)).then_inc(n3_s, 16)
                L = lambda o, i: sp.dma_start(o, i).then_inc(n3_l, 16)
                L(wq[:], A["L3_gnn_Wq"])
                L(w1kv[:, 0:D], A["L3_gnn_v_w1"])
                L(w1kv[:, D:F], A["L3_gnn_k_w1"])
                L(w2v[0:D, :], A["L3_gnn_v_w2"])
                L(w2v[D:D + 1, :], A["L3_gnn_v_b2"])
                L(w2k[D:128, :], A["L3_gnn_k_w2"])
                L(w_out[:], A["L3_gnn_W_out"])
                L(w_self[:], A["L3_gnn_W_self"])
                with nc.allow_non_contiguous_dma(reason="biases as columns"):
                    L(b1kv[0:D, :], A["L3_gnn_v_b1"].rearrange("a f -> f a"))
                    L(b1kv[D:F, :], A["L3_gnn_k_b1"].rearrange("a f -> f a"))
                    L(b2k[:], A["L3_gnn_k_b2"].rearrange("a f -> f a"))
                    L(gcol[:], A["L3_gnn_gamma"].rearrange("a f -> f a"))
                    L(bcol[:], A["L3_gnn_beta"].rearrange("a f -> f a"))
                for m, w in ((ck, "Cqk"), (cv, "Cv")):
                    L(m[0:D, :, :], A["L3_gnn_" + w][:, 0:NS:2, :])
                    L(m[D:128, 0:NZ - 1, :], A["L3_gnn_" + w][:, 1:NS:2, :])
                for part in range(3):
                    sp.wait_ge(n3_sd, 2 * part + 1)
                    sp.dma_start(SH[part].rearrange("(p f) -> p f", p=128), shp[:, part, :]).then_inc(n3_o, 16)
                sp.dma_start(QW[N:NW, :], zero[:, 0:F]).then_inc(n3_o, 16)
                sp.wait_ge(n3_dve, 9)
                for a in range(2):
                    sp.dma_start(XX.rearrange("(j p) f -> p j f", p=PN)[:, :, a * D:(a + 1) * D], H[:]).then_inc(n3_o, 16)
                sp.wait_ge(n3_qc, len(rounds(NJ, 4)))
                sp.dma_start(QW[0:N, :].rearrange("(j p) f -> p j f", p=PN), tab[:]).then_inc(n3_o, 16)
                sp.wait_ge(n3_o, 7 * 16)
                sp.wait_ge(n3_l, NL3 * 16)

            @block.gpsimd
            def _(pool):
                pool.memset(shsel_f[:], 0.0).then_inc(n3_p, 1)
                n = 1
                for part in range(3):
                    pool.wait_ge(n3_p, n)
                    pool.affine_select(out=shsel_f[:].rearrange("p j (a c) -> p j a c", a=2),
                                       in_=shsel_f[:].rearrange("p j (a c) -> p j a c", a=2),
                                       compare_op=ALU.not_equal, fill=1.0, base=-NS * part,
                                       pattern=[[-2, NZ], [-1, 2], [0, D]], channel_multiplier=1).then_inc(n3_p, 1)
                    n += 1
                pool.memset(sel_b[:], 1.0).then_inc(n3_p, 1)
                n += 1
                pool.wait_ge(n3_p, n)
                pool.affine_select(out=sel_b[:], in_=sel_b[:], compare_op=ALU.is_ge, fill=0.0, base=0,
                                   pattern=[[1, 128]], channel_multiplier=-16).then_inc(n3_p, 1)
                n += 1
                pool.wait_ge(n3_p, n)
                pool.affine_select(out=sel_b[:], in_=sel_b[:], compare_op=ALU.is_ge, fill=0.0, base=15,
                                   pattern=[[-1, 128]], channel_multiplier=16).then_inc(n3_p, 1)

            @block.vector
            def _(dve):
                c = Chain(dve, n3_dve)
                ln_relu_steps(c, n3_var, n3_std, 1, XC=XC)
                c.mark(dve.memset(acc[:, 0:2, :], 0.0))
                s = Chain(dve, n3_sd)
                dve.wait_ge(n3_s, 16)
                s.link(dve.tensor_copy(shp[:, 0, :], shf[:]))
                for part in range(1, 3):
                    s.link(dve.tensor_tensor(shf[:], shf[:], shp[:, part - 1, :], ALU.subtract))
                    s.link(dve.tensor_copy(shp[:, part, :], shf[:]))
                dve.wait_ge(n3_p, 4)
                dve.tensor_copy(shsel[:], shsel_f[:]).then_inc(n3_c, 1)

            @block.scalar
            def _(act):
                ln_std_step(act, n3_var, n3_std, 1)
                transposed_copy_steps(act, n3_t, n3_tc)
                for r, (j0, n) in enumerate(rounds(NJ, 4)):
                    act.wait_ge(n3_q, r + 1)
                    act.activation(tab[:, j0:j0 + n, :], bank[2 + r % 2][0:PN, 0:n * 128].rearrange("p (j f) -> p j f", j=n),
                                   ACT.Copy).then_inc(n3_qc, 1)

            @block.tensor
            def _(pe):
                pe.wait_ge(n3_dve, 8)
                transpose_steps(pe, n3_t, n3_tc)
                pe.wait_ge(n3_l, NL3 * 16)
                for r, (j0, n) in enumerate(rounds(NJ, 4)):
                    pe.wait_ge(n3_tc, r + 1)
                    if r >= 2:
                        pe.wait_ge(n3_qc, r - 1)
                    for j in range(n):
                        last = pe.matmul(bank[2 + r % 2][0:PN, j * 128:(j + 1) * 128], HT[:, (j0 + j) * PN:(j0 + j + 1) * PN],
                                         wq[:], start=True, stop=True)
                    last.then_inc(n3_q, 1)
        layer.close()

        e3_g = [sem(f"e3_g{k}") for k in range(UG)]
        WR = 2
        e3_w = [sem(f"e3_w{k}") for k in range(WR)]
        e3_e = [sem(f"e3_e{k}") for k in range(2)]
        (e3_idx, e3_step, e3_one, e3_T, e3_oT, e3_X, e3_xT, e3_H, e3_h, e3_sh, e3_z, e3_Q, e3_q, e3_K, e3_Wk, e3_wk, e3_kt, e3_pr,
         e3_V, e3_Wv, e3_wv, e3_vw, e3_P, e3_S, e3_acc, e3_M, e3_Mx, e3_i, e3_sp) = [sem("e3_" + x) for x in
            ("idx", "step", "one", "T", "oT", "X", "xT", "H", "h", "sh", "z", "Q", "q", "K", "Wk", "wk", "kt", "pr",
             "V", "Wv", "wv", "vw", "P", "S", "acc", "M", "Mx", "i", "sp")]
        S3 = softmax_sems("b3")
        GR = 4
        ga = tmp("ga3", [128, GR * GT, F])
        win = tmp("win3", [128, WR * GT, F])
        one = tmp("one3", [128, UT, 128])
        oneT = acc[:, 2, 0 * 512:1 * 512]
        xT = acc[:, 2, 1 * 512:2 * 512]
        ef = tmp("ef", [D, 2, GT * W])
        shl = tmp("shl", [3 * NS, 2, GT * W], BF16)
        spare = edge_a[:].rearrange("p t h -> p (t h)")
        hv = spare[0:D + 1, 0:GT * W]
        hk = spare[:, GT * W:2 * GT * W]
        z = tmp("z", [128, 2, NZ, GT * W])
        qs = acc[:, 2, 2 * 512:3 * 512]
        wks = acc[:, 2, 3 * 512:4 * 512]
        kt = acc[:, 2, 4 * 512:5 * 512]
        wvs = spare[:, 2 * GT * W:3 * GT * W].rearrange("p (t f) -> p t f", t=GT)
        vw = tmp("vw", [128, UT, F])
        M3 = tmp("M3", [128, 2, GT, 2, F])
        hsel = tmp("hsel", [128, 8])
        with nc.Block() as block:
            @block.gpsimd
            def _(pool):
                gather_program(ga, pool, XX, F, e3_g, e3_X, e3_idx, e3_step, ring=GR)

            @block.sync
            def _(sp):
                def body(i, k):
                    g = i * UG + k
                    cols = bass.ds(g * GT * W, GT * W)
                    wait(sp, e3_H, g - 1)
                    sp.sem_inc(e3_sp, 1)
                    wait(sp, e3_sh, (g - 1) * NZ)
                    sp.sem_inc(e3_sp, 1)
                    sp.dma_start(ef[:, k % 2, :], A["ea64"][:, cols]).then_inc(e3_e[k % 2], 16)
                    for part in range(3):
                        sp.dma_start(shl[part * NS:(part + 1) * NS, k % 2, :],
                                     SH[part].rearrange("(s e) -> s e", s=NS)[:, cols]).then_inc(e3_e[k % 2], 16)
                    starts = [base_of(sp, i, k, t) for t in range(GT)]
                    wait(sp, e3_Q, g - (WR - 1))
                    sp.sem_inc(e3_sp, 1)
                    for t, b in enumerate(starts):
                        sp.dma_start(win[:, (k % WR) * GT + t, :], QW[bass.ds(b, W), :]).then_inc(e3_w[k % WR], 16)
                each_group(sp, body)

            @block.scalar
            def _(act):
                def weights(i, k):
                    g = i * UG + k
                    s, kk = k // KG, k % KG
                    wait(act, e3_S, (g - 1) * 2)
                    act.wait_ge(S3["ex"], (i * 2 + s) * 2 + 1)
                    act.activation(M3[:, k % 2, :, 1, 0:8],
                                   ex[:, s, 0, :].rearrange("p (h t) -> p t h", h=8)[:, kk * GT:(kk + 1) * GT, :],
                                   ACT.Copy).then_inc(e3_Mx, 1)

                def body(i, k):
                    g = i * UG + k
                    if back(i, k, KG):
                        weights(*back(i, k, KG))
                    act.wait_ge(e3_T, g + 1)
                    wait(act, e3_Q, g)
                    act.activation(oneT[:], bank[0][:], ACT.Copy).then_inc(e3_oT, 1)
                    act.wait_ge(e3_X, g + 1)
                    wait(act, e3_z, g * NZ)
                    act.activation(xT[:], bank[0][:], ACT.Copy).then_inc(e3_xT, 1)
                    act.wait_ge(e3_H, g + 1)
                    wait(act, e3_Wk, g)
                    wait(act, e3_Wv, g)
                    act.activation(hv[0:D, :], bank[0][0:D, :], ACT.Relu, bias=b1kv[0:D, 0:1]).then_inc(e3_h, 1)
                    act.activation(hk[D:128, :], bank[0][D:128, :], ACT.Relu, bias=b1kv[D:128, 0:1]).then_inc(e3_h, 1)
                    act.wait_ge(e3_Q, g + 1)
                    wait(act, e3_pr, g)
                    act.activation(qs[:], bank[7][:], ACT.Copy).then_inc(e3_q, 1)
                    act.wait_ge(e3_Wk, g + 1)
                    wait(act, e3_kt, g)
                    act.activation(wks[:], bank[7][:], ACT.Identity, bias=b2k[:, 0:1]).then_inc(e3_wk, 1)
                    act.wait_ge(e3_Wv, g + 1)
                    wait(act, e3_vw, g)
                    act.activation(wvs[:], bank[7][:].rearrange("p (t f) -> p t f", t=GT), ACT.Copy).then_inc(e3_wv, 1)
                    if k % KG == KG - 1:
                        softmax_act(act, S3, i * 2 + k // KG, k // KG, bank[4][:, 128:160], 8, 2, 1)
                act.wait_ge(e3_i, 4)
                each_group(act, body)
                for k in range(KG, UG):
                    weights(NI - 1, k)

            @block.tensor
            def _(pe):
                def sums(i, k, half):
                    g = i * UG + k
                    if half == 0:
                        pe.wait_ge(e3_M, g + 1)
                        pe.wait_ge(e3_Mx, g + 1)
                    else:
                        pe.wait_ge(e3_acc, g * 8 + 4)
                    for t in range(2 * half, 2 * half + 2):
                        for r in range(2):
                            last = pe.matmul(bank[7][:, (t % 2) * 256 + r * 128:(t % 2) * 256 + (r + 1) * 128], M3[:, k % 2, t, r, :],
                                             one[:, k * GT + t, :], start=True, stop=True)
                    last.then_inc(e3_S, 1)

                def harmonics(i, k, j):
                    u = (i * UG + k) * NZ + j
                    m = 128 if j < NZ - 1 else D
                    wait(pe, e3_z, u - 1)
                    pe.matmul(bank[1 + (k * NZ + j) % 2][0:m, :], shsel[:, j, 0:m], shl[:, k % 2, :], start=True, stop=True)\
                      .then_inc(e3_sh, 1)

                def body(i, k):
                    g = i * UG + k
                    s, kk = k // KG, k % KG
                    old = back(i, k, KG)
                    pe.wait_ge(e3_one, g + 1)
                    wait(pe, e3_h, g * 2)
                    for t in range(GT):
                        last = pe.transpose(bank[0][:, t * 128:(t + 1) * 128], one[:, k * GT + t, :], ident[:])
                    last.then_inc(e3_T, 1)
                    wait(pe, e3_wv, g)
                    if old:
                        sums(*old, 0)
                    pe.wait_ge(e3_g[k], i * 64 + 64)
                    pe.wait_ge(e3_oT, g + 1)
                    for t in range(GT):
                        last = pe.transpose(bank[0][:, t * 128:(t + 1) * 128], ga[:, (k % GR) * GT + t, :], ident[:])
                    last.then_inc(e3_X, 1)
                    pe.wait_ge(e3_e[k % 2], i * (UG // 2 * 64) + (k // 2 + 1) * 64)
                    for j in range(2):
                        harmonics(i, k, j)
                    if old:
                        sums(*old, 1)
                    pe.wait_ge(e3_xT, g + 1)
                    pe.matmul(bank[0][:], w1kv[:], ef[:, k % 2, :], start=True, stop=True).then_inc(e3_H, 1)
                    if old:
                        pe.wait_ge(e3_acc, (old[0] * UG + old[1]) * 8 + 8)
                    pe.wait_ge(e3_w[k % WR], i * (UG // WR * 64) + (k // WR + 1) * 64)
                    for t in range(GT):
                        last = pe.matmul(bank[7][:, t * 128:(t + 1) * 128], win[:, (k % WR) * GT + t, :],
                                         oneT[:, t * 128:(t + 1) * 128], start=True, stop=True)
                    last.then_inc(e3_Q, 1)
                    wait(pe, e3_kt, g)
                    for j in range(NZ):
                        m = 128 if j < NZ - 1 else D
                        pe.wait_ge(e3_z, g * NZ + (j + 1))
                        last = pe.matmul(bank[5][:], ck[0:m, j, :], z[0:m, k % 2, j, :], start=(j == 0), stop=(j == NZ - 1))
                        if j + 2 < NZ:
                            harmonics(i, k, j + 2)
                    last.then_inc(e3_K, 1)
                    pe.wait_ge(e3_h, g * 2 + 2)
                    pe.wait_ge(e3_q, g + 1)
                    pe.matmul(bank[7][:], w2k[D:128, :], hk[D:128, :], start=True, stop=True).then_inc(e3_Wk, 1)
                    wait(pe, e3_vw, g)
                    for t in range(GT):
                        for j in range(NZ):
                            m = 128 if j < NZ - 1 else D
                            last = pe.matmul(bank[6][:, t * 128:(t + 1) * 128], z[0:m, k % 2, j, t * 128:(t + 1) * 128], cv[0:m, j, :],
                                             start=(j == 0), stop=(j == NZ - 1))
                    last.then_inc(e3_V, 1)
                    pe.wait_ge(e3_wk, g + 1)
                    for t in range(GT):
                        last = pe.matmul(bank[7][:, t * 128:(t + 1) * 128], hv[:, t * 128:(t + 1) * 128], w2v[:], start=True, stop=True)
                    last.then_inc(e3_Wv, 1)
                    pe.wait_ge(e3_pr, g + 1)
                    if kk == 0:
                        wait(pe, S3["ex"], i * 4 + s * 2)
                    for t in range(GT):
                        o = (kk * GT + t) * 8
                        last = pe.matmul(bank[4][:, o:o + 8], kt[:, t * 128:(t + 1) * 128], hsel[:], start=True, stop=True)
                    last.then_inc(e3_P, 1)
                    if kk == KG - 1:
                        softmax_pe(pe, S3, i * 2 + s, bank[4][:, 128:160], 8, sel8, 2)
                each_group(pe, body)
                for k in range(KG, UG):
                    sums(NI - 1, k, 0)
                    sums(NI - 1, k, 1)

            @block.vector
            def _(dve):
                dve.memset(M3[:], 0.0).then_inc(e3_i, 1)
                dve.memset(crow[:], -BIG).then_inc(e3_i, 1)
                dve.memset(hv[D:D + 1, :], 1.0).then_inc(e3_i, 1)
                dve.tensor_reduce(hsel[:], ident[:].rearrange("p (h c) -> p h c", h=8), AX.X, ALU.add).then_inc(e3_i, 1)
                dve.wait_ge(e3_i, 4)

                def values(i, k):
                    g = i * UG + k
                    s, kk = k // KG, k % KG
                    wait(dve, e3_S, (g - 1) * 2)
                    dve.wait_ge(S3["ex"], (i * 2 + s) * 2 + 2)
                    w = ex[:, s, 0, :].rearrange("p (h t) -> p t h", h=8)[:, kk * GT:(kk + 1) * GT, :]
                    dve.tensor_tensor(M3[:, k % 2, :, 0, :].rearrange("p t (h c) -> p t h c", h=8),
                                      vw[:, k * GT:(k + 1) * GT, :].rearrange("p t (h c) -> p t h c", h=8),
                                      w.unsqueeze(3).to_broadcast([128, GT, 8, 16]), ALU.mult).then_inc(e3_M, 1)

                def add_sums(i, k):
                    g = i * UG + k
                    s, kk = k // KG, k % KG
                    for t in range(GT):
                        b = base_of(dve, i, k, t)
                        wait(dve, e3_acc, g * 8 + 2 * t)
                        a = acc[:, 0:2, bass.ds(b, 1)]
                        dve.tensor_tensor(a, a, fac[:, s, 0:2, kk * GT + t:kk * GT + t + 1], ALU.mult).then_inc(e3_acc, 1)
                        dve.wait_ge(e3_acc, g * 8 + (2 * t + 1))
                        dve.wait_ge(e3_S, g * 2 + (t // 2 + 1))
                        a = acc[:, 0:2, bass.ds(b, W)]
                        dve.tensor_tensor(a, a, bank[7][:, (t % 2) * 256:(t % 2 + 1) * 256].rearrange("p (r n) -> p r n", r=2),
                                          ALU.add).then_inc(e3_acc, 1)

                def body(i, k):
                    g = i * UG + k
                    s = k // KG
                    q = i * 2 + s
                    old = back(i, k, KG)
                    if old:
                        values(*old)
                    wait(dve, e3_S, g * 2 - 14)
                    one_hot_ring_step(one, dve, i, k, e3_one)
                    if old:
                        add_sums(*old)
                    wait(dve, e3_V, g - 1)
                    dve.wait_ge(e3_xT, g + 1)
                    for j in range(NZ):
                        m = 128 if j < NZ - 1 else D
                        dve.wait_ge(e3_sh, g * NZ + (j + 1))
                        dve.tensor_tensor(z[0:m, k % 2, j, :], bank[1 + (k * NZ + j) % 2][0:m, :], xT[0:m, :], ALU.mult).then_inc(e3_z, 1)
                    dve.wait_ge(e3_K, g + 1)
                    dve.wait_ge(e3_wk, g + 1)
                    wait(dve, e3_P, g)
                    dve.tensor_tensor(kt[:], bank[5][:], wks[:], ALU.mult).then_inc(e3_kt, 1)
                    dve.wait_ge(e3_kt, g + 1)
                    dve.wait_ge(e3_q, g + 1)
                    dve.tensor_tensor(kt[:], kt[:], qs[:], ALU.mult).then_inc(e3_pr, 1)
                    dve.wait_ge(e3_V, g + 1)
                    dve.wait_ge(e3_wv, g + 1)
                    dve.tensor_tensor(vw[:, k * GT:(k + 1) * GT, :], bank[6][:].rearrange("p (t f) -> p t f", t=GT), wvs[:],
                                      ALU.mult).then_inc(e3_vw, 1)
                    if k % KG < KG - 1:
                        return

                    def scores(c):
                        if c is None:
                            return 1
                        dve.wait_ge(e3_P, g + 1)
                        c.link(dve.tensor_copy(am[:].rearrange("p (h t) -> p h t", h=8),
                                               bank[4][:, 0:128].rearrange("p (t h) -> p h t", h=8)))

                    def after(c, m):
                        dve.tensor_tensor(ex[:, s, 0, :], am[:], m, ALU.subtract).then_inc(S3["pen"], 1)
                        dve.wait_ge(S3["pen"], q + 1)
                        dve.sem_inc(S3["sub"], 1)
                    softmax_dve(dve, S3, q, i * UT + s * SG, s, 8, scores, after)
                each_group(dve, body)
                for k in range(KG, UG):
                    values(NI - 1, k)
                    add_sums(NI - 1, k)
        layer.close()

        m3_r, m3_b, m3_u, m3_m, m3_c, m3_dve, m3_sd, m3_t, m3_x, m3_o = [sem("m3_" + x) for x in
            ("r", "b", "u", "m", "c", "dve", "sd", "t", "x", "o")]
        OT = tmp("OT", [D, N])
        sq = tmp("sq", [D, N])
        rden = tmp("rden", [8, N])
        bn = tmp("bn", [D, 8])
        CH = rounds(N, 512)
        with nc.Block() as block:
            @block.vector
            def _(dve):
                c = Chain(dve, m3_r)
                c.link(dve.tensor_scalar(rden[:], acc[0:8, 1, 0:N], 1e-16, None, ALU.add))
                c.mark(dve.reciprocal(rden[:], rden[:]))
                for n, (a, w) in enumerate(CH):
                    dve.wait_ge(m3_b, n + 1)
                    dve.tensor_tensor(acc[:, 0, a:a + w], acc[:, 0, a:a + w], bank[n % 2][:, 0:w], ALU.mult).then_inc(m3_u, 1)
                dve.wait_ge(m3_c, len(CH))
                c = Chain(dve, m3_dve)
                c.link(dve.tensor_reduce(bn[:, 0:1], OT[:], AX.X, ALU.add))
                c.link(dve.tensor_scalar(bn[:, 1:2], bn[:, 0:1], -1.0 / N, None, ALU.mult))
                c.link(dve.tensor_scalar(OT[:], OT[:], bn[:, 1:2], None, ALU.add))
                c.link(dve.tensor_tensor(sq[:], OT[:], OT[:], ALU.mult))
                c.link(dve.tensor_reduce(bn[:, 2:3], sq[:], AX.X, ALU.add))
                c.link(dve.tensor_scalar(bn[:, 3:4], bn[:, 2:3], 1.0 / N, EPS, ALU.mult, ALU.add))
                dve.wait_ge(m3_sd, 1)
                c.link(dve.reciprocal(bn[:, 5:6], bn[:, 4:5]))
                c.link(dve.tensor_tensor(bn[:, 6:7], bn[:, 5:6], gcol[:], ALU.mult))
                c.link(dve.tensor_scalar(OT[:], OT[:], bn[:, 6:7], bcol[:, 0:1], ALU.mult, ALU.add))
                for r, (j0, n) in enumerate(rounds(NJ, 4)):
                    dve.wait_ge(m3_t, r + 1)
                    dve.tensor_tensor(X[:, j0:j0 + n, :], X[:, j0:j0 + n, :],
                                      bank[4 + r % 2][0:PN, 0:n * D].rearrange("p (j f) -> p j f", j=n), ALU.add).then_inc(m3_x, 1)

            @block.tensor
            def _(pe):
                pe.wait_ge(m3_r, 2)
                for n, (a, w) in enumerate(CH):
                    if n >= 2:
                        pe.wait_ge(m3_u, n - 1)
                    pe.matmul(bank[n % 2][:, 0:w], sel_b[:], rden[:, a:a + w], start=True, stop=True).then_inc(m3_b, 1)
                    pe.wait_ge(m3_u, n + 1)
                    if n >= 2:
                        pe.wait_ge(m3_c, n - 1)
                    pe.matmul(bank[2 + n % 2][0:D, 0:w], w_self[:], HT[:, a:a + w], start=True, stop=False)
                    pe.matmul(bank[2 + n % 2][0:D, 0:w], w_out[:], acc[:, 0, a:a + w], start=False, stop=True).then_inc(m3_m, 1)
                pe.wait_ge(m3_dve, 9)
                for r, (j0, n) in enumerate(rounds(NJ, 4)):
                    if r >= 2:
                        pe.wait_ge(m3_x, r - 1)
                    for j in range(n):
                        last = pe.transpose(bank[4 + r % 2][0:PN, j * D:(j + 1) * D], OT[:, (j0 + j) * PN:(j0 + j + 1) * PN],
                                            ident[0:D, 0:D])
                    last.then_inc(m3_t, 1)

            @block.scalar
            def _(act):
                for n, (a, w) in enumerate(CH):
                    act.wait_ge(m3_m, n + 1)
                    act.activation(OT[:, a:a + w], bank[2 + n % 2][0:D, 0:w], ACT.Copy).then_inc(m3_c, 1)
                act.wait_ge(m3_dve, 6)
                act.activation(bn[:, 4:5], bn[:, 3:4], ACT.Sqrt).then_inc(m3_sd, 1)

            @block.sync
            def _(sp):
                o = out.rearrange("(j p) f -> p j f", p=PN)
                for r, (j0, n) in enumerate(rounds(NJ, 4)):
                    sp.wait_ge(m3_x, r + 1)
                    sp.dma_start(o[:, j0:j0 + n, :], X[:, j0:j0 + n, :]).then_inc(m3_o, 16)
                sp.wait_ge(m3_o, 16 * len(rounds(NJ, 4)))
        end_of_layer()


def kernel(**inputs):
    import numpy as np
    import concourse.bacc as bacc
    from concourse.bass_utils import run_bass_kernel_spmd as run

    nc = bacc.Bacc("TRN2", target_bir_lowering=False, num_devices=1)
    a = {k: np.asarray(v) for k, v in inputs.items()}
    fill = EP - E

    def rows(v, value):
        return np.pad(v, (0, fill), constant_values=value)

    a["src"] = rows(a["src"], 0).reshape(NT, W).T
    a["dst"] = rows(a["dst"], -1).reshape(NT, W).T
    dst = a["dst"].T.reshape(-1)
    a["dst_before"] = np.concatenate([np.full(1, -2, dst.dtype), dst[:-1]]).reshape(NT, W).T
    a["rel"] = rows(a.pop("edge_type_8"), 0).reshape(1, EP)
    a["ea16"] = np.pad(a.pop("edge_attr_16"), ((0, fill), (0, 0))).T
    a["ea64"] = np.pad(a.pop("edge_attr_64"), ((0, fill), (0, 0))).T
    a["ea9"] = np.pad(a.pop("edge_attr_9"), ((0, fill), (0, 0))).T
    a["L2_gnn_WT"] = a.pop("L2_gnn_W").T
    for k, v in a.items():
        a[k] = np.ascontiguousarray(v.reshape(1, -1) if v.ndim == 1 else v)
    arrays = {f"in_{k}": v for k, v in a.items()}
    aps = {k: nc.dram_tensor(f"in_{k}", v.shape, mybir.dt.from_np(v.dtype), kind="ExternalInput").ap() for k, v in a.items()}
    out = nc.dram_tensor("out_x", (N, D), F32, kind="ExternalOutput").ap()
    build(nc, aps, out)
    return run(nc, [arrays], core_ids=[0]).results[0]["out_x"]
```

```python
from contextlib import ExitStack

import concourse.bass as bass
from concourse import mybir

F32 = mybir.dt.float32
BF16 = mybir.dt.bfloat16
I32 = mybir.dt.int32
ALU = mybir.AluOpType
ACT = mybir.ActivationFunctionType
AX = mybir.AxisListType

N = 3125
D = 64
E = 53125
PN = 125
NJ = N // PN
W = 128
NT = -(-E // (32 * W)) * 32
EP = NT * W
GT = 4
UG = 8
UT = GT * UG
NI = NT // UT
NW = N + W
REL = 8
EPS = 1e-5
SLOPE = 0.2
BIG = 1e30
GCOL = 128
LAST = "L3"
STAGES = ["L0", "L1", "L2", "L3"]


def wait(eng, sem, value):
    if not isinstance(value, int) or value > 0:
        eng.wait_ge(sem, value)


class Chain:

    def __init__(self, eng, sem):
        self.eng, self.sem, self.n = eng, sem, 0

    def mark(self, ins):
        self.n += 1
        ins.then_inc(self.sem, 1)

    def link(self, ins):
        self.mark(ins)
        self.eng.wait_ge(self.sem, self.n)


class LoopChain:

    def __init__(self, eng, sem, i, steps):
        self.eng, self.sem, self.at, self.k, self.steps = eng, sem, i * steps, 0, steps

    def link(self, ins):
        self.mark(ins)
        self.eng.wait_ge(self.sem, self.at + self.k)

    def mark(self, ins):
        self.k += 1
        ins.then_inc(self.sem, 1)

    def done(self):
        assert self.k == self.steps, (self.k, self.steps)


def rounds(n, k):
    return [(a, min(k, n - a)) for a in range(0, n, k)]


def build(nc, A, out):
    with ExitStack() as ctx:
        def sb(name, shape, dt=F32):
            return ctx.enter_context(nc.sbuf_tensor(name, shape, dt))

        layer = ExitStack()
        sems = []

        def tmp(name, shape, dt=F32):
            return layer.enter_context(nc.sbuf_tensor(name, shape, dt))

        def sem(name):
            sems.append(nc.alloc_semaphore(name=name))
            return sems[-1]

        def end_of_layer():
            layer.close()
            nc.clear_and_free_semaphores(sems)
            sems.clear()
            nc.all_engine_barrier()

        def dram(name, shape, dt=F32):
            return nc.dram_tensor(name, shape, dt, kind="Internal").ap()

        bank = [ctx.enter_context(nc.psum_tensor(f"bank{b}", [128, 512], F32)) for b in range(8)]

        X = sb("X", [PN, NJ, D])
        H = sb("H", [PN, NJ, D])
        HT = sb("HT", [D, N])
        acc = sb("acc", [128, 3, NW])
        ident = sb("ident", [128, 128])
        iota_row = sb("iota_row", [128, 128])
        iota_i = sb("iota_i", [128, 128], I32)
        iota_p = sb("iota_p", [128, 1])
        iota_pi = sb("iota_pi", [128, 1], I32)
        src_i = sb("src_i", [128, NT], I32)
        dst_i = sb("dst_i", [128, NT], I32)
        base_i = sb("base_i", [128, NT], I32)
        dloc = sb("dloc", [128, NT])
        base_f = sb("base_f", [128, NT])
        edge_a = sb("edge_a", [128, NT, 4])
        st = sb("st", [PN, 8, NJ])
        cnt = sb("cnt", [PN, NJ])
        zero = sb("zero", [128, 256])
        idx = sb("idx", [128, UT], I32)

        loop_a = sb("loop_a", [PN, NJ, 4])

        w1 = sb("w1", [D, 2, D])
        wre = sb("wre", [REL + 16, D + 4])
        b1r = sb("b1r", [REL, D])
        w2x = sb("w2x", [D + 5, D + 5])
        wedge = sb("wedge", [16, 4, 64])
        atte = sb("atte", [16, 4, 64])
        v16 = sb("v16", [16, 4])

        s_done = {}

        TA = dram("TA", [N, D])
        TB = dram("TB", [NW, D])
        DL = dram("DL", [1, EP], BF16)

        l_x, l_i, l_w0 = sem("l_x"), sem("l_i"), sem("l_w0")
        c_pool, c_dve, c_zero = sem("c_pool"), sem("c_dve"), sem("c_zero")
        l_zero, l_d, l_dl = sem("l_zero"), sem("l_d"), sem("l_dl")
        dr_i = tmp("dr_i", [NT // GT, GT, W], I32)
        dr_f = tmp("dr_f", [NT // GT, GT, W])
        dr_b = tmp("dr_b", [NT // GT, GT, W], BF16)
        with nc.Block() as block:
            @block.sync
            def _(sp):
                sp.dma_start(X[:], A["x"].rearrange("(j p) f -> p j f", p=PN)).then_inc(l_x, 16)
                sp.dma_start(dr_i[:], A["dst_rows"].rearrange("(p t) e -> p t e", t=GT)).then_inc(l_d, 16)
                sp.dma_start(src_i[:], A["src"]).then_inc(l_i, 16)
                sp.dma_start(dst_i[:], A["dst"]).then_inc(l_i, 16)
                sp.dma_start(base_i[:], A["dst"][0:1, :].partition_broadcast(128)).then_inc(l_i, 16)
                w1d = A["L0_gnn_W1"]
                sp.dma_start(w1[:], w1d[0:2 * D, :].rearrange("(a k) n -> k a n", a=2)).then_inc(l_w0, 16)
                sp.dma_start(b1r[:], A["L0_gnn_b1"].partition_broadcast(REL)).then_inc(l_w0, 16)
                sp.wait_ge(c_zero, 1)
                sp.dma_start(wre[0:REL, 0:D], w1d[2 * D:2 * D + REL, :]).then_inc(l_w0, 16)
                sp.dma_start(w2x[0:D, 0:D], A["L0_gnn_W2"]).then_inc(l_w0, 16)
                sp.dma_start(w2x[D:D + 1, 0:D], A["L0_gnn_b2"]).then_inc(l_w0, 16)
                sp.dma_start(wedge[:], A["L1_gnn_W_edge"].rearrange("k (h c) -> k h c", h=4)).then_inc(l_w0, 16)
                sp.dma_start(atte[:], A["L1_gnn_att_edge"].partition_broadcast(16)).then_inc(l_w0, 16)
                sp.wait_ge(c_dve, 2)
                sp.dma_start(TB[N:NW, :], zero[:, 0:D]).then_inc(l_zero, 16)
                sp.wait_ge(c_dve, 12)
                sp.dma_start(DL.rearrange("o (p f) -> (o p) f", p=NT // GT), dr_b[:].rearrange("p t e -> p (t e)")).then_inc(l_dl, 16)
                sp.dma_start(wre[REL:REL + 16, D:D + 4], v16[:]).then_inc(l_dl, 16)
                sp.wait_ge(l_dl, 32)
                sp.wait_ge(l_zero, 16)
                sp.wait_ge(l_x, 16)
                sp.wait_ge(l_i, 48)
                sp.wait_ge(l_w0, 7 * 16)

            @block.gpsimd
            def _(pool):
                pool.memset(w2x[:], 0.0).then_inc(c_pool, 1)
                pool.memset(wre[:], 0.0).then_inc(c_pool, 1)
                pool.memset(ident[:], 0.0).then_inc(c_pool, 1)
                pool.iota(iota_i[:], [[1, 128]], 0, 0).then_inc(c_pool, 1)
                pool.iota(iota_pi[:], [[0, 1]], 0, 1).then_inc(c_pool, 1)
                pool.wait_ge(c_pool, 5)
                pool.affine_select(out=ident[:], in_=ident[:], compare_op=ALU.not_equal, fill=1.0, base=0,
                                   pattern=[[-1, 128]], channel_multiplier=1).then_inc(c_pool, 1)
                pool.affine_select(out=w2x[:, D:D + 5], in_=w2x[:, D:D + 5], compare_op=ALU.not_equal, fill=1.0,
                                   base=-D, pattern=[[-1, 5]], channel_multiplier=1).then_inc(c_zero, 1)

            @block.vector
            def _(dve):
                c = Chain(dve, c_dve)
                c.mark(dve.memset(acc[:], 0.0))
                c.mark(dve.memset(zero[:], 0.0))
                dve.wait_ge(c_pool, 5)
                c.mark(dve.tensor_copy(iota_row[:], iota_i[:]))
                c.mark(dve.tensor_copy(iota_p[:], iota_pi[:]))
                dve.wait_ge(l_i, 48)
                c.mark(dve.tensor_copy(dloc[:], dst_i[:]))
                c.link(dve.tensor_copy(base_f[:], base_i[:]))
                c.mark(dve.tensor_tensor(dloc[:], dloc[:], base_f[:], ALU.subtract))
                dve.wait_ge(l_w0, 7 * 16)
                c.mark(dve.tensor_tensor(wre[0:REL, 0:D], wre[0:REL, 0:D], b1r[:], ALU.add))
                c.link(dve.tensor_tensor(wedge[:], wedge[:], atte[:], ALU.mult))
                c.mark(dve.tensor_reduce(v16[:], wedge[:], AX.X, ALU.add))
                dve.wait_ge(l_d, 16)
                c.link(dve.tensor_copy(dr_f[:], dr_i[:]))
                c.mark(dve.tensor_tensor(dr_b[:], dr_f[:], dr_f[:, :, 0:1].to_broadcast([NT // GT, GT, W]), ALU.subtract))

        layer.close()

        def node_buffers(p):
            return tmp(p + "_XC", [PN, NJ, D]), tmp(p + "_yn", [PN, NJ, D]), tmp(p + "_tab", [PN, NJ, 2 * D])

        def ln_relu_steps(c, s_var, s_std, n, dst=H, src=X, relu=True, XC=None):
            dve = c.eng
            bc = lambda r: st[:, r, :].unsqueeze(2).to_broadcast([PN, NJ, D])
            c.link(dve.tensor_reduce(st[:, 0, :], src[:], AX.X, ALU.add))
            c.link(dve.tensor_scalar(st[:, 1, :], st[:, 0, :], -1.0 / D, None, ALU.mult))
            c.link(dve.tensor_tensor(XC[:], src[:], bc(1), ALU.add))
            c.link(dve.tensor_tensor(dst[:], XC[:], XC[:], ALU.mult))
            c.link(dve.tensor_reduce(st[:, 2, :], dst[:], AX.X, ALU.add))
            dve.tensor_scalar(st[:, 3, :], st[:, 2, :], 1.0 / D, EPS, ALU.mult, ALU.add).then_inc(s_var, 1)
            dve.wait_ge(s_std, n)
            c.link(dve.reciprocal(st[:, 5, :], st[:, 4, :]))
            c.link(dve.tensor_tensor(dst[:], XC[:], bc(5), ALU.mult))
            if relu:
                c.link(dve.tensor_scalar(dst[:], dst[:], 0.0, None, ALU.max))

        def ln_std_step(act, s_var, s_std, n):
            act.wait_ge(s_var, n)
            act.activation(st[:, 4, :], st[:, 3, :], ACT.Sqrt).then_inc(s_std, 1)

        def transpose_steps(pe, s_t, s_free, src=H):
            for r, (j0, n) in enumerate(rounds(NJ, 4)):
                if r >= 2:
                    pe.wait_ge(s_free, r - 1)
                for j in range(n):
                    last = pe.transpose(bank[r % 2][0:D, j * PN:(j + 1) * PN], src[:, j0 + j, :], ident[0:PN, 0:PN])
                last.then_inc(s_t, 1)

        def transposed_copy_steps(act, s_t, s_free, dst=HT):
            for r, (j0, n) in enumerate(rounds(NJ, 4)):
                act.wait_ge(s_t, r + 1)
                act.activation(dst[0:D, j0 * PN:(j0 + n) * PN], bank[r % 2][0:D, 0:n * PN], ACT.Copy).then_inc(s_free, 1)

        def gather_program(ga, pool, table, width, s_g, s_used, s_idx, s_step, ring=UG, per=1):
            def half(i, hh):
                for k in range(hh * 4, hh * 4 + 4):
                    wait(pool, s_g[k], i * 64)
                pool.tensor_copy(idx[:, hh * 16:hh * 16 + 16], src_i[:, bass.ds(i * UT + hh * 16, 16)]).then_inc(s_idx, 1)
                pool.wait_ge(s_idx, i * 2 + (hh + 1))
                pool.sem_inc(s_step, 1)
                for k in range(hh * 4, hh * 4 + 4):
                    if not isinstance(i, int) or k >= ring:
                        pool.wait_ge(s_used, (i * UG + (k - ring + 1)) * per)
                        pool.sem_inc(s_step, 1)
                    for t in range(GT):
                        o = ga[:, (k % ring) * GT + t, 0:width]
                        pool.indirect_dma_start(o, None, table, bass.IndirectOffsetOnAxis(
                            ap=idx[:, k * GT + t:k * GT + t + 1], axis=0)).then_inc(s_g[k], 16)
            for hh in range(2):
                half(0, hh)
            with pool.Fori(1, NI) as i:
                for hh in range(2):
                    half(i, hh)

        def each_group(eng, body):
            for k in range(UG):
                body(0, k)
            with eng.Fori(1, NI) as i:
                for k in range(UG):
                    body(i, k)

        def before(i, k):
            if k:
                return i, k - 1
            return None if isinstance(i, int) and i == 0 else (i - 1, UG - 1)

        def back(i, k, n):
            if k >= n:
                return i, k - n
            return None if isinstance(i, int) and i == 0 else (i - 1, UG + k - n)

        def base_of(eng, i, k, t):
            return eng.value_load(base_i[0:1, bass.ds(i * UT + (k * GT + t), 1)], min_val=0, max_val=N - 1)

        def bases_of(eng, i, k):
            _, values = nc.values_load_multi_w_load_instructions(
                base_i[0:1, bass.ds(i * UT + k * GT, GT)], engines=[eng.engine], min_val=0, max_val=N - 1,
                skip_runtime_bounds_check_because="a destination is a node")
            return values

        def window_loads(win, eng, i, k, table, width, s_w, s_used, s_step, tiles=range(GT), ring=UG):
            starts = bases_of(eng, i, k)
            wait(eng, s_used, i * UG + (k - ring + 1))
            eng.sem_inc(s_step, 1)
            for t in tiles:
                b = starts[t]
                eng.dma_start(win[:, (k % ring) * GT + t, 0:width], table[bass.ds(b, W), :]).then_inc(s_w[k % ring], 16)

        DR = 4

        def place_load(dl, eng, i, k, s_dl, s_oT, s_step):
            wait(eng, s_oT, i * UG + (k - DR + 1))
            eng.sem_inc(s_step, 1)
            cols = bass.ds((i * UG + k) * GT * W, GT * W)
            eng.dma_start(dl[:, k % DR, :], DL[:, cols].partition_broadcast(128)).then_inc(s_dl[k % DR], 16)

        def transposed_one_hot_step(o, dl, dve, i, k, s_dl, s_oT):
            dve.wait_ge(s_dl[k % DR], i * (UG // DR * 16) + (k // DR + 1) * 16)
            dve.tensor_scalar(o, dl[:, k % DR, :], iota_p[:, 0:1], None, ALU.is_equal).then_inc(s_oT, 1)

        def one_hot_ring_step(one, dve, i, k, s_one):
            dve.tensor_tensor(one[:, k * GT:(k + 1) * GT, :], iota_row[:].unsqueeze(1).to_broadcast([128, GT, 128]),
                              dloc[:, bass.ds(i * UT + k * GT, GT)].unsqueeze(2).to_broadcast([128, GT, 128]),
                              ALU.is_equal).then_inc(s_one, 1)

        n0_dve, n0_var, n0_std, n0_t, n0_tc, n0_m, n0_mc, n0_o = [sem("n0_" + x) for x in
            ("dve", "var", "std", "t", "tc", "m", "mc", "o")]
        XC, yn, tab = node_buffers("n0")
        with nc.Block() as block:
            @block.vector
            def _(dve):
                c = Chain(dve, n0_dve)
                ln_relu_steps(c, n0_var, n0_std, 1, XC=XC)

            @block.scalar
            def _(act):
                ln_std_step(act, n0_var, n0_std, 1)
                transposed_copy_steps(act, n0_t, n0_tc)
                for r, (j0, n) in enumerate(rounds(NJ, 4)):
                    act.wait_ge(n0_m, r + 1)
                    act.activation(tab[:, j0:j0 + n, :], bank[2 + r % 2][0:PN, 0:n * 128].rearrange("p (j f) -> p j f", j=n),
                                   ACT.Copy).then_inc(n0_mc, 1)

            @block.tensor
            def _(pe):
                pe.wait_ge(n0_dve, 8)
                transpose_steps(pe, n0_t, n0_tc)
                for r, (j0, n) in enumerate(rounds(NJ, 4)):
                    pe.wait_ge(n0_tc, r + 1)
                    if r >= 2:
                        pe.wait_ge(n0_mc, r - 1)
                    for j in range(n):
                        last = pe.matmul(bank[2 + r % 2][0:PN, j * 128:(j + 1) * 128], HT[:, (j0 + j) * PN:(j0 + j + 1) * PN],
                                         w1[:].rearrange("k a n -> k (a n)"), start=True, stop=True)
                    last.then_inc(n0_m, 1)

            @block.sync
            def _(sp):
                sp.wait_ge(n0_mc, len(rounds(NJ, 4)))
                sp.dma_start(TA.rearrange("(j p) f -> p j f", p=PN), tab[:, :, 0:D]).then_inc(n0_o, 16)
                sp.dma_start(TB[0:N, :].rearrange("(j p) f -> p j f", p=PN), tab[:, :, D:2 * D]).then_inc(n0_o, 16)
                sp.wait_ge(n0_o, 32)

        layer.close()

        e0_g = [sem(f"e0_g{k}") for k in range(UG)]
        e0_w = [sem(f"e0_w{k}") for k in range(UG)]
        e0_e = [sem(f"e0_e{k}") for k in range(2)]
        e0_dl = [sem(f"e0_dl{k}") for k in range(DR)]
        e0_idx, e0_step, e0_sp, e0_act, e0_one, e0_oT, e0_rel, e0_P, e0_pre, e0_ms, e0_S, e0_acc = [sem("e0_" + x) for x in
            ("idx", "step", "sp", "act", "one", "oT", "rel", "P", "pre", "ms", "S", "acc")]
        ga = tmp("ga0", [128, UT, D])
        win = tmp("win0", [128, UT, D])
        one = tmp("one0", [128, UT, 128])
        oneT = tmp("oneT0", [128, 2, GT * W])
        dl = tmp("dl0", [128, DR, GT * W], BF16)
        rel_i = tmp("rel_i", [REL, 2, GT * W], I32)
        re = tmp("re", [REL + 16, 2, GT * W])
        pre = tmp("pre", [128, 2, GT, D])
        msg = tmp("msg", [128, 2, GT, D + 5])
        MS = D + 5
        e0_ones = sem("e0_ones")
        with nc.Block() as block:
            @block.gpsimd
            def _(pool):
                pool.memset(msg[:, :, :, D:D + 1], 1.0).then_inc(e0_ones, 1)
                gather_program(ga, pool, TA, D, e0_g, e0_pre, e0_idx, e0_step)

            @block.sync
            def _(sp):
                def body(i, k):
                    place_load(dl, sp, i, k, e0_dl, e0_oT, e0_sp)
                    window_loads(win, sp, i, k, TB, D, e0_w, e0_P, e0_sp, range(0, GT // 2))
                each_group(sp, body)

            @block.scalar
            def _(act):
                def loads(i, k):
                    wait(act, e0_P, i * UG + (k - 1))
                    wait(act, e0_rel, i * UG + (k - 1))
                    cols = bass.ds((i * UG + k) * GT * W, GT * W)
                    act.dma_start(rel_i[:, k % 2, :], A["rel"][:, cols].partition_broadcast(REL)).then_inc(e0_e[k % 2], 16)
                    act.dma_start(re[REL:REL + 16, k % 2, :], A["ea16"][:, cols]).then_inc(e0_e[k % 2], 16)
                    window_loads(win, act, i, k, TB, D, e0_w, e0_P, e0_act, range(GT // 2, GT))

                def messages(i, k):
                    g = i * UG + k
                    P = bank[k % 2][:, 0:GT * (D + 4)].rearrange("p (t f) -> p t f", t=GT)
                    act.wait_ge(e0_pre, g + 1)
                    wait(act, e0_S, g - 1)
                    act.activation(msg[:, k % 2, :, 0:D], pre[:, k % 2], ACT.Relu).then_inc(e0_ms, 1)
                    act.activation(msg[:, k % 2, :, D + 1:MS], P[:, :, D:D + 4], ACT.Copy).then_inc(e0_ms, 1)
                    act.activation(edge_a[:, bass.ds(g * GT, GT), :], P[:, :, D:D + 4], ACT.Copy).then_inc(e0_ms, 1)

                def body(i, k):
                    loads(i, k)
                    if before(i, k):
                        messages(*before(i, k))
                act.wait_ge(e0_ones, 1)
                each_group(act, body)
                messages(NI - 1, UG - 1)

            @block.tensor
            def _(pe):
                def sums(i, k):
                    g = i * UG + k
                    pe.wait_ge(e0_ms, g * 3 + 3)
                    wait(pe, e0_acc, (g - 1) * GT)
                    for t in range(GT):
                        last = pe.matmul(bank[4 + k % 2][0:MS, t * 128:(t + 1) * 128], msg[:, k % 2, t, :], one[:, k * GT + t, :],
                                         start=True, stop=True)
                    last.then_inc(e0_S, 1)

                def body(i, k):
                    g = i * UG + k
                    pe.wait_ge(e0_oT, g + 1)
                    pe.wait_ge(e0_rel, g + 1)
                    pe.wait_ge(e0_w[k], i * 64 + 64)
                    wait(pe, e0_ms, (g - 1) * 3)
                    for t in range(GT):
                        o = t * (D + 4)
                        P = bank[k % 2]
                        pe.matmul(P[:, o:o + D + 4], re[:, k % 2, t * W:(t + 1) * W], wre[:], start=True, stop=False)
                        last = pe.matmul(P[:, o:o + D], oneT[:, k % 2, t * 128:(t + 1) * 128], win[:, k * GT + t, 0:D],
                                         start=False, stop=True)
                    last.then_inc(e0_P, 1)
                    if back(i, k, 2):
                        sums(*back(i, k, 2))
                each_group(pe, body)
                sums(NI - 1, UG - 2)
                sums(NI - 1, UG - 1)

            @block.vector
            def _(dve):
                def add_sums(i, k, starts):
                    g = i * UG + k
                    dve.wait_ge(e0_S, g + 1)
                    for t, b in enumerate(starts):
                        wait(dve, e0_acc, g * GT + t)
                        a = acc[0:MS, 0, bass.ds(b, W)]
                        dve.tensor_tensor(a, a, bank[4 + k % 2][0:MS, t * 128:(t + 1) * 128], ALU.add).then_inc(e0_acc, 1)

                def with_gathered(i, k):
                    g = i * UG + k
                    dve.wait_ge(e0_P, g + 1)
                    dve.wait_ge(e0_g[k], i * 64 + 64)
                    wait(dve, e0_ms, (g - 1) * 3)
                    P = bank[k % 2][:, 0:GT * (D + 4)].rearrange("p (t f) -> p t f", t=GT)
                    dve.tensor_tensor(pre[:, k % 2], ga[:, k * GT:(k + 1) * GT, 0:D], P[:, :, 0:D], ALU.add).then_inc(e0_pre, 1)

                def body(i, k):
                    g = i * UG + k
                    wait(dve, e0_S, g - 7)
                    one_hot_ring_step(one, dve, i, k, e0_one)
                    wait(dve, e0_P, g - 1)
                    transposed_one_hot_step(oneT[:, k % 2, :], dl, dve, i, k, e0_dl, e0_oT)
                    dve.wait_ge(e0_e[k % 2], i * (UG // 2 * 32) + (k // 2 + 1) * 32)
                    dve.tensor_scalar(re[0:REL, k % 2, :], rel_i[:, k % 2, :], iota_p[0:REL, 0:1], None, ALU.is_equal).then_inc(e0_rel, 1)
                    old = back(i, k, 3)
                    if old:
                        starts = bases_of(dve, *old)
                    if before(i, k):
                        with_gathered(*before(i, k))
                    if old:
                        add_sums(*old, starts)
                each_group(dve, body)
                with_gathered(NI - 1, UG - 1)
                for k in range(UG - 3, UG):
                    add_sums(NI - 1, k, bases_of(dve, NI - 1, k))

        layer.close()
        m0_m, m0_dve, m0_c, m0_f = [sem("m0_" + x) for x in ("m", "dve", "c", "f")]
        with nc.Block() as block:
            @block.tensor
            def _(pe):
                for r, (j0, n) in enumerate(rounds(NJ, 4)):
                    if r >= 2:
                        pe.wait_ge(m0_f, r - 1)
                    for j in range(n):
                        last = pe.matmul(bank[r % 2][0:PN, j * 128:j * 128 + MS], acc[0:MS, 0, (j0 + j) * PN:(j0 + j + 1) * PN],
                                         w2x[:], start=True, stop=True)
                    last.then_inc(m0_m, 1)

            @block.vector
            def _(dve):
                c = Chain(dve, m0_dve)
                c.link(dve.tensor_tensor(X[:], X[:], H[:], ALU.add))
                for r, (j0, n) in enumerate(rounds(NJ, 4)):
                    dve.wait_ge(m0_m, r + 1)
                    P = bank[r % 2][0:PN, 0:n * 128].rearrange("p (j f) -> p j f", j=n)
                    c.mark(dve.tensor_tensor(X[:, j0:j0 + n, :], X[:, j0:j0 + n, :], P[:, :, 0:D], ALU.add))
                    c.mark(dve.tensor_copy(cnt[:, j0:j0 + n], P[:, :, D]))
                    c.mark(dve.tensor_copy(loop_a[:, j0:j0 + n, :], P[:, :, D + 1:MS]))
                    dve.wait_ge(m0_dve, c.n)
                    dve.sem_inc(m0_f, 1)

        def finish(stage):
            if LAST != stage:
                return False
            z_o = sem("z_o")
            with nc.Block() as block:
                @block.sync
                def _(sp):
                    sp.dma_start(out.rearrange("(j p) f -> p j f", p=PN), X[:]).then_inc(z_o, 16)
                    sp.wait_ge(z_o, 16)
            return True
        end_of_layer()
        if finish("L0"):
            return

        SG = 16
        KG = SG // GT
        pl = sb("pl", [1, NT])
        ql = sb("ql", [1, NT])
        first = sb("first", [128, NT])
        sel = sb("sel", [128, 3, 128])
        sel8 = sb("sel8", [128, 2, 128])
        delta_t = sb("delta_t", [128, SG])
        dst_f = sb("dst_f", [128, NT])
        al = sb("al", [128, 2, 128])
        am = sb("am", [128, 128])
        lp = sb("lp", [128, 64])
        dsth = sb("dsth", [128, 128])
        dT = sb("dT", [128, 130])
        pen = sb("pen", [128, 129])
        f1 = sb("f1", [128, 128])
        mx = sb("mx", [128, 128])
        mlast = sb("mlast", [128, 1])
        crow = sb("crow", [1, 8, SG + 1])
        prow = sb("prow", [1, 8, SG + 1])
        lrow = sb("lrow", [1, 8, SG + 1])
        cshift = sb("cshift", [1, 8, SG])
        ccol = sb("ccol", [128, 1])
        cm = sb("cm", [128, 1])
        fdiag = sb("fdiag", [128, SG])
        fac = sb("fac", [128, 2, 3, SG])
        ex = sb("ex", [128, 2, 2, 128])
        s_b = {}

        def softmax_sems(p):
            return {x: sem(f"{p}_{x}") for x in ("al", "T1", "dT", "pen", "f1", "ml", "cr", "cc", "mx", "cm", "pen2", "pe", "fd", "me",
                                                 "fac", "sub", "ex", "bd")}

        flat = lambda v, heads: v[:, 0:heads, :].rearrange("p h t -> p (h t)")
        rows_of = lambda v, heads: v.unsqueeze(1).to_broadcast([v.shape[0], heads, SG])
        SOFT = 14

        def softmax_dve_0(dve, S, c, c0, heads):
            R = heads * SG
            c.mark(dve.tensor_copy(dsth[:, 0:R].rearrange("p (h t) -> p h t", h=heads), rows_of(dst_f[:, bass.ds(c0, SG)], heads)))
            c.link(dve.tensor_copy(prow[:, 0:heads, 1:SG + 1], rows_of(pl[:, bass.ds(c0, SG)], heads)))
            dve.sem_inc(S["al"], 1)

        def softmax_dve_1(dve, S, c, q, heads):
            R = heads * SG
            dve.wait_ge(S["dT"], q + 1)
            c.link(dve.tensor_tensor(pen[0:R, 1:128], dT[0:R, 1:128], dT[0:R, 0:127], ALU.is_equal))
            c.link(dve.tensor_scalar(pen[0:R, 1:128], pen[0:R, 1:128], -1.0, BIG, ALU.add, ALU.mult))
            c.link(dve.tensor_tensor_scan(f1[0:R, :], pen[0:R, 0:128], bank[3][0:R, 0:128], -BIG, ALU.add, ALU.max))
            dve.sem_inc(S["f1"], 1)

        def softmax_dve_2(dve, S, c, q, c0, heads):
            R = heads * SG
            dve.wait_ge(S["ml"], q + 1)
            c.link(dve.tensor_copy(crow[:, 0:heads, 1:SG + 1], bank[3][0:1, 256:256 + R].rearrange("p (h t) -> p h t", h=heads)))
            c.link(dve.tensor_tensor_scan(flat(lrow, heads), flat(prow, heads), flat(crow, heads), -BIG, ALU.add, ALU.max))
            c.mark(dve.tensor_copy(crow[:, 0:heads, 0:1], lrow[:, 0:heads, SG:SG + 1]))
            c.link(dve.tensor_tensor(cshift[:, 0:heads, :], lrow[:, 0:heads, 0:SG], rows_of(ql[:, bass.ds(c0, SG)], heads), ALU.add))
            dve.sem_inc(S["cr"], 1)

        def softmax_dve_3(dve, S, c, q, heads):
            R = heads * SG
            dve.wait_ge(S["cc"], q + 1)
            c.link(dve.tensor_copy(ccol[0:R, :], bank[3][0:R, 384:385]))
            c.link(dve.tensor_tensor_scan(f1[0:R, :], pen[0:R, 0:128], bank[3][0:R, 0:128], ccol[0:R, 0:1], ALU.add, ALU.max))
            c.link(dve.tensor_tensor_scan(mx[0:R, ::-1], pen[0:R, 128:0:-1], f1[0:R, ::-1], -BIG, ALU.add, ALU.max))
            c.link(dve.tensor_tensor(cm[0:R, :], ccol[0:R, :], mx[0:R, 0:1], ALU.subtract))
            dve.sem_inc(S["mx"], 1)

        def softmax_dve_4(dve, S, c, q, heads):
            R = heads * SG
            dve.wait_ge(S["cm"], q + 1)
            c.link(dve.tensor_scalar(fdiag[0:R, :], delta_t[0:R, :], cm[0:R, 0:1], None, ALU.mult))
            dve.sem_inc(S["fd"], 1)
            c.done()
            dve.wait_ge(S["me"], q + 1)
            return bank[3][:, 128:128 + R]

        def softmax_pe_0(pe, S, q, heads):
            R = heads * SG
            pe.wait_ge(S["al"], q + 1)
            wait(pe, S["ex"], q * 2)
            pe.sem_inc(S["pe"], 1)
            pe.transpose(bank[3][0:R, 0:128], am[:, 0:R], ident[:])
            pe.transpose(bank[3][0:R, 128:256], dsth[:, 0:R], ident[:]).then_inc(S["T1"], 1)

        def softmax_pe_1(pe, S, q, heads):
            R = heads * SG
            pe.wait_ge(S["f1"], q + 1)
            pe.sem_inc(S["pe"], 1)
            pe.transpose(bank[3][0:1, 256:256 + R], f1[0:R, 127:128], ident[0:R, 0:R]).then_inc(S["ml"], 1)

        def softmax_pe_2(pe, S, q, heads):
            R = heads * SG
            pe.wait_ge(S["cr"], q + 1)
            pe.sem_inc(S["pe"], 1)
            pe.transpose(bank[3][0:R, 384:385], flat(cshift, heads), ident[0:1, 0:1]).then_inc(S["cc"], 1)

        def softmax_pe_3(pe, S, q, heads):
            R = heads * SG
            pe.wait_ge(S["mx"], q + 1)
            pe.sem_inc(S["pe"], 1)
            pe.transpose(bank[3][:, 128:128 + R], mx[0:R, :], ident[0:R, 0:R]).then_inc(S["me"], 1)

        def softmax_pe_4(pe, S, q, fb, heads, selm, nr):
            R = heads * SG
            pe.wait_ge(S["fd"], q + 1)
            pe.sem_inc(S["pe"], 1)
            for r in range(nr):
                last = pe.matmul(fb[:, r * SG:(r + 1) * SG], selm[0:R, r, :], fdiag[0:R, :], start=True, stop=True)
            last.then_inc(S["fac"], 1)

        def softmax_act_1(act, S, q, heads):
            act.wait_ge(S["T1"], q + 1)
            act.activation(dT[0:heads * SG, 0:128], bank[3][0:heads * SG, 128:256], ACT.Copy).then_inc(S["dT"], 1)

        def softmax_act_3(act, S, q, heads):
            act.wait_ge(S["mx"], q + 1)
            act.activation(cm[0:heads * SG, :], cm[0:heads * SG, :], ACT.Exp).then_inc(S["cm"], 1)

        def softmax_act_4(act, S, q, s, heads, nex):
            act.wait_ge(S["sub"], q + 1)
            act.activation(ex[:, s, 0:nex, 0:heads * SG], ex[:, s, 0:nex, 0:heads * SG], ACT.Exp).then_inc(S["ex"], 1)

        def softmax_act_5(act, S, q, s, fb, nr):
            act.wait_ge(S["fac"], q + 1)
            act.activation(fac[:, s, 0:nr, :], fb[:, 0:nr * SG].rearrange("p (r t) -> p r t", r=nr), ACT.Copy).then_inc(S["ex"], 1)

        LATE = KG + 1

        def pending(i, k):
            if k % KG or not before(i, k):
                return None
            a, b = before(i, k)
            return a, b // KG

        k_i, k_d, k_l, k_p = sem("k_i"), sem("k_d"), sem("k_l"), sem("k_p")
        dprev = sb("dprev", [128, NT], I32)
        lastr = sb("lastr", [1, NT + 1], I32)
        with nc.Block() as block:
            @block.sync
            def _(sp):
                sp.dma_start(dprev[:], A["dst_before"]).then_inc(k_l, 16)
                sp.wait_ge(k_d, 1)
                sp.dma_start(lastr[:, 1:NT + 1], A["dst"][W - 1:W, :]).then_inc(k_l, 16)

            @block.gpsimd
            def _(pool):
                for m in (sel, sel8, delta_t):
                    pool.memset(m[:], 0.0).then_inc(k_i, 1)
                pool.wait_ge(k_i, 3)
                n = 3
                for h in range(8):
                    pool.affine_select(out=delta_t[:], in_=delta_t[:], compare_op=ALU.not_equal, fill=1.0, base=-h * SG,
                                       pattern=[[-1, SG]], channel_multiplier=1).then_inc(k_i, 1)
                    n += 1
                    pool.wait_ge(k_i, n)
                for m, heads, cw in ((sel, 4, 64), (sel8, 8, 16)):
                    nr = 2 if heads == 4 else 1
                    for r in range(nr):
                        v = m[:, r, :]
                        pool.memset(v, 1.0).then_inc(k_i, 1)
                        n += 1
                        pool.wait_ge(k_i, n)
                        per = 128 // cw
                        vv = v.rearrange("p (a c) -> p a c", a=per)
                        pool.affine_select(out=vv, in_=vv, compare_op=ALU.is_ge, fill=0.0, base=-SG * per * r,
                                           pattern=[[-SG, per], [0, cw]], channel_multiplier=1).then_inc(k_i, 1)
                        n += 1
                        pool.wait_ge(k_i, n)
                        pool.affine_select(out=vv, in_=vv, compare_op=ALU.is_ge, fill=0.0, base=SG * per * r + SG - 1,
                                           pattern=[[SG, per], [0, cw]], channel_multiplier=-1).then_inc(k_i, 1)
                        n += 1
                        pool.wait_ge(k_i, n)
                    reps = 2 if heads == 4 else 1
                    v = m[:, nr, 0:8]
                    pool.memset(v, 1.0).then_inc(k_i, 1)
                    n += 1
                    pool.wait_ge(k_i, n)
                    vv = v.rearrange("p (b h) -> p b h", b=reps)
                    pool.affine_select(out=vv, in_=vv, compare_op=ALU.is_ge, fill=0.0, base=0,
                                       pattern=[[0, reps], [-SG, heads]], channel_multiplier=1).then_inc(k_i, 1)
                    n += 1
                    pool.wait_ge(k_i, n)
                    pool.affine_select(out=vv, in_=vv, compare_op=ALU.is_ge, fill=0.0, base=SG - 1,
                                       pattern=[[0, reps], [SG, heads]], channel_multiplier=-1).then_inc(k_i, 1)
                    n += 1
                    pool.wait_ge(k_i, n)

            @block.vector
            def _(dve):
                c = Chain(dve, k_d)
                c.mark(dve.memset(lastr[:, 0:1], -2))
                c.mark(dve.memset(pen[:], 0.0))
                c.mark(dve.memset(prow[:], -BIG))
                c.mark(dve.tensor_copy(dst_f[:], dst_i[:]))
                dve.wait_ge(k_l, 32)
                c.mark(dve.tensor_tensor(first[:], dst_i[:], dprev[:], ALU.not_equal))
                c.mark(dve.tensor_tensor(pl[:], lastr[:, 1:NT + 1], lastr[:, 0:NT], ALU.is_equal))
                c.link(dve.tensor_tensor(ql[:], base_i[0:1, :], lastr[:, 0:NT], ALU.is_equal))
                c.mark(dve.tensor_scalar(pl[:], pl[:], -1.0, BIG, ALU.add, ALU.mult))
                c.mark(dve.tensor_scalar(ql[:], ql[:], -1.0, BIG, ALU.add, ALU.mult))

        WD = 4 * 64
        wsd = sb("wsd", [D, 2, 4])
        ww0 = sb("ww0", [D, 4, D])
        wwbd = sb("wwbd", [128, 2, 2, D])
        biasc = sb("biasc", [128, 2])
        biasb = sb("biasb", [128, 2, PN])
        cb = sb("cb", [PN, D])
        bpb = sb("bpb", [PN, D])
        gamma = sb("gamma", [PN, D])
        beta = sb("beta", [PN, D])
        w_att = tmp("w_att", [D, 4, 64])
        att = tmp("att", [D, 2, 4, 64])
        gw = tmp("gw", [D, WD])
        wp = tmp("wp", [128, 2, D])
        wT = tmp("wT", [128, 2, D])
        asd = tmp("asd", [PN, NJ, 8])
        dw = tmp("dw", [PN, NJ, 8])
        T1 = dram("T1", [N, D + 4])
        T1W = dram("T1W", [NW, 8])
        n1_l, n1_dve, n1_var, n1_std, n1_t, n1_tc, n1_pw, n1_aw, n1_m, n1_o, n1_pp = [sem("n1_" + x) for x in
            ("l", "dve", "var", "std", "t", "tc", "pw", "aw", "m", "o", "pp")]
        XC, yn, tab = node_buffers("n1")
        with nc.Block() as block:
            @block.sync
            def _(sp):
                sp.dma_start(gw[:], A["L1_gnn_W"]).then_inc(n1_l, 16)
                sp.dma_start(att[:, 0], A["L1_gnn_att_src"].rearrange("h c -> (h c)").unsqueeze(0).partition_broadcast(D)).then_inc(n1_l, 16)
                sp.dma_start(att[:, 1], A["L1_gnn_att_dst"].rearrange("h c -> (h c)").unsqueeze(0).partition_broadcast(D)).then_inc(n1_l, 16)
                sp.dma_start(wp[:], A["L1_gnn_Wp"].rearrange("(g p) o -> p g o", g=2)).then_inc(n1_l, 16)
                sp.dma_start(bpb[:], A["L1_gnn_bp"].partition_broadcast(PN)).then_inc(n1_l, 16)
                sp.dma_start(gamma[:], A["L1_gnn_gamma"].partition_broadcast(PN)).then_inc(n1_l, 16)
                sp.dma_start(beta[:], A["L1_gnn_beta"].partition_broadcast(PN)).then_inc(n1_l, 16)
                with nc.allow_non_contiguous_dma(reason="256 floats, a column for each pair of heads"):
                    sp.dma_start(biasc[:], A["L1_gnn_bias"].rearrange("a (g p) -> (a p) g", g=2)).then_inc(n1_l, 16)
                sp.dma_start(T1W[N:NW, :], zero[:, 0:8]).then_inc(n1_o, 16)
                sp.wait_ge(n1_dve, 24)
                sp.dma_start(T1.rearrange("(j p) f -> p j f", p=PN)[:, :, 0:D], H[:]).then_inc(n1_o, 16)
                sp.dma_start(T1.rearrange("(j p) f -> p j f", p=PN)[:, :, D:D + 4], asd[:, :, 0:4]).then_inc(n1_o, 16)
                sp.dma_start(T1W[0:N, :].rearrange("(j p) f -> p j f", p=PN), dw[:]).then_inc(n1_o, 16)
                sp.wait_ge(n1_o, 64)

            @block.vector
            def _(dve):
                c = Chain(dve, n1_dve)
                ln_relu_steps(c, n1_var, n1_std, 1, XC=XC)
                c.mark(dve.memset(acc[:], 0.0))
                c.mark(dve.memset(wwbd[:], 0.0))
                dve.wait_ge(n1_l, 8 * 16)
                for a in range(2):
                    c.link(dve.tensor_tensor(w_att[:], gw[:].rearrange("k (h c) -> k h c", h=4), att[:, a], ALU.mult))
                    c.link(dve.tensor_reduce(wsd[:, a, :], w_att[:], AX.X, ALU.add))
                for g in range(2):
                    c.mark(dve.tensor_scalar(biasb[:, g, :], zero[:, 0:PN], biasc[:, g:g + 1], None, ALU.add))
                dve.wait_ge(n1_pw, 1)
                c.mark(dve.tensor_copy(wT[:], bank[4][:, 0:128].rearrange("p (g k) -> p g k", g=2)))
                dve.wait_ge(n1_pw, 2)
                c.mark(dve.tensor_copy(ww0[:], bank[5][0:D, 0:WD].rearrange("p (h o) -> p h o", h=4)))
                for g in range(2):
                    for hh in range(2):
                        P = slice(64 * hh, 64 * hh + 64)
                        dve.tensor_copy(wwbd[P, g, hh, :], bank[6][P, g * D:(g + 1) * D])
                c.link(dve.tensor_tensor(cb[:], bpb[:], bank[7][0:PN, 0:D], ALU.add))
                dve.wait_ge(n1_m, 1)
                c.link(dve.tensor_copy(asd[:], bank[2][0:PN, 0:NJ * 8].rearrange("p (j f) -> p j f", j=NJ)))
                c.link(dve.tensor_scalar(st[:, 6, :], cnt[:], 1.0, None, ALU.max))
                c.link(dve.reciprocal(st[:, 7, :], st[:, 6, :]))
                c.link(dve.tensor_tensor(loop_a[:], loop_a[:], st[:, 7, :].unsqueeze(2).to_broadcast([PN, NJ, 4]), ALU.mult))
                dve.tensor_copy(dw[:, :, 0:4], asd[:, :, 4:8]).then_inc(n1_aw, 1)
                dve.tensor_tensor(loop_a[:], loop_a[:], asd[:, :, 0:4], ALU.add).then_inc(n1_aw, 1)
                dve.wait_ge(n1_aw, 2)
                dve.tensor_tensor(loop_a[:], loop_a[:], asd[:, :, 4:8], ALU.add).then_inc(n1_aw, 1)
                dve.wait_ge(n1_aw, 3)
                c.mark(dve.scalar_tensor_tensor(dw[:, :, 4:8], loop_a[:], SLOPE, loop_a[:], ALU.mult, ALU.max))

            @block.scalar
            def _(act):
                ln_std_step(act, n1_var, n1_std, 1)
                transposed_copy_steps(act, n1_t, n1_tc)

            @block.tensor
            def _(pe):
                pe.wait_ge(n1_l, 8 * 16)
                for g in range(2):
                    last = pe.transpose(bank[4][:, g * D:(g + 1) * D], gw[:, g * 128:(g + 1) * 128], ident[0:D, 0:D])
                last.then_inc(n1_pw, 1)
                pe.wait_ge(n1_dve, 17)
                c = Chain(pe, n1_pp)
                for h in range(4):
                    P = slice(64 * (h % 2), 64 * (h % 2) + 64)
                    c.link(pe.matmul(bank[5][0:D, h * D:(h + 1) * D], wT[P, h // 2, :], wp[P, h // 2, :], start=True, stop=True))
                    c.link(pe.matmul(bank[6][P, (h // 2) * D:(h // 2 + 1) * D], wT[P, h // 2, :], wp[P, h // 2, :],
                                     start=True, stop=True))
                for g in range(2):
                    last = pe.matmul(bank[7][0:PN, 0:D], biasb[:, g, :], wp[:, g, :], start=(g == 0), stop=(g == 1))
                last.then_inc(n1_pw, 1)
                transpose_steps(pe, n1_t, n1_tc)
                pe.wait_ge(n1_tc, len(rounds(NJ, 4)))
                for j in range(NJ):
                    last = pe.matmul(bank[2][0:PN, j * 8:(j + 1) * 8], HT[:, j * PN:(j + 1) * PN],
                                     wsd[:].rearrange("k a h -> k (a h)"), start=True, stop=True)
                last.then_inc(n1_m, 1)

        layer.close()

        e1_g = [sem(f"e1_g{k}") for k in range(UG)]
        e1_w = [sem(f"e1_w{k}") for k in range(UG)]
        e1_dl = [sem(f"e1_dl{k}") for k in range(DR)]
        e1_idx, e1_step, e1_one, e1_oT, e1_P, e1_M, e1_Mx, e1_S, e1_acc, e1_z2, e1_sp = [sem("e1_" + x) for x in
            ("idx", "step", "one", "oT", "P", "M", "Mx", "S", "acc", "z2", "sp")]
        S1 = softmax_sems("b1")
        ga = tmp("ga1", [128, UT, D + 4])
        win = tmp("win1", [128, UT, 8])
        one = tmp("one1", [128, UT, 128])
        oneT = tmp("oneT1", [128, 2, GT * W])
        dl = tmp("dl1", [128, DR, GT * W], BF16)
        M1 = tmp("M1", [128, 2, GT, 3, 128])
        with nc.Block() as block:
            @block.gpsimd
            def _(pool):
                gather_program(ga, pool, T1, D + 4, e1_g, e1_M, e1_idx, e1_step, per=2)

            @block.sync
            def _(sp):
                def body(i, k):
                    place_load(dl, sp, i, k, e1_dl, e1_oT, e1_sp)
                    window_loads(win, sp, i, k, T1W, 8, e1_w, e1_P, e1_sp)
                each_group(sp, body)

            @block.scalar
            def _(act):
                def weights(i, k):
                    g = i * UG + k
                    s, kk = k // KG, k % KG
                    wait(act, e1_S, (g - 1) * GT)
                    act.wait_ge(S1["ex"], (i * 2 + s) * 2 + 1)
                    act.activation(M1[:, k % 2, :, 2, 0:4],
                                   ex[:, s, 0, 0:64].rearrange("p (h t) -> p t h", h=4)[:, kk * GT:(kk + 1) * GT, :],
                                   ACT.Copy).then_inc(e1_Mx, 1)

                def softmax(i, s):
                    q = i * 2 + s
                    softmax_act_1(act, S1, q, 4)
                    softmax_act_3(act, S1, q, 4)
                    softmax_act_4(act, S1, q, s, 4, 2)
                    softmax_act_5(act, S1, q, s, bank[1 + s][:, 128:176], 3)

                def body(i, k):
                    if pending(i, k):
                        softmax(*pending(i, k))
                    if back(i, k, KG):
                        weights(*back(i, k, KG))
                each_group(act, body)
                softmax(NI - 1, 1)
                for k in range(KG, UG):
                    weights(NI - 1, k)

            @block.tensor
            def _(pe):
                def sums(i, k, t):
                    g = i * UG + k
                    if t == 0:
                        pe.wait_ge(e1_M, g * 2 + 2)
                        pe.wait_ge(e1_Mx, g + 1)
                    wait(pe, e1_acc, (g - 1) * 2 * GT + 2 * t + 2)
                    for r in range(3):
                        last = pe.matmul(bank[4 + t][:, r * 128:(r + 1) * 128], M1[:, k % 2, t, r, :], one[:, k * GT + t, :],
                                         start=True, stop=True)
                    last.then_inc(e1_S, 1)

                def softmax_and_sums(i, s, old):
                    q = i * 2 + s
                    softmax_pe_0(pe, S1, q, 4)
                    for t in range(GT):
                        if old:
                            sums(*old, t)
                        if t == 0:
                            softmax_pe_1(pe, S1, q, 4)
                        if t == 1:
                            softmax_pe_2(pe, S1, q, 4)
                        if t == 2:
                            softmax_pe_3(pe, S1, q, 4)
                    softmax_pe_4(pe, S1, q, bank[1 + s][:, 128:176], 4, sel, 3)

                def body(i, k):
                    g = i * UG + k
                    s, kk = k // KG, k % KG
                    pe.wait_ge(e1_oT, g + 1)
                    pe.wait_ge(e1_w[k], i * 64 + 64)
                    if kk == 0:
                        wait(pe, S1["ex"], i * 4 + (s * 2 - 2))
                    for t in range(GT):
                        o = (kk * GT + t) * 8
                        last = pe.matmul(bank[1 + s][:, o:o + 8], oneT[:, k % 2, t * W:(t + 1) * W], win[:, k * GT + t, 0:8],
                                         start=True, stop=True)
                    last.then_inc(e1_P, 1)
                    old = back(i, k, LATE)
                    if pending(i, k):
                        softmax_and_sums(*pending(i, k), old)
                    elif old:
                        for t in range(GT):
                            sums(*old, t)
                each_group(pe, body)
                softmax_and_sums(NI - 1, 1, (NI - 1, UG - LATE))
                for k in range(KG, UG):
                    for t in range(GT):
                        sums(NI - 1, k, t)

            @block.vector
            def _(dve):
                c = Chain(dve, e1_z2)
                c.mark(dve.memset(M1[:], 0.0))
                c.link(dve.memset(crow[:], -BIG))

                def weighted(i, k):
                    g = i * UG + k
                    s, kk = k // KG, k % KG
                    wait(dve, e1_S, (g - 1) * GT)
                    dve.wait_ge(S1["ex"], (i * 2 + s) * 2 + 2)
                    w = lambda x: ex[:, s, x, 0:64].rearrange("p (h t) -> p t h", h=4)[:, kk * GT:(kk + 1) * GT, :]
                    tiles = bass.ds(i * UT + k * GT, GT)
                    dve.tensor_tensor(M1[:, k % 2, :, 2, 4:8], w(1), first[:, tiles].unsqueeze(2).to_broadcast([128, GT, 4]),
                                      ALU.mult).then_inc(e1_M, 1)
                    dve.tensor_tensor(M1[:, k % 2, :, 0:2, :].rearrange("p t r (b c) -> p t (r b) c", b=2),
                                      ga[:, k * GT:(k + 1) * GT, 0:D].unsqueeze(2).to_broadcast([128, GT, 4, D]),
                                      w(0).unsqueeze(3).to_broadcast([128, GT, 4, D]), ALU.mult).then_inc(e1_M, 1)

                def add_sums(i, k, t, b):
                    g = i * UG + k
                    s, kk = k // KG, k % KG
                    wait(dve, e1_acc, g * 2 * GT + 2 * t)
                    a = acc[:, :, bass.ds(b, 1)]
                    dve.tensor_tensor(a, a, fac[:, s, :, kk * GT + t:kk * GT + t + 1], ALU.mult).then_inc(e1_acc, 1)
                    dve.wait_ge(e1_acc, g * 2 * GT + (2 * t + 1))
                    dve.wait_ge(e1_S, g * GT + (t + 1))
                    a = acc[:, :, bass.ds(b, W)]
                    dve.tensor_tensor(a, a, bank[4 + t][:, 0:384].rearrange("p (r n) -> p r n", r=3), ALU.add).then_inc(e1_acc, 1)

                def scores(c, i, s):
                    q = i * 2 + s
                    for kk in range(KG):
                        dve.wait_ge(e1_g[s * KG + kk], i * 64 + 64)
                    dve.wait_ge(e1_P, i * UG + (s + 1) * KG)
                    P = bank[1 + s][:, 0:128].rearrange("p (t f) -> p f t", f=8)
                    v = lambda x: x.rearrange("p (h t) -> p h t", h=4)
                    c.mark(dve.tensor_copy(v(lp[:]), P[:, 4:8, :]))
                    c.link(dve.tensor_tensor(v(al[:, 0, 0:64]), ga[:, s * SG:(s + 1) * SG, D:D + 4].rearrange("p t f -> p f t"),
                                             P[:, 0:4, :], ALU.add))
                    c.link(dve.tensor_tensor(v(al[:, 0, 0:64]), v(al[:, 0, 0:64]),
                                             edge_a[:, bass.ds(i * UT + s * SG, SG), :].rearrange("p t f -> p f t"), ALU.add))
                    c.link(dve.scalar_tensor_tensor(al[:, 0, 0:64], al[:, 0, 0:64], SLOPE, al[:, 0, 0:64], ALU.mult, ALU.max))
                    c.mark(dve.tensor_tensor(am[:, 0:64], al[:, 0, 0:64], lp[:], ALU.max))
                    softmax_dve_0(dve, S1, c, i * UT + s * SG, 4)

                def softmax_and_sums(i, s, old):
                    q = i * 2 + s
                    c = LoopChain(dve, S1["bd"], q, 5 + SOFT)
                    if old:
                        starts = bases_of(dve, *old)
                    scores(c, i, s)
                    softmax_dve_1(dve, S1, c, q, 4)
                    if old:
                        add_sums(*old, 0, starts[0])
                    softmax_dve_2(dve, S1, c, q, i * UT + s * SG, 4)
                    if old:
                        add_sums(*old, 1, starts[1])
                    softmax_dve_3(dve, S1, c, q, 4)
                    if old:
                        add_sums(*old, 2, starts[2])
                    m = softmax_dve_4(dve, S1, c, q, 4)
                    dve.tensor_tensor(ex[:, s, 0, 0:64], al[:, 0, 0:64], m, ALU.subtract).then_inc(S1["pen2"], 1)
                    dve.tensor_tensor(ex[:, s, 1, 0:64], lp[:], m, ALU.subtract).then_inc(S1["pen2"], 1)
                    dve.wait_ge(S1["pen2"], q * 2 + 2)
                    dve.sem_inc(S1["sub"], 1)
                    if old:
                        add_sums(*old, 3, starts[3])

                def body(i, k):
                    g = i * UG + k
                    wait(dve, e1_P, g - 1)
                    transposed_one_hot_step(oneT[:, k % 2, :], dl, dve, i, k, e1_dl, e1_oT)
                    wait(dve, e1_S, (g - 7) * GT)
                    one_hot_ring_step(one, dve, i, k, e1_one)
                    old = back(i, k, LATE)
                    if pending(i, k):
                        softmax_and_sums(*pending(i, k), old)
                    elif old:
                        starts = bases_of(dve, *old)
                        for t in range(GT):
                            add_sums(*old, t, starts[t])
                    if back(i, k, KG):
                        weighted(*back(i, k, KG))
                each_group(dve, body)
                softmax_and_sums(NI - 1, 1, (NI - 1, UG - LATE))
                weighted(NI - 1, KG)
                for k in range(KG, UG):
                    starts = bases_of(dve, NI - 1, k)
                    if k + 1 < UG:
                        weighted(NI - 1, k + 1)
                    for t in range(GT):
                        add_sums(NI - 1, k, t, starts[t])

        layer.close()
        den = tmp("den", [PN, NJ, 8])
        yl = tmp("yl", [PN, 2, 4, D])
        m1_d, m1_dve, m1_m, m1_act = [sem("m1_" + x) for x in ("d", "dve", "m", "act")]
        m1_var, m1_std = sem("m1_var"), sem("m1_std")
        XC, yn, tab = node_buffers("m1")
        with nc.Block() as block:
            @block.tensor
            def _(pe):
                for j in range(NJ):
                    last = pe.transpose(bank[0][0:PN, j * 8:(j + 1) * 8], acc[0:8, 2, j * PN:(j + 1) * PN], ident[0:8, 0:8])
                last.then_inc(m1_d, 1)
                for j in range(NJ):
                    if j >= 2:
                        pe.wait_ge(m1_dve, 5 + 4 * (j - 1))
                    b = bank[1 + j % 2]
                    for g in range(2):
                        pe.matmul(b[0:PN, g * 128:(g + 1) * 128], acc[:, g, j * PN:(j + 1) * PN],
                                  wwbd[:, g].rearrange("p a o -> p (a o)"), start=True, stop=True)
                    pe.matmul(b[0:PN, 256:512], HT[:, j * PN:(j + 1) * PN], ww0[:].rearrange("p h o -> p (h o)"),
                              start=True, stop=True).then_inc(m1_m, 1)

            @block.vector
            def _(dve):
                c = Chain(dve, m1_dve)
                dve.wait_ge(m1_d, 1)
                c.link(dve.tensor_copy(den[:], bank[0][0:PN, 0:NJ * 8].rearrange("p (j f) -> p j f", j=NJ)))
                c.link(dve.tensor_scalar(st[:, 6, :], cnt[:], 0.0, None, ALU.is_equal))
                c.link(dve.tensor_tensor(den[:, :, 4:8], den[:, :, 4:8], st[:, 6, :].unsqueeze(2).to_broadcast([PN, NJ, 4]), ALU.add))
                c.link(dve.tensor_tensor(den[:, :, 0:4], den[:, :, 0:4], den[:, :, 4:8], ALU.add))
                c.link(dve.reciprocal(den[:, :, 0:4], den[:, :, 0:4]))
                for j in range(NJ):
                    dve.wait_ge(m1_m, j + 1)
                    b = bank[1 + j % 2]
                    y = yl[:, j % 2]
                    wl = den[:, j, 4:8].unsqueeze(2).to_broadcast([PN, 4, D])
                    rd = den[:, j, 0:4].unsqueeze(2).to_broadcast([PN, 4, D])
                    c.link(dve.tensor_tensor(y, b[0:PN, 256:512].rearrange("p (h o) -> p h o", h=4), wl, ALU.mult))
                    c.link(dve.tensor_tensor(y, b[0:PN, 0:256].rearrange("p (h o) -> p h o", h=4), y, ALU.add))
                    c.link(dve.tensor_tensor(y, y, rd, ALU.mult))
                    c.mark(dve.tensor_reduce(XC[:, j, :], y.rearrange("p h o -> p o h"), AX.X, ALU.add))
                dve.wait_ge(m1_dve, c.n)
                bc = lambda v: v[:].unsqueeze(1).to_broadcast([PN, NJ, D])
                c.link(dve.tensor_tensor(XC[:], XC[:], bc(cb), ALU.add))
                c.link(dve.tensor_scalar(tab[:, :, 0:D], XC[:], 0.0, None, ALU.min))
                m1_min = c.n
                c.link(dve.tensor_scalar(XC[:], XC[:], 0.0, -1.0, ALU.max, ALU.add))
                s_done["m1_min"] = m1_min
                c.link(dve.tensor_tensor(H[:], H[:], XC[:], ALU.add))
                dve.wait_ge(m1_act, 1)
                c.link(dve.tensor_tensor(H[:], H[:], tab[:, :, D:2 * D], ALU.add))
                ln_relu_steps(c, m1_var, m1_std, 1, dst=yn, src=H, relu=False, XC=XC)
                c.link(dve.tensor_tensor(yn[:], yn[:], bc(gamma), ALU.mult))
                c.link(dve.tensor_tensor(yn[:], yn[:], bc(beta), ALU.add))
                c.link(dve.tensor_tensor(X[:], X[:], yn[:], ALU.add))

            @block.scalar
            def _(act):
                act.wait_ge(m1_dve, 5 + 4 * NJ + 2)
                act.activation(tab[:, :, D:2 * D], tab[:, :, 0:D], ACT.Exp).then_inc(m1_act, 1)
                ln_std_step(act, m1_var, m1_std, 1)
        end_of_layer()
        if finish("L1"):
            return

        w2t = sb("w2t", [D, D])
        b2b = sb("b2b", [PN, D])
        dis = sb("dis", [PN, NJ])
        T2 = dram("T2", [N, D])
        n2_l, n2_dve, n2_var, n2_std, n2_deg, n2_t, n2_tc, n2_o = [sem("n2_" + x) for x in ("l", "dve", "var", "std", "deg", "t", "tc", "o")]
        XC, yn, tab = node_buffers("n2")
        with nc.Block() as block:
            @block.vector
            def _(dve):
                c = Chain(dve, n2_dve)
                c.link(dve.tensor_scalar(st[:, 6, :], cnt[:], 1.0, None, ALU.add))
                dve.wait_ge(n2_deg, 1)
                c.link(dve.reciprocal(dis[:], st[:, 7, :]))
                c.mark(dve.memset(acc[:], 0.0))
                ln_relu_steps(c, n2_var, n2_std, 1, XC=XC)
                c.mark(dve.tensor_tensor(yn[:], H[:], dis[:].unsqueeze(2).to_broadcast([PN, NJ, D]), ALU.mult))

            @block.scalar
            def _(act):
                act.wait_ge(n2_dve, 1)
                act.activation(st[:, 7, :], st[:, 6, :], ACT.Sqrt).then_inc(n2_deg, 1)
                ln_std_step(act, n2_var, n2_std, 1)
                transposed_copy_steps(act, n2_t, n2_tc)

            @block.tensor
            def _(pe):
                pe.wait_ge(n2_dve, 12)
                transpose_steps(pe, n2_t, n2_tc, src=yn)

            @block.sync
            def _(sp):
                sp.dma_start(w2t[:], A["L2_gnn_WT"]).then_inc(n2_l, 16)
                sp.dma_start(b2b[:], A["L2_gnn_b"].partition_broadcast(PN)).then_inc(n2_l, 16)
                sp.wait_ge(n2_dve, 12)
                sp.dma_start(T2.rearrange("(j p) f -> p j f", p=PN), yn[:]).then_inc(n2_o, 16)
                sp.wait_ge(n2_o, 16)
                sp.wait_ge(n2_l, 32)
        layer.close()

        e2_g = [sem(f"e2_g{k}") for k in range(UG)]
        e2_idx, e2_step, e2_one, e2_S, e2_acc = [sem("e2_" + x) for x in ("idx", "step", "one", "S", "acc")]
        ga = tmp("ga2", [128, UT, D])
        one = tmp("one2", [128, UT, 128])
        with nc.Block() as block:
            @block.gpsimd
            def _(pool):
                gather_program(ga, pool, T2, D, e2_g, e2_S, e2_idx, e2_step)

            @block.tensor
            def _(pe):
                def body(i, k):
                    g = i * UG + k
                    pe.wait_ge(e2_one, g + 1)
                    pe.wait_ge(e2_g[k], i * 64 + 64)
                    wait(pe, e2_acc, (g - 1) * GT)
                    for t in range(GT):
                        last = pe.matmul(bank[k % 2][0:D, t * 128:(t + 1) * 128], ga[:, k * GT + t, :], one[:, k * GT + t, :],
                                         start=True, stop=True)
                    last.then_inc(e2_S, 1)
                each_group(pe, body)

            @block.vector
            def _(dve):
                def add_sums(i, k):
                    g = i * UG + k
                    starts = bases_of(dve, i, k)
                    dve.wait_ge(e2_S, g + 1)
                    for t, b in enumerate(starts):
                        wait(dve, e2_acc, g * GT + t)
                        a = acc[0:D, 0, bass.ds(b, W)]
                        dve.tensor_tensor(a, a, bank[k % 2][0:D, t * 128:(t + 1) * 128], ALU.add).then_inc(e2_acc, 1)

                def body(i, k):
                    g = i * UG + k
                    wait(dve, e2_S, g - 7)
                    one_hot_ring_step(one, dve, i, k, e2_one)
                    if before(i, k):
                        add_sums(*before(i, k))
                each_group(dve, body)
                add_sums(NI - 1, UG - 1)
        layer.close()

        m2_m, m2_dve = sem("m2_m"), sem("m2_dve")
        XC, yn, tab = node_buffers("m2")
        with nc.Block() as block:
            @block.tensor
            def _(pe):
                for r, (j0, n) in enumerate(rounds(NJ, 4)):
                    if r >= 2:
                        pe.wait_ge(m2_dve, r - 1)
                    for j in range(n):
                        cols = slice((j0 + j) * PN, (j0 + j + 1) * PN)
                        o = bank[r % 2][0:PN, j * D:(j + 1) * D]
                        pe.matmul(o, acc[0:D, 0, cols], w2t[:], start=True, stop=False)
                        last = pe.matmul(o, HT[:, cols], w2t[:], start=False, stop=True)
                    last.then_inc(m2_m, 1)

            @block.vector
            def _(dve):
                c = Chain(dve, m2_dve)
                for r, (j0, n) in enumerate(rounds(NJ, 4)):
                    dve.wait_ge(m2_m, r + 1)
                    c.mark(dve.tensor_tensor(yn[:, j0:j0 + n, :], bank[r % 2][0:PN, 0:n * D].rearrange("p (j f) -> p j f", j=n),
                                             dis[:, j0:j0 + n].unsqueeze(2).to_broadcast([PN, n, D]), ALU.mult))
                dve.wait_ge(m2_dve, c.n)
                c.link(dve.tensor_tensor(yn[:], yn[:], b2b[:].unsqueeze(1).to_broadcast([PN, NJ, D]), ALU.add))
                c.link(dve.scalar_tensor_tensor(X[:], yn[:], 0.0, X[:], ALU.max, ALU.add))
        end_of_layer()
        if finish("L2"):
            return

        F = 128
        NS = 9
        NZ = 5
        wq = sb("wq", [D, F])
        w1kv = sb("w1kv", [D, F])
        b1kv = sb("b1kv", [F, 1])
        w2v = sb("w2v", [D + 1, F])
        w2k = sb("w2k", [128, F])
        b2k = sb("b2k", [F, 1])
        ck = sb("ck", [128, NZ, F])
        cv = sb("cv", [128, NZ, F])
        w_out = sb("w_out", [F, D])
        w_self = sb("w_self", [D, D])
        gcol = sb("gcol", [D, 1])
        bcol = sb("bcol", [D, 1])
        shsel = sb("shsel", [3 * NS, NZ, 128], BF16)
        sel_b = sb("sel_b", [8, 128])
        XX = dram("XX", [N, 2 * D])
        QW = dram("QW", [NW, F])
        SH = dram("SH", [3, NS * EP], BF16)
        n3_l, n3_s, n3_sd, n3_p, n3_dve, n3_var, n3_std, n3_t, n3_tc, n3_q, n3_qc, n3_o, n3_c = [sem("n3_" + x) for x in
            ("l", "s", "sd", "p", "dve", "var", "std", "t", "tc", "q", "qc", "o", "c")]
        NL3 = 17
        SF = NS * EP // 128
        XC, yn, tab = node_buffers("n3")
        shf = tmp("shf", [128, SF])
        shp = tmp("shp", [128, 3, SF], BF16)
        shsel_f = tmp("shsel_f", [3 * NS, NZ, 128])
        with nc.Block() as block:
            @block.sync
            def _(sp):
                sp.dma_start(shf[:], A["ea9"].rearrange("s (a f) -> (s a) f", a=1).rearrange("s f -> (s f)")
                             .rearrange("(p f) -> p f", p=128)).then_inc(n3_s, 16)
                L = lambda o, i: sp.dma_start(o, i).then_inc(n3_l, 16)
                L(wq[:], A["L3_gnn_Wq"])
                L(w1kv[:, 0:D], A["L3_gnn_v_w1"])
                L(w1kv[:, D:F], A["L3_gnn_k_w1"])
                L(w2v[0:D, :], A["L3_gnn_v_w2"])
                L(w2v[D:D + 1, :], A["L3_gnn_v_b2"])
                L(w2k[D:128, :], A["L3_gnn_k_w2"])
                L(w_out[:], A["L3_gnn_W_out"])
                L(w_self[:], A["L3_gnn_W_self"])
                with nc.allow_non_contiguous_dma(reason="biases as columns"):
                    L(b1kv[0:D, :], A["L3_gnn_v_b1"].rearrange("a f -> f a"))
                    L(b1kv[D:F, :], A["L3_gnn_k_b1"].rearrange("a f -> f a"))
                    L(b2k[:], A["L3_gnn_k_b2"].rearrange("a f -> f a"))
                    L(gcol[:], A["L3_gnn_gamma"].rearrange("a f -> f a"))
                    L(bcol[:], A["L3_gnn_beta"].rearrange("a f -> f a"))
                for m, w in ((ck, "Cqk"), (cv, "Cv")):
                    L(m[0:D, :, :], A["L3_gnn_" + w][:, 0:NS:2, :])
                    L(m[D:128, 0:NZ - 1, :], A["L3_gnn_" + w][:, 1:NS:2, :])
                for part in range(3):
                    sp.wait_ge(n3_sd, 2 * part + 1)
                    sp.dma_start(SH[part].rearrange("(p f) -> p f", p=128), shp[:, part, :]).then_inc(n3_o, 16)
                sp.dma_start(QW[N:NW, :], zero[:, 0:F]).then_inc(n3_o, 16)
                sp.wait_ge(n3_dve, 9)
                for a in range(2):
                    sp.dma_start(XX.rearrange("(j p) f -> p j f", p=PN)[:, :, a * D:(a + 1) * D], H[:]).then_inc(n3_o, 16)
                sp.wait_ge(n3_qc, len(rounds(NJ, 4)))
                sp.dma_start(QW[0:N, :].rearrange("(j p) f -> p j f", p=PN), tab[:]).then_inc(n3_o, 16)
                sp.wait_ge(n3_o, 7 * 16)
                sp.wait_ge(n3_l, NL3 * 16)

            @block.gpsimd
            def _(pool):
                pool.memset(shsel_f[:], 0.0).then_inc(n3_p, 1)
                n = 1
                for part in range(3):
                    pool.wait_ge(n3_p, n)
                    pool.affine_select(out=shsel_f[:].rearrange("p j (a c) -> p j a c", a=2),
                                       in_=shsel_f[:].rearrange("p j (a c) -> p j a c", a=2),
                                       compare_op=ALU.not_equal, fill=1.0, base=-NS * part,
                                       pattern=[[-2, NZ], [-1, 2], [0, D]], channel_multiplier=1).then_inc(n3_p, 1)
                    n += 1
                pool.memset(sel_b[:], 1.0).then_inc(n3_p, 1)
                n += 1
                pool.wait_ge(n3_p, n)
                pool.affine_select(out=sel_b[:], in_=sel_b[:], compare_op=ALU.is_ge, fill=0.0, base=0,
                                   pattern=[[1, 128]], channel_multiplier=-16).then_inc(n3_p, 1)
                n += 1
                pool.wait_ge(n3_p, n)
                pool.affine_select(out=sel_b[:], in_=sel_b[:], compare_op=ALU.is_ge, fill=0.0, base=15,
                                   pattern=[[-1, 128]], channel_multiplier=16).then_inc(n3_p, 1)

            @block.vector
            def _(dve):
                c = Chain(dve, n3_dve)
                ln_relu_steps(c, n3_var, n3_std, 1, XC=XC)
                c.mark(dve.memset(acc[:, 0:2, :], 0.0))
                s = Chain(dve, n3_sd)
                dve.wait_ge(n3_s, 16)
                s.link(dve.tensor_copy(shp[:, 0, :], shf[:]))
                for part in range(1, 3):
                    s.link(dve.tensor_tensor(shf[:], shf[:], shp[:, part - 1, :], ALU.subtract))
                    s.link(dve.tensor_copy(shp[:, part, :], shf[:]))
                dve.wait_ge(n3_p, 4)
                dve.tensor_copy(shsel[:], shsel_f[:]).then_inc(n3_c, 1)

            @block.scalar
            def _(act):
                ln_std_step(act, n3_var, n3_std, 1)
                transposed_copy_steps(act, n3_t, n3_tc)
                for r, (j0, n) in enumerate(rounds(NJ, 4)):
                    act.wait_ge(n3_q, r + 1)
                    act.activation(tab[:, j0:j0 + n, :], bank[2 + r % 2][0:PN, 0:n * 128].rearrange("p (j f) -> p j f", j=n),
                                   ACT.Copy).then_inc(n3_qc, 1)

            @block.tensor
            def _(pe):
                pe.wait_ge(n3_dve, 8)
                transpose_steps(pe, n3_t, n3_tc)
                pe.wait_ge(n3_l, NL3 * 16)
                for r, (j0, n) in enumerate(rounds(NJ, 4)):
                    pe.wait_ge(n3_tc, r + 1)
                    if r >= 2:
                        pe.wait_ge(n3_qc, r - 1)
                    for j in range(n):
                        last = pe.matmul(bank[2 + r % 2][0:PN, j * 128:(j + 1) * 128], HT[:, (j0 + j) * PN:(j0 + j + 1) * PN],
                                         wq[:], start=True, stop=True)
                    last.then_inc(n3_q, 1)
        layer.close()

        e3_g = [sem(f"e3_g{k}") for k in range(UG)]
        WR = 2
        e3_w = [sem(f"e3_w{k}") for k in range(WR)]
        e3_e = [sem(f"e3_e{k}") for k in range(2)]
        e3_dl = [sem(f"e3_dl{k}") for k in range(2)]
        (e3_idx, e3_step, e3_one, e3_oT, e3_X, e3_xT, e3_H, e3_h, e3_sh, e3_z, e3_Q, e3_q, e3_K, e3_Wk, e3_wk, e3_kt, e3_pr,
         e3_V, e3_Wv, e3_wv, e3_vw, e3_P, e3_S, e3_acc, e3_M, e3_Mx, e3_i, e3_sp) = [sem("e3_" + x) for x in
            ("idx", "step", "one", "oT", "X", "xT", "H", "h", "sh", "z", "Q", "q", "K", "Wk", "wk", "kt", "pr",
             "V", "Wv", "wv", "vw", "P", "S", "acc", "M", "Mx", "i", "sp")]
        S3 = softmax_sems("b3")
        GR = 4
        ga = tmp("ga3", [128, GR * GT, F])
        win = tmp("win3", [128, WR * GT, F])
        one = tmp("one3", [128, UT, 128])
        oneT = acc[:, 2, 0 * 512:1 * 512]
        xT = acc[:, 2, 1 * 512:2 * 512]
        dl = tmp("dl3", [128, 2, GT * W], BF16)
        ef = tmp("ef", [D, 2, GT * W])
        shl = tmp("shl", [3 * NS, 2, GT * W], BF16)
        spare = edge_a[:].rearrange("p t h -> p (t h)")
        hv = spare[0:D + 1, 0:GT * W]
        hk = spare[:, GT * W:2 * GT * W]
        z = tmp("z", [128, 2, NZ, GT * W])
        qs = acc[:, 2, 2 * 512:3 * 512]
        wks = acc[:, 2, 3 * 512:4 * 512]
        kt = acc[:, 2, 4 * 512:5 * 512]
        wvs = spare[:, 2 * GT * W:3 * GT * W].rearrange("p (t f) -> p t f", t=GT)
        vw = tmp("vw", [128, UT, F])
        M3 = tmp("M3", [128, 2, GT, 2, F])
        hsel = tmp("hsel", [128, 8])
        with nc.Block() as block:
            @block.gpsimd
            def _(pool):
                gather_program(ga, pool, XX, F, e3_g, e3_X, e3_idx, e3_step, ring=GR)

            @block.sync
            def _(sp):
                def body(i, k):
                    g = i * UG + k
                    cols = bass.ds(g * GT * W, GT * W)
                    wait(sp, e3_oT, g - 1)
                    sp.sem_inc(e3_sp, 1)
                    sp.dma_start(dl[:, k % 2, :], DL[:, cols].partition_broadcast(128)).then_inc(e3_dl[k % 2], 16)
                    wait(sp, e3_H, g - 1)
                    sp.sem_inc(e3_sp, 1)
                    wait(sp, e3_sh, (g - 1) * NZ)
                    sp.sem_inc(e3_sp, 1)
                    sp.dma_start(ef[:, k % 2, :], A["ea64"][:, cols]).then_inc(e3_e[k % 2], 16)
                    for part in range(3):
                        sp.dma_start(shl[part * NS:(part + 1) * NS, k % 2, :],
                                     SH[part].rearrange("(s e) -> s e", s=NS)[:, cols]).then_inc(e3_e[k % 2], 16)
                    window_loads(win, sp, i, k, QW, F, e3_w, e3_Q, e3_sp, ring=WR)
                each_group(sp, body)

            @block.scalar
            def _(act):
                def weights(i, k):
                    g = i * UG + k
                    s, kk = k // KG, k % KG
                    wait(act, e3_S, (g - 1) * 2)
                    act.wait_ge(S3["ex"], (i * 2 + s) * 2 + 1)
                    act.activation(M3[:, k % 2, :, 1, 0:8],
                                   ex[:, s, 0, :].rearrange("p (h t) -> p t h", h=8)[:, kk * GT:(kk + 1) * GT, :],
                                   ACT.Copy).then_inc(e3_Mx, 1)

                def body(i, k):
                    g = i * UG + k
                    p = pending(i, k)
                    if p:
                        q, s = p[0] * 2 + p[1], p[1]
                    if back(i, k, LATE):
                        weights(*back(i, k, LATE))
                    act.wait_ge(e3_X, g + 1)
                    wait(act, e3_z, g * NZ)
                    act.activation(xT[:], bank[0][:], ACT.Copy).then_inc(e3_xT, 1)
                    if p:
                        softmax_act_1(act, S3, q, 8)
                    act.wait_ge(e3_H, g + 1)
                    wait(act, e3_Wk, g)
                    wait(act, e3_Wv, g)
                    act.activation(hv[0:D, :], bank[0][0:D, :], ACT.Relu, bias=b1kv[0:D, 0:1]).then_inc(e3_h, 1)
                    act.activation(hk[D:128, :], bank[0][D:128, :], ACT.Relu, bias=b1kv[D:128, 0:1]).then_inc(e3_h, 1)
                    act.wait_ge(e3_Q, g + 1)
                    wait(act, e3_pr, g)
                    act.activation(qs[:], bank[7][:], ACT.Copy).then_inc(e3_q, 1)
                    if p:
                        softmax_act_3(act, S3, q, 8)
                    act.wait_ge(e3_Wk, g + 1)
                    wait(act, e3_kt, g)
                    act.activation(wks[:], bank[7][:], ACT.Identity, bias=b2k[:, 0:1]).then_inc(e3_wk, 1)
                    if p:
                        softmax_act_4(act, S3, q, s, 8, 1)
                    act.wait_ge(e3_Wv, g + 1)
                    wait(act, e3_vw, g)
                    act.activation(wvs[:], bank[7][:].rearrange("p (t f) -> p t f", t=GT), ACT.Copy).then_inc(e3_wv, 1)
                    if p:
                        softmax_act_5(act, S3, q, s, bank[4][:, 128:160], 2)
                act.wait_ge(e3_i, 4)
                each_group(act, body)
                weights(NI - 1, UG - LATE)
                q = NI * 2 - 1
                softmax_act_1(act, S3, q, 8)
                softmax_act_3(act, S3, q, 8)
                softmax_act_4(act, S3, q, 1, 8, 1)
                softmax_act_5(act, S3, q, 1, bank[4][:, 128:160], 2)
                for k in range(KG, UG):
                    weights(NI - 1, k)

            @block.tensor
            def _(pe):
                def sums(i, k, half):
                    g = i * UG + k
                    if half == 0:
                        pe.wait_ge(e3_M, g + 1)
                        pe.wait_ge(e3_Mx, g + 1)
                    else:
                        pe.wait_ge(e3_acc, g * 8 + 4)
                    for t in range(2 * half, 2 * half + 2):
                        for r in range(2):
                            last = pe.matmul(bank[7][:, (t % 2) * 256 + r * 128:(t % 2) * 256 + (r + 1) * 128], M3[:, k % 2, t, r, :],
                                             one[:, k * GT + t, :], start=True, stop=True)
                    last.then_inc(e3_S, 1)

                def harmonics(i, k, j):
                    u = (i * UG + k) * NZ + j
                    m = 128 if j < NZ - 1 else D
                    wait(pe, e3_z, u - 1)
                    pe.matmul(bank[1 + (k * NZ + j) % 2][0:m, :], shsel[:, j, 0:m], shl[:, k % 2, :], start=True, stop=True)\
                      .then_inc(e3_sh, 1)

                def body(i, k):
                    g = i * UG + k
                    s, kk = k // KG, k % KG
                    old = back(i, k, LATE)
                    p = pending(i, k)
                    if p:
                        q = p[0] * 2 + p[1]
                    pe.wait_ge(e3_g[k], i * 64 + 64)
                    wait(pe, e3_h, g * 2)
                    for t in range(GT):
                        last = pe.transpose(bank[0][:, t * 128:(t + 1) * 128], ga[:, (k % GR) * GT + t, :], ident[:])
                    last.then_inc(e3_X, 1)
                    if p:
                        softmax_pe_0(pe, S3, q, 8)
                    wait(pe, e3_wv, g)
                    if old:
                        sums(*old, 0)
                    pe.wait_ge(e3_e[k % 2], i * (UG // 2 * 64) + (k // 2 + 1) * 64)
                    for j in range(2):
                        harmonics(i, k, j)
                    pe.wait_ge(e3_xT, g + 1)
                    pe.matmul(bank[0][:], w1kv[:], ef[:, k % 2, :], start=True, stop=True).then_inc(e3_H, 1)
                    if p:
                        softmax_pe_1(pe, S3, q, 8)
                    if old:
                        sums(*old, 1)
                    wait(pe, e3_kt, g)
                    for j in range(NZ):
                        if j == 2:
                            if old:
                                pe.wait_ge(e3_acc, (old[0] * UG + old[1]) * 8 + 8)
                            pe.wait_ge(e3_w[k % WR], i * (UG // WR * 64) + (k // WR + 1) * 64)
                            pe.wait_ge(e3_oT, g + 1)
                            for t in range(GT):
                                last = pe.matmul(bank[7][:, t * 128:(t + 1) * 128], win[:, (k % WR) * GT + t, :],
                                                 oneT[:, t * 128:(t + 1) * 128], start=True, stop=True)
                            last.then_inc(e3_Q, 1)
                        m = 128 if j < NZ - 1 else D
                        pe.wait_ge(e3_z, g * NZ + (j + 1))
                        last = pe.matmul(bank[5][:], ck[0:m, j, :], z[0:m, k % 2, j, :], start=(j == 0), stop=(j == NZ - 1))
                        if j + 2 < NZ:
                            harmonics(i, k, j + 2)
                        if p and j == 1:
                            softmax_pe_2(pe, S3, q, 8)
                    last.then_inc(e3_K, 1)
                    if p:
                        softmax_pe_3(pe, S3, q, 8)
                    pe.wait_ge(e3_h, g * 2 + 2)
                    pe.wait_ge(e3_q, g + 1)
                    pe.matmul(bank[7][:], w2k[D:128, :], hk[D:128, :], start=True, stop=True).then_inc(e3_Wk, 1)
                    wait(pe, e3_vw, g)
                    for t in range(GT):
                        if t == 2:
                            pe.wait_ge(e3_wk, g + 1)
                            for u in range(GT):
                                last = pe.matmul(bank[7][:, u * 128:(u + 1) * 128], hv[:, u * 128:(u + 1) * 128], w2v[:],
                                                 start=True, stop=True)
                            last.then_inc(e3_Wv, 1)
                        for j in range(NZ):
                            m = 128 if j < NZ - 1 else D
                            last = pe.matmul(bank[6][:, t * 128:(t + 1) * 128], z[0:m, k % 2, j, t * 128:(t + 1) * 128], cv[0:m, j, :],
                                             start=(j == 0), stop=(j == NZ - 1))
                    last.then_inc(e3_V, 1)
                    if p:
                        softmax_pe_4(pe, S3, q, bank[4][:, 128:160], 8, sel8, 2)
                    pe.wait_ge(e3_pr, g + 1)
                    if kk == 0:
                        wait(pe, S3["ex"], i * 4 + s * 2)
                    for t in range(GT):
                        o = (kk * GT + t) * 8
                        last = pe.matmul(bank[4][:, o:o + 8], kt[:, t * 128:(t + 1) * 128], hsel[:], start=True, stop=True)
                    last.then_inc(e3_P, 1)
                each_group(pe, body)
                sums(NI - 1, UG - LATE, 0)
                sums(NI - 1, UG - LATE, 1)
                q = NI * 2 - 1
                softmax_pe_0(pe, S3, q, 8)
                softmax_pe_1(pe, S3, q, 8)
                softmax_pe_2(pe, S3, q, 8)
                softmax_pe_3(pe, S3, q, 8)
                softmax_pe_4(pe, S3, q, bank[4][:, 128:160], 8, sel8, 2)
                for k in range(KG, UG):
                    if k == KG:
                        pe.wait_ge(e3_acc, (NI * UG - LATE) * 8 + 8)
                    else:
                        pe.wait_ge(e3_acc, ((NI - 1) * UG + k) * 8)
                    sums(NI - 1, k, 0)
                    sums(NI - 1, k, 1)

            @block.vector
            def _(dve):
                dve.memset(M3[:], 0.0).then_inc(e3_i, 1)
                dve.memset(crow[:], -BIG).then_inc(e3_i, 1)
                dve.memset(hv[D:D + 1, :], 1.0).then_inc(e3_i, 1)
                dve.tensor_reduce(hsel[:], ident[:].rearrange("p (h c) -> p h c", h=8), AX.X, ALU.add).then_inc(e3_i, 1)
                dve.wait_ge(e3_i, 4)

                def values(i, k):
                    g = i * UG + k
                    s, kk = k // KG, k % KG
                    wait(dve, e3_S, (g - 1) * 2)
                    dve.wait_ge(S3["ex"], (i * 2 + s) * 2 + 2)
                    w = ex[:, s, 0, :].rearrange("p (h t) -> p t h", h=8)[:, kk * GT:(kk + 1) * GT, :]
                    dve.tensor_tensor(M3[:, k % 2, :, 0, :].rearrange("p t (h c) -> p t h c", h=8),
                                      vw[:, k * GT:(k + 1) * GT, :].rearrange("p t (h c) -> p t h c", h=8),
                                      w.unsqueeze(3).to_broadcast([128, GT, 8, 16]), ALU.mult).then_inc(e3_M, 1)

                def add_sums(i, k, half, starts):
                    g = i * UG + k
                    s, kk = k // KG, k % KG
                    for t in range(2 * half, 2 * half + 2):
                        b = starts[t]
                        wait(dve, e3_acc, g * 8 + 2 * t)
                        a = acc[:, 0:2, bass.ds(b, 1)]
                        dve.tensor_tensor(a, a, fac[:, s, 0:2, kk * GT + t:kk * GT + t + 1], ALU.mult).then_inc(e3_acc, 1)
                        dve.wait_ge(e3_acc, g * 8 + (2 * t + 1))
                        if t == 2 * half:
                            dve.wait_ge(e3_S, g * 2 + (half + 1))
                        a = acc[:, 0:2, bass.ds(b, W)]
                        dve.tensor_tensor(a, a, bank[7][:, (t % 2) * 256:(t % 2 + 1) * 256].rearrange("p (r n) -> p r n", r=2),
                                          ALU.add).then_inc(e3_acc, 1)

                def scores(c, q, s):
                    dve.wait_ge(e3_P, (q + 1) * KG)
                    c.link(dve.tensor_copy(am[:].rearrange("p (h t) -> p h t", h=8),
                                           bank[4][:, 0:128].rearrange("p (t h) -> p h t", h=8)))

                def exponents(c, q, s):
                    m = softmax_dve_4(dve, S3, c, q, 8)
                    dve.tensor_tensor(ex[:, s, 0, :], am[:], m, ALU.subtract).then_inc(S3["pen"], 1)
                    dve.wait_ge(S3["pen"], q + 1)
                    dve.sem_inc(S3["sub"], 1)

                def body(i, k):
                    g = i * UG + k
                    old = back(i, k, LATE)
                    p = pending(i, k)
                    if p:
                        q, s = p[0] * 2 + p[1], p[1]
                        c0 = p[0] * UT + s * SG
                        c = LoopChain(dve, S3["bd"], q, 1 + SOFT)
                        scores(c, q, s)
                        softmax_dve_0(dve, S3, c, c0, 8)
                    if old:
                        starts = bases_of(dve, *old)
                        values(*old)
                    wait(dve, e3_S, g * 2 - 14)
                    one_hot_ring_step(one, dve, i, k, e3_one)
                    if p:
                        softmax_dve_1(dve, S3, c, q, 8)
                    if old:
                        add_sums(*old, 0, starts)
                    wait(dve, e3_V, g - 1)
                    dve.wait_ge(e3_xT, g + 1)
                    for j in range(NZ):
                        if j == 1:
                            wait(dve, e3_Q, g)
                            dve.wait_ge(e3_dl[k % 2], i * (UG // 2 * 16) + (k // 2 + 1) * 16)
                            dve.tensor_scalar(oneT[:], dl[:, k % 2, :], iota_p[:, 0:1], None, ALU.is_equal).then_inc(e3_oT, 1)
                        if old and j == 2:
                            add_sums(*old, 1, starts)
                        if p and j == 2:
                            softmax_dve_2(dve, S3, c, q, c0, 8)
                        if p and j == NZ - 1:
                            softmax_dve_3(dve, S3, c, q, 8)
                        m = 128 if j < NZ - 1 else D
                        dve.wait_ge(e3_sh, g * NZ + (j + 1))
                        dve.tensor_tensor(z[0:m, k % 2, j, :], bank[1 + (k * NZ + j) % 2][0:m, :], xT[0:m, :], ALU.mult).then_inc(e3_z, 1)
                    if p:
                        exponents(c, q, s)
                    dve.wait_ge(e3_K, g + 1)
                    dve.wait_ge(e3_wk, g + 1)
                    wait(dve, e3_P, g)
                    dve.tensor_tensor(kt[:], bank[5][:], wks[:], ALU.mult).then_inc(e3_kt, 1)
                    dve.wait_ge(e3_kt, g + 1)
                    dve.wait_ge(e3_q, g + 1)
                    dve.tensor_tensor(kt[:], kt[:], qs[:], ALU.mult).then_inc(e3_pr, 1)
                    dve.wait_ge(e3_V, g + 1)
                    dve.wait_ge(e3_wv, g + 1)
                    dve.tensor_tensor(vw[:, k * GT:(k + 1) * GT, :], bank[6][:].rearrange("p (t f) -> p t f", t=GT), wvs[:],
                                      ALU.mult).then_inc(e3_vw, 1)
                each_group(dve, body)
                starts = bases_of(dve, NI - 1, UG - LATE)
                values(NI - 1, UG - LATE)
                for half in range(2):
                    add_sums(NI - 1, UG - LATE, half, starts)
                q, c0 = NI * 2 - 1, NT - SG
                c = LoopChain(dve, S3["bd"], q, 1 + SOFT)
                scores(c, q, 1)
                softmax_dve_0(dve, S3, c, c0, 8)
                softmax_dve_1(dve, S3, c, q, 8)
                softmax_dve_2(dve, S3, c, q, c0, 8)
                softmax_dve_3(dve, S3, c, q, 8)
                exponents(c, q, 1)
                for k in range(KG, UG):
                    starts = bases_of(dve, NI - 1, k)
                    values(NI - 1, k)
                    for half in range(2):
                        add_sums(NI - 1, k, half, starts)
        layer.close()

        m3_r, m3_b, m3_u, m3_m, m3_c, m3_dve, m3_sd, m3_t, m3_x, m3_o = [sem("m3_" + x) for x in
            ("r", "b", "u", "m", "c", "dve", "sd", "t", "x", "o")]
        OT = tmp("OT", [D, N])
        sq = tmp("sq", [D, N])
        rden = tmp("rden", [8, N])
        bn = tmp("bn", [D, 8])
        CH = rounds(N, 512)
        with nc.Block() as block:
            @block.vector
            def _(dve):
                c = Chain(dve, m3_r)
                c.link(dve.tensor_scalar(rden[:], acc[0:8, 1, 0:N], 1e-16, None, ALU.add))
                c.mark(dve.reciprocal(rden[:], rden[:]))
                for n, (a, w) in enumerate(CH):
                    dve.wait_ge(m3_b, n + 1)
                    dve.tensor_tensor(acc[:, 0, a:a + w], acc[:, 0, a:a + w], bank[n % 2][:, 0:w], ALU.mult).then_inc(m3_u, 1)
                dve.wait_ge(m3_c, len(CH))
                c = Chain(dve, m3_dve)
                c.link(dve.tensor_reduce(bn[:, 0:1], OT[:], AX.X, ALU.add))
                c.link(dve.tensor_scalar(bn[:, 1:2], bn[:, 0:1], -1.0 / N, None, ALU.mult))
                c.link(dve.tensor_scalar(OT[:], OT[:], bn[:, 1:2], None, ALU.add))
                c.link(dve.tensor_tensor(sq[:], OT[:], OT[:], ALU.mult))
                c.link(dve.tensor_reduce(bn[:, 2:3], sq[:], AX.X, ALU.add))
                c.link(dve.tensor_scalar(bn[:, 3:4], bn[:, 2:3], 1.0 / N, EPS, ALU.mult, ALU.add))
                dve.wait_ge(m3_sd, 1)
                c.link(dve.reciprocal(bn[:, 5:6], bn[:, 4:5]))
                c.link(dve.tensor_tensor(bn[:, 6:7], bn[:, 5:6], gcol[:], ALU.mult))
                c.link(dve.tensor_scalar(OT[:], OT[:], bn[:, 6:7], bcol[:, 0:1], ALU.mult, ALU.add))
                for r, (j0, n) in enumerate(rounds(NJ, 4)):
                    dve.wait_ge(m3_t, r + 1)
                    dve.tensor_tensor(X[:, j0:j0 + n, :], X[:, j0:j0 + n, :],
                                      bank[4 + r % 2][0:PN, 0:n * D].rearrange("p (j f) -> p j f", j=n), ALU.add).then_inc(m3_x, 1)

            @block.tensor
            def _(pe):
                pe.wait_ge(m3_r, 2)
                for n, (a, w) in enumerate(CH):
                    if n >= 2:
                        pe.wait_ge(m3_u, n - 1)
                    pe.matmul(bank[n % 2][:, 0:w], sel_b[:], rden[:, a:a + w], start=True, stop=True).then_inc(m3_b, 1)
                    pe.wait_ge(m3_u, n + 1)
                    if n >= 2:
                        pe.wait_ge(m3_c, n - 1)
                    pe.matmul(bank[2 + n % 2][0:D, 0:w], w_self[:], HT[:, a:a + w], start=True, stop=False)
                    pe.matmul(bank[2 + n % 2][0:D, 0:w], w_out[:], acc[:, 0, a:a + w], start=False, stop=True).then_inc(m3_m, 1)
                pe.wait_ge(m3_dve, 9)
                for r, (j0, n) in enumerate(rounds(NJ, 4)):
                    if r >= 2:
                        pe.wait_ge(m3_x, r - 1)
                    for j in range(n):
                        last = pe.transpose(bank[4 + r % 2][0:PN, j * D:(j + 1) * D], OT[:, (j0 + j) * PN:(j0 + j + 1) * PN],
                                            ident[0:D, 0:D])
                    last.then_inc(m3_t, 1)

            @block.scalar
            def _(act):
                for n, (a, w) in enumerate(CH):
                    act.wait_ge(m3_m, n + 1)
                    act.activation(OT[:, a:a + w], bank[2 + n % 2][0:D, 0:w], ACT.Copy).then_inc(m3_c, 1)
                act.wait_ge(m3_dve, 6)
                act.activation(bn[:, 4:5], bn[:, 3:4], ACT.Sqrt).then_inc(m3_sd, 1)

            @block.sync
            def _(sp):
                o = out.rearrange("(j p) f -> p j f", p=PN)
                for r, (j0, n) in enumerate(rounds(NJ, 4)):
                    sp.wait_ge(m3_x, r + 1)
                    sp.dma_start(o[:, j0:j0 + n, :], X[:, j0:j0 + n, :]).then_inc(m3_o, 16)
                sp.wait_ge(m3_o, 16 * len(rounds(NJ, 4)))
        end_of_layer()


def kernel(**inputs):
    import numpy as np
    import concourse.bacc as bacc
    from concourse.bass_utils import run_bass_kernel_spmd as run

    nc = bacc.Bacc("TRN2", target_bir_lowering=False, num_devices=1)
    a = {k: np.asarray(v) for k, v in inputs.items()}
    fill = EP - E

    def rows(v, value):
        return np.pad(v, (0, fill), constant_values=value)

    a["src"] = rows(a["src"], 0).reshape(NT, W).T
    a["dst"] = rows(a["dst"], -1).reshape(NT, W).T
    dst = a["dst"].T.reshape(-1)
    a["dst_rows"] = dst.reshape(NT, W)
    a["dst_before"] = np.concatenate([np.full(1, -2, dst.dtype), dst[:-1]]).reshape(NT, W).T
    a["rel"] = rows(a.pop("edge_type_8"), 0).reshape(1, EP)
    a["ea16"] = np.pad(a.pop("edge_attr_16"), ((0, fill), (0, 0))).T
    a["ea64"] = np.pad(a.pop("edge_attr_64"), ((0, fill), (0, 0))).T
    a["ea9"] = np.pad(a.pop("edge_attr_9"), ((0, fill), (0, 0))).T
    a["L2_gnn_WT"] = a.pop("L2_gnn_W").T
    for k, v in a.items():
        a[k] = np.ascontiguousarray(v.reshape(1, -1) if v.ndim == 1 else v)
    arrays = {f"in_{k}": v for k, v in a.items()}
    aps = {k: nc.dram_tensor(f"in_{k}", v.shape, mybir.dt.from_np(v.dtype), kind="ExternalInput").ap() for k, v in a.items()}
    out = nc.dram_tensor("out_x", (N, D), F32, kind="ExternalOutput").ap()
    build(nc, aps, out)
    return run(nc, [arrays], core_ids=[0]).results[0]["out_x"]
```

```python
from contextlib import ExitStack

import concourse.bass as bass
from concourse import mybir

F32 = mybir.dt.float32
BF16 = mybir.dt.bfloat16
I32 = mybir.dt.int32
ALU = mybir.AluOpType
ACT = mybir.ActivationFunctionType
AX = mybir.AxisListType

N = 3125
D = 64
E = 53125
PN = 125
NJ = N // PN
W = 128
NT = -(-E // (32 * W)) * 32
EP = NT * W
GT = 4
UG = 8
UT = GT * UG
NI = NT // UT
NW = N + W
REL = 8
EPS = 1e-5
SLOPE = 0.2
BIG = 1e30
GCOL = 128
LAST = "L3"
STAGES = ["L0", "L1", "L2", "L3"]


def wait(eng, sem, value):
    if not isinstance(value, int) or value > 0:
        eng.wait_ge(sem, value)


class Chain:

    def __init__(self, eng, sem):
        self.eng, self.sem, self.n = eng, sem, 0

    def mark(self, ins):
        self.n += 1
        ins.then_inc(self.sem, 1)

    def link(self, ins):
        self.mark(ins)
        self.eng.wait_ge(self.sem, self.n)


class LoopChain:

    def __init__(self, eng, sem, i, steps, done=0):
        self.eng, self.sem, self.at, self.k, self.steps = eng, sem, i * steps, done, steps

    def link(self, ins):
        self.mark(ins)
        self.eng.wait_ge(self.sem, self.at + self.k)

    def mark(self, ins):
        self.k += 1
        ins.then_inc(self.sem, 1)

    def done(self):
        assert self.k == self.steps, (self.k, self.steps)


def rounds(n, k):
    return [(a, min(k, n - a)) for a in range(0, n, k)]


def build(nc, A, out):
    with ExitStack() as ctx:
        def sb(name, shape, dt=F32):
            return ctx.enter_context(nc.sbuf_tensor(name, shape, dt))

        layer = ExitStack()
        sems = []

        def tmp(name, shape, dt=F32):
            return layer.enter_context(nc.sbuf_tensor(name, shape, dt))

        def sem(name):
            sems.append(nc.alloc_semaphore(name=name))
            return sems[-1]

        def end_of_layer():
            layer.close()
            nc.clear_and_free_semaphores(sems)
            sems.clear()
            nc.all_engine_barrier()

        def dram(name, shape, dt=F32):
            return nc.dram_tensor(name, shape, dt, kind="Internal").ap()

        bank = [ctx.enter_context(nc.psum_tensor(f"bank{b}", [128, 512], F32)) for b in range(8)]

        X = sb("X", [PN, NJ, D])
        H = sb("H", [PN, NJ, D])
        HT = sb("HT", [D, N])
        acc = sb("acc", [128, 3, NW])
        ident = sb("ident", [128, 128])
        iota_row = sb("iota_row", [128, 128])
        iota_i = sb("iota_i", [128, 128], I32)
        iota_p = sb("iota_p", [128, 1])
        iota_pi = sb("iota_pi", [128, 1], I32)
        src_i = sb("src_i", [128, NT], I32)
        dst_i = sb("dst_i", [128, NT], I32)
        base_i = sb("base_i", [128, NT], I32)
        dloc = sb("dloc", [128, NT])
        base_f = sb("base_f", [128, NT])
        edge_a = sb("edge_a", [128, NT, 4])
        st = sb("st", [PN, 8, NJ])
        cnt = sb("cnt", [PN, NJ])
        zero = sb("zero", [128, 256])
        idx = sb("idx", [128, UT], I32)

        loop_a = sb("loop_a", [PN, NJ, 4])

        w1 = sb("w1", [D, 2, D])
        wre = sb("wre", [REL + 16, D + 4])
        b1r = sb("b1r", [REL, D])
        w2x = sb("w2x", [D + 5, D + 5])
        wedge = sb("wedge", [16, 4, 64])
        atte = sb("atte", [16, 4, 64])
        v16 = sb("v16", [16, 4])

        s_done = {}

        TA = dram("TA", [N, D])
        TB = dram("TB", [NW, D])
        DL = dram("DL", [1, EP], BF16)

        l_x, l_i, l_w0 = sem("l_x"), sem("l_i"), sem("l_w0")
        c_pool, c_dve, c_zero = sem("c_pool"), sem("c_dve"), sem("c_zero")
        l_zero, l_d, l_dl = sem("l_zero"), sem("l_d"), sem("l_dl")
        dr_i = tmp("dr_i", [NT // GT, GT, W], I32)
        dr_f = tmp("dr_f", [NT // GT, GT, W])
        dr_b = tmp("dr_b", [NT // GT, GT, W], BF16)
        with nc.Block() as block:
            @block.sync
            def _(sp):
                sp.dma_start(X[:], A["x"].rearrange("(j p) f -> p j f", p=PN)).then_inc(l_x, 16)
                sp.dma_start(dr_i[:], A["dst_rows"].rearrange("(p t) e -> p t e", t=GT)).then_inc(l_d, 16)
                sp.dma_start(src_i[:], A["src"]).then_inc(l_i, 16)
                sp.dma_start(dst_i[:], A["dst"]).then_inc(l_i, 16)
                sp.dma_start(base_i[:], A["dst"][0:1, :].partition_broadcast(128)).then_inc(l_i, 16)
                w1d = A["L0_gnn_W1"]
                sp.dma_start(w1[:], w1d[0:2 * D, :].rearrange("(a k) n -> k a n", a=2)).then_inc(l_w0, 16)
                sp.dma_start(b1r[:], A["L0_gnn_b1"].partition_broadcast(REL)).then_inc(l_w0, 16)
                sp.wait_ge(c_zero, 1)
                sp.dma_start(wre[0:REL, 0:D], w1d[2 * D:2 * D + REL, :]).then_inc(l_w0, 16)
                sp.dma_start(w2x[0:D, 0:D], A["L0_gnn_W2"]).then_inc(l_w0, 16)
                sp.dma_start(w2x[D:D + 1, 0:D], A["L0_gnn_b2"]).then_inc(l_w0, 16)
                sp.dma_start(wedge[:], A["L1_gnn_W_edge"].rearrange("k (h c) -> k h c", h=4)).then_inc(l_w0, 16)
                sp.dma_start(atte[:], A["L1_gnn_att_edge"].partition_broadcast(16)).then_inc(l_w0, 16)
                sp.wait_ge(c_dve, 2)
                sp.dma_start(TB[N:NW, :], zero[:, 0:D]).then_inc(l_zero, 16)
                sp.wait_ge(c_dve, 12)
                sp.dma_start(DL.rearrange("o (p f) -> (o p) f", p=NT // GT), dr_b[:].rearrange("p t e -> p (t e)")).then_inc(l_dl, 16)
                sp.dma_start(wre[REL:REL + 16, D:D + 4], v16[:]).then_inc(l_dl, 16)
                sp.wait_ge(l_dl, 32)
                sp.wait_ge(l_zero, 16)
                sp.wait_ge(l_x, 16)
                sp.wait_ge(l_i, 48)
                sp.wait_ge(l_w0, 7 * 16)

            @block.gpsimd
            def _(pool):
                pool.memset(w2x[:], 0.0).then_inc(c_pool, 1)
                pool.memset(wre[:], 0.0).then_inc(c_pool, 1)
                pool.memset(ident[:], 0.0).then_inc(c_pool, 1)
                pool.iota(iota_i[:], [[1, 128]], 0, 0).then_inc(c_pool, 1)
                pool.iota(iota_pi[:], [[0, 1]], 0, 1).then_inc(c_pool, 1)
                pool.wait_ge(c_pool, 5)
                pool.affine_select(out=ident[:], in_=ident[:], compare_op=ALU.not_equal, fill=1.0, base=0,
                                   pattern=[[-1, 128]], channel_multiplier=1).then_inc(c_pool, 1)
                pool.affine_select(out=w2x[:, D:D + 5], in_=w2x[:, D:D + 5], compare_op=ALU.not_equal, fill=1.0,
                                   base=-D, pattern=[[-1, 5]], channel_multiplier=1).then_inc(c_zero, 1)

            @block.vector
            def _(dve):
                c = Chain(dve, c_dve)
                c.mark(dve.memset(acc[:], 0.0))
                c.mark(dve.memset(zero[:], 0.0))
                dve.wait_ge(c_pool, 5)
                c.mark(dve.tensor_copy(iota_row[:], iota_i[:]))
                c.mark(dve.tensor_copy(iota_p[:], iota_pi[:]))
                dve.wait_ge(l_i, 48)
                c.mark(dve.tensor_copy(dloc[:], dst_i[:]))
                c.link(dve.tensor_copy(base_f[:], base_i[:]))
                c.mark(dve.tensor_tensor(dloc[:], dloc[:], base_f[:], ALU.subtract))
                dve.wait_ge(l_w0, 7 * 16)
                c.mark(dve.tensor_tensor(wre[0:REL, 0:D], wre[0:REL, 0:D], b1r[:], ALU.add))
                c.link(dve.tensor_tensor(wedge[:], wedge[:], atte[:], ALU.mult))
                c.mark(dve.tensor_reduce(v16[:], wedge[:], AX.X, ALU.add))
                dve.wait_ge(l_d, 16)
                c.link(dve.tensor_copy(dr_f[:], dr_i[:]))
                c.mark(dve.tensor_tensor(dr_b[:], dr_f[:], dr_f[:, :, 0:1].to_broadcast([NT // GT, GT, W]), ALU.subtract))

        layer.close()

        def node_buffers(p):
            return tmp(p + "_XC", [PN, NJ, D]), tmp(p + "_yn", [PN, NJ, D]), tmp(p + "_tab", [PN, NJ, 2 * D])

        def ln_relu_steps(c, s_var, s_std, n, dst=H, src=X, relu=True, XC=None):
            dve = c.eng
            bc = lambda r: st[:, r, :].unsqueeze(2).to_broadcast([PN, NJ, D])
            c.link(dve.tensor_reduce(st[:, 0, :], src[:], AX.X, ALU.add))
            c.link(dve.tensor_scalar(st[:, 1, :], st[:, 0, :], -1.0 / D, None, ALU.mult))
            c.link(dve.tensor_tensor(XC[:], src[:], bc(1), ALU.add))
            c.link(dve.tensor_tensor(dst[:], XC[:], XC[:], ALU.mult))
            c.link(dve.tensor_reduce(st[:, 2, :], dst[:], AX.X, ALU.add))
            dve.tensor_scalar(st[:, 3, :], st[:, 2, :], 1.0 / D, EPS, ALU.mult, ALU.add).then_inc(s_var, 1)
            dve.wait_ge(s_std, n)
            c.link(dve.reciprocal(st[:, 5, :], st[:, 4, :]))
            c.link(dve.tensor_tensor(dst[:], XC[:], bc(5), ALU.mult))
            if relu:
                c.link(dve.tensor_scalar(dst[:], dst[:], 0.0, None, ALU.max))

        def ln_std_step(act, s_var, s_std, n):
            act.wait_ge(s_var, n)
            act.activation(st[:, 4, :], st[:, 3, :], ACT.Sqrt).then_inc(s_std, 1)

        def transpose_steps(pe, s_t, s_free, src=H):
            for r, (j0, n) in enumerate(rounds(NJ, 4)):
                if r >= 2:
                    pe.wait_ge(s_free, r - 1)
                for j in range(n):
                    last = pe.transpose(bank[r % 2][0:D, j * PN:(j + 1) * PN], src[:, j0 + j, :], ident[0:PN, 0:PN])
                last.then_inc(s_t, 1)

        def transposed_copy_steps(act, s_t, s_free, dst=HT):
            for r, (j0, n) in enumerate(rounds(NJ, 4)):
                act.wait_ge(s_t, r + 1)
                act.activation(dst[0:D, j0 * PN:(j0 + n) * PN], bank[r % 2][0:D, 0:n * PN], ACT.Copy).then_inc(s_free, 1)

        def gather_program(ga, pool, table, width, s_g, s_used, s_idx, s_step, ring=UG, per=1):
            def half(i, hh):
                for k in range(hh * 4, hh * 4 + 4):
                    wait(pool, s_g[k], i * 64)
                pool.tensor_copy(idx[:, hh * 16:hh * 16 + 16], src_i[:, bass.ds(i * UT + hh * 16, 16)]).then_inc(s_idx, 1)
                pool.wait_ge(s_idx, i * 2 + (hh + 1))
                pool.sem_inc(s_step, 1)
                for k in range(hh * 4, hh * 4 + 4):
                    if not isinstance(i, int) or k >= ring:
                        pool.wait_ge(s_used, (i * UG + (k - ring + 1)) * per)
                        pool.sem_inc(s_step, 1)
                    for t in range(GT):
                        o = ga[:, (k % ring) * GT + t, 0:width]
                        pool.indirect_dma_start(o, None, table, bass.IndirectOffsetOnAxis(
                            ap=idx[:, k * GT + t:k * GT + t + 1], axis=0)).then_inc(s_g[k], 16)
            for hh in range(2):
                half(0, hh)
            with pool.Fori(1, NI) as i:
                for hh in range(2):
                    half(i, hh)

        def each_group(eng, body):
            for k in range(UG):
                body(0, k)
            with eng.Fori(1, NI) as i:
                for k in range(UG):
                    body(i, k)

        def before(i, k):
            if k:
                return i, k - 1
            return None if isinstance(i, int) and i == 0 else (i - 1, UG - 1)

        def back(i, k, n):
            if k >= n:
                return i, k - n
            return None if isinstance(i, int) and i == 0 else (i - 1, UG + k - n)

        def base_of(eng, i, k, t):
            return eng.value_load(base_i[0:1, bass.ds(i * UT + (k * GT + t), 1)], min_val=0, max_val=N - 1)

        def bases_of(eng, i, k):
            _, values = nc.values_load_multi_w_load_instructions(
                base_i[0:1, bass.ds(i * UT + k * GT, GT)], engines=[eng.engine], min_val=0, max_val=N - 1,
                skip_runtime_bounds_check_because="a destination is a node")
            return values

        def window_loads(win, eng, i, k, table, width, s_w, s_used, s_step, tiles=range(GT), ring=UG):
            starts = bases_of(eng, i, k)
            wait(eng, s_used, i * UG + (k - ring + 1))
            eng.sem_inc(s_step, 1)
            for t in tiles:
                b = starts[t]
                eng.dma_start(win[:, (k % ring) * GT + t, 0:width], table[bass.ds(b, W), :]).then_inc(s_w[k % ring], 16)

        DR = 4

        def place_load(dl, eng, i, k, s_dl, s_oT, s_step):
            wait(eng, s_oT, i * UG + (k - DR + 1))
            eng.sem_inc(s_step, 1)
            cols = bass.ds((i * UG + k) * GT * W, GT * W)
            eng.dma_start(dl[:, k % DR, :], DL[:, cols].partition_broadcast(128)).then_inc(s_dl[k % DR], 16)

        def transposed_one_hot_step(o, dl, dve, i, k, s_dl, s_oT):
            dve.wait_ge(s_dl[k % DR], i * (UG // DR * 16) + (k // DR + 1) * 16)
            dve.tensor_scalar(o, dl[:, k % DR, :], iota_p[:, 0:1], None, ALU.is_equal).then_inc(s_oT, 1)

        def one_hot_ring_step(one, dve, i, k, s_one):
            dve.tensor_tensor(one[:, k * GT:(k + 1) * GT, :], iota_row[:].unsqueeze(1).to_broadcast([128, GT, 128]),
                              dloc[:, bass.ds(i * UT + k * GT, GT)].unsqueeze(2).to_broadcast([128, GT, 128]),
                              ALU.is_equal).then_inc(s_one, 1)

        n0_dve, n0_var, n0_std, n0_t, n0_tc, n0_m, n0_mc, n0_o = [sem("n0_" + x) for x in
            ("dve", "var", "std", "t", "tc", "m", "mc", "o")]
        XC, yn, tab = node_buffers("n0")
        with nc.Block() as block:
            @block.vector
            def _(dve):
                c = Chain(dve, n0_dve)
                ln_relu_steps(c, n0_var, n0_std, 1, XC=XC)

            @block.scalar
            def _(act):
                ln_std_step(act, n0_var, n0_std, 1)
                transposed_copy_steps(act, n0_t, n0_tc)
                for r, (j0, n) in enumerate(rounds(NJ, 4)):
                    act.wait_ge(n0_m, r + 1)
                    act.activation(tab[:, j0:j0 + n, :], bank[2 + r % 2][0:PN, 0:n * 128].rearrange("p (j f) -> p j f", j=n),
                                   ACT.Copy).then_inc(n0_mc, 1)

            @block.tensor
            def _(pe):
                pe.wait_ge(n0_dve, 8)
                transpose_steps(pe, n0_t, n0_tc)
                for r, (j0, n) in enumerate(rounds(NJ, 4)):
                    pe.wait_ge(n0_tc, r + 1)
                    if r >= 2:
                        pe.wait_ge(n0_mc, r - 1)
                    for j in range(n):
                        last = pe.matmul(bank[2 + r % 2][0:PN, j * 128:(j + 1) * 128], HT[:, (j0 + j) * PN:(j0 + j + 1) * PN],
                                         w1[:].rearrange("k a n -> k (a n)"), start=True, stop=True)
                    last.then_inc(n0_m, 1)

            @block.sync
            def _(sp):
                sp.wait_ge(n0_mc, len(rounds(NJ, 4)))
                sp.dma_start(TA.rearrange("(j p) f -> p j f", p=PN), tab[:, :, 0:D]).then_inc(n0_o, 16)
                sp.dma_start(TB[0:N, :].rearrange("(j p) f -> p j f", p=PN), tab[:, :, D:2 * D]).then_inc(n0_o, 16)
                sp.wait_ge(n0_o, 32)

        layer.close()

        e0_g = [sem(f"e0_g{k}") for k in range(UG)]
        e0_w = [sem(f"e0_w{k}") for k in range(UG)]
        e0_e = [sem(f"e0_e{k}") for k in range(2)]
        e0_dl = [sem(f"e0_dl{k}") for k in range(DR)]
        e0_idx, e0_step, e0_sp, e0_act, e0_one, e0_oT, e0_rel, e0_P, e0_pre, e0_ms, e0_S, e0_acc = [sem("e0_" + x) for x in
            ("idx", "step", "sp", "act", "one", "oT", "rel", "P", "pre", "ms", "S", "acc")]
        ga = tmp("ga0", [128, UT, D])
        win = tmp("win0", [128, UT, D])
        one = tmp("one0", [128, UT, 128])
        oneT = tmp("oneT0", [128, 2, GT * W])
        dl = tmp("dl0", [128, DR, GT * W], BF16)
        rel_i = tmp("rel_i", [REL, 2, GT * W], I32)
        re = tmp("re", [REL + 16, 2, GT * W])
        pre = tmp("pre", [128, 2, GT, D])
        msg = tmp("msg", [128, 2, GT, D + 5])
        MS = D + 5
        e0_ones = sem("e0_ones")
        with nc.Block() as block:
            @block.gpsimd
            def _(pool):
                pool.memset(msg[:, :, :, D:D + 1], 1.0).then_inc(e0_ones, 1)
                gather_program(ga, pool, TA, D, e0_g, e0_pre, e0_idx, e0_step)

            @block.sync
            def _(sp):
                def body(i, k):
                    place_load(dl, sp, i, k, e0_dl, e0_oT, e0_sp)
                    window_loads(win, sp, i, k, TB, D, e0_w, e0_P, e0_sp, range(0, GT // 2))
                each_group(sp, body)

            @block.scalar
            def _(act):
                def loads(i, k):
                    wait(act, e0_P, i * UG + (k - 1))
                    wait(act, e0_rel, i * UG + (k - 1))
                    cols = bass.ds((i * UG + k) * GT * W, GT * W)
                    act.dma_start(rel_i[:, k % 2, :], A["rel"][:, cols].partition_broadcast(REL)).then_inc(e0_e[k % 2], 16)
                    act.dma_start(re[REL:REL + 16, k % 2, :], A["ea16"][:, cols]).then_inc(e0_e[k % 2], 16)
                    window_loads(win, act, i, k, TB, D, e0_w, e0_P, e0_act, range(GT // 2, GT))

                def messages(i, k):
                    g = i * UG + k
                    P = bank[k % 2][:, 0:GT * (D + 4)].rearrange("p (t f) -> p t f", t=GT)
                    act.wait_ge(e0_pre, g + 1)
                    wait(act, e0_S, g - 1)
                    act.activation(msg[:, k % 2, :, 0:D], pre[:, k % 2], ACT.Relu).then_inc(e0_ms, 1)
                    act.activation(msg[:, k % 2, :, D + 1:MS], P[:, :, D:D + 4], ACT.Copy).then_inc(e0_ms, 1)
                    act.activation(edge_a[:, bass.ds(g * GT, GT), :], P[:, :, D:D + 4], ACT.Copy).then_inc(e0_ms, 1)

                def body(i, k):
                    loads(i, k)
                    if before(i, k):
                        messages(*before(i, k))
                act.wait_ge(e0_ones, 1)
                each_group(act, body)
                messages(NI - 1, UG - 1)

            @block.tensor
            def _(pe):
                def sums(i, k):
                    g = i * UG + k
                    pe.wait_ge(e0_ms, g * 3 + 3)
                    wait(pe, e0_acc, (g - 1) * GT)
                    for t in range(GT):
                        last = pe.matmul(bank[4 + k % 2][0:MS, t * 128:(t + 1) * 128], msg[:, k % 2, t, :], one[:, k * GT + t, :],
                                         start=True, stop=True)
                    last.then_inc(e0_S, 1)

                def body(i, k):
                    g = i * UG + k
                    pe.wait_ge(e0_oT, g + 1)
                    pe.wait_ge(e0_rel, g + 1)
                    pe.wait_ge(e0_w[k], i * 64 + 64)
                    wait(pe, e0_ms, (g - 1) * 3)
                    for t in range(GT):
                        o = t * (D + 4)
                        P = bank[k % 2]
                        pe.matmul(P[:, o:o + D + 4], re[:, k % 2, t * W:(t + 1) * W], wre[:], start=True, stop=False)
                        last = pe.matmul(P[:, o:o + D], oneT[:, k % 2, t * 128:(t + 1) * 128], win[:, k * GT + t, 0:D],
                                         start=False, stop=True)
                    last.then_inc(e0_P, 1)
                    if back(i, k, 2):
                        sums(*back(i, k, 2))
                each_group(pe, body)
                sums(NI - 1, UG - 2)
                sums(NI - 1, UG - 1)

            @block.vector
            def _(dve):
                def add_sums(i, k, starts):
                    g = i * UG + k
                    dve.wait_ge(e0_S, g + 1)
                    for t, b in enumerate(starts):
                        wait(dve, e0_acc, g * GT + t)
                        a = acc[0:MS, 0, bass.ds(b, W)]
                        dve.tensor_tensor(a, a, bank[4 + k % 2][0:MS, t * 128:(t + 1) * 128], ALU.add).then_inc(e0_acc, 1)

                def with_gathered(i, k):
                    g = i * UG + k
                    dve.wait_ge(e0_P, g + 1)
                    dve.wait_ge(e0_g[k], i * 64 + 64)
                    wait(dve, e0_ms, (g - 1) * 3)
                    P = bank[k % 2][:, 0:GT * (D + 4)].rearrange("p (t f) -> p t f", t=GT)
                    dve.tensor_tensor(pre[:, k % 2], ga[:, k * GT:(k + 1) * GT, 0:D], P[:, :, 0:D], ALU.add).then_inc(e0_pre, 1)

                def body(i, k):
                    g = i * UG + k
                    wait(dve, e0_S, g - 7)
                    one_hot_ring_step(one, dve, i, k, e0_one)
                    wait(dve, e0_P, g - 1)
                    transposed_one_hot_step(oneT[:, k % 2, :], dl, dve, i, k, e0_dl, e0_oT)
                    dve.wait_ge(e0_e[k % 2], i * (UG // 2 * 32) + (k // 2 + 1) * 32)
                    dve.tensor_scalar(re[0:REL, k % 2, :], rel_i[:, k % 2, :], iota_p[0:REL, 0:1], None, ALU.is_equal).then_inc(e0_rel, 1)
                    old = back(i, k, 3)
                    if old:
                        starts = bases_of(dve, *old)
                    if before(i, k):
                        with_gathered(*before(i, k))
                    if old:
                        add_sums(*old, starts)
                each_group(dve, body)
                with_gathered(NI - 1, UG - 1)
                for k in range(UG - 3, UG):
                    add_sums(NI - 1, k, bases_of(dve, NI - 1, k))

        layer.close()
        m0_m, m0_dve, m0_c, m0_f = [sem("m0_" + x) for x in ("m", "dve", "c", "f")]
        with nc.Block() as block:
            @block.tensor
            def _(pe):
                for r, (j0, n) in enumerate(rounds(NJ, 4)):
                    if r >= 2:
                        pe.wait_ge(m0_f, r - 1)
                    for j in range(n):
                        last = pe.matmul(bank[r % 2][0:PN, j * 128:j * 128 + MS], acc[0:MS, 0, (j0 + j) * PN:(j0 + j + 1) * PN],
                                         w2x[:], start=True, stop=True)
                    last.then_inc(m0_m, 1)

            @block.vector
            def _(dve):
                c = Chain(dve, m0_dve)
                c.link(dve.tensor_tensor(X[:], X[:], H[:], ALU.add))
                for r, (j0, n) in enumerate(rounds(NJ, 4)):
                    dve.wait_ge(m0_m, r + 1)
                    P = bank[r % 2][0:PN, 0:n * 128].rearrange("p (j f) -> p j f", j=n)
                    c.mark(dve.tensor_tensor(X[:, j0:j0 + n, :], X[:, j0:j0 + n, :], P[:, :, 0:D], ALU.add))
                    c.mark(dve.tensor_copy(cnt[:, j0:j0 + n], P[:, :, D]))
                    c.mark(dve.tensor_copy(loop_a[:, j0:j0 + n, :], P[:, :, D + 1:MS]))
                    dve.wait_ge(m0_dve, c.n)
                    dve.sem_inc(m0_f, 1)

        def finish(stage):
            if LAST != stage:
                return False
            z_o = sem("z_o")
            with nc.Block() as block:
                @block.sync
                def _(sp):
                    sp.dma_start(out.rearrange("(j p) f -> p j f", p=PN), X[:]).then_inc(z_o, 16)
                    sp.wait_ge(z_o, 16)
            return True
        end_of_layer()
        if finish("L0"):
            return

        SG = 16
        KG = SG // GT
        pl = sb("pl", [1, NT])
        ql = sb("ql", [1, NT])
        first = sb("first", [128, NT])
        sel = sb("sel", [128, 3, 128])
        sel8 = sb("sel8", [128, 2, 128])
        delta_t = sb("delta_t", [128, SG])
        dst_f = sb("dst_f", [128, NT])
        al = sb("al", [128, 1, 64])
        exf = sb("exf", [128, 128])
        exb = sb("exb", [128, 2, 3, 128], BF16)
        parts8 = sb("parts8", [24, 8])
        am = sb("am", [128, 128])
        lp = sb("lp", [128, 64])
        dsth = sb("dsth", [128, 128])
        dT = sb("dT", [128, 130])
        pen = sb("pen", [128, 129])
        f1 = sb("f1", [128, 128])
        mx = sb("mx", [128, 128])
        mlast = sb("mlast", [128, 1])
        crow = sb("crow", [1, 8, SG + 1])
        prow = sb("prow", [1, 8, SG + 1])
        lrow = sb("lrow", [1, 8, SG + 1])
        cshift = sb("cshift", [1, 8, SG])
        ccol = sb("ccol", [128, 1])
        cm = sb("cm", [128, 1])
        fdiag = sb("fdiag", [128, SG])
        fac = sb("fac", [128, 2, 3, SG])
        ex = sb("ex", [128, 2, 2, 128])
        s_b = {}

        def softmax_sems(p):
            return {x: sem(f"{p}_{x}") for x in ("xc", "xb", "al", "T1", "dT", "pen", "f1", "ml", "cr", "cc", "mx", "cm", "pen2", "pe", "fd", "me",
                                                 "fac", "sub", "ex", "bd")}

        flat = lambda v, heads: v[:, 0:heads, :].rearrange("p h t -> p (h t)")
        rows_of = lambda v, heads: v.unsqueeze(1).to_broadcast([v.shape[0], heads, SG])
        SOFT = 14
        SOFT_1 = 9

        def softmax_dve_0(dve, S, c, c0, heads):
            R = heads * SG
            c.mark(dve.tensor_copy(dsth[:, 0:R].rearrange("p (h t) -> p h t", h=heads), rows_of(dst_f[:, bass.ds(c0, SG)], heads)))
            c.link(dve.tensor_copy(prow[:, 0:heads, 1:SG + 1], rows_of(pl[:, bass.ds(c0, SG)], heads)))
            dve.sem_inc(S["al"], 1)

        def softmax_dve_1(dve, S, c, q, heads):
            R = heads * SG
            dve.wait_ge(S["dT"], q + 1)
            c.link(dve.tensor_tensor(pen[0:R, 1:128], dT[0:R, 1:128], dT[0:R, 0:127], ALU.is_equal))
            c.link(dve.tensor_scalar(pen[0:R, 1:128], pen[0:R, 1:128], -1.0, BIG, ALU.add, ALU.mult))
            c.link(dve.tensor_tensor_scan(f1[0:R, :], pen[0:R, 0:128], bank[3][0:R, 0:128], -BIG, ALU.add, ALU.max))
            dve.sem_inc(S["f1"], 1)

        def softmax_dve_2(dve, S, c, q, c0, heads):
            R = heads * SG
            dve.wait_ge(S["ml"], q + 1)
            c.link(dve.tensor_copy(crow[:, 0:heads, 1:SG + 1], bank[3][0:1, 256:256 + R].rearrange("p (h t) -> p h t", h=heads)))
            c.link(dve.tensor_tensor_scan(flat(lrow, heads), flat(prow, heads), flat(crow, heads), -BIG, ALU.add, ALU.max))
            c.mark(dve.tensor_copy(crow[:, 0:heads, 0:1], lrow[:, 0:heads, SG:SG + 1]))
            c.link(dve.tensor_tensor(cshift[:, 0:heads, :], lrow[:, 0:heads, 0:SG], rows_of(ql[:, bass.ds(c0, SG)], heads), ALU.add))
            dve.sem_inc(S["cr"], 1)

        def softmax_dve_3(dve, S, c, q, heads):
            R = heads * SG
            dve.wait_ge(S["cc"], q + 1)
            c.link(dve.tensor_copy(ccol[0:R, :], bank[3][0:R, 384:385]))
            c.link(dve.tensor_tensor_scan(f1[0:R, :], pen[0:R, 0:128], bank[3][0:R, 0:128], ccol[0:R, 0:1], ALU.add, ALU.max))
            c.link(dve.tensor_tensor_scan(mx[0:R, ::-1], pen[0:R, 128:0:-1], f1[0:R, ::-1], -BIG, ALU.add, ALU.max))
            c.link(dve.tensor_tensor(cm[0:R, :], ccol[0:R, :], mx[0:R, 0:1], ALU.subtract))
            dve.sem_inc(S["mx"], 1)

        def softmax_dve_4(dve, S, c, q, heads):
            R = heads * SG
            dve.wait_ge(S["cm"], q + 1)
            c.link(dve.tensor_scalar(fdiag[0:R, :], delta_t[0:R, :], cm[0:R, 0:1], None, ALU.mult))
            dve.sem_inc(S["fd"], 1)
            c.done()
            dve.wait_ge(S["me"], q + 1)
            return bank[3][:, 128:128 + R]

        def softmax_pe_0(pe, S, q, heads):
            R = heads * SG
            pe.wait_ge(S["al"], q + 1)
            wait(pe, S["ex"], q * 2)
            pe.sem_inc(S["pe"], 1)
            pe.transpose(bank[3][0:R, 0:128], am[:, 0:R], ident[:])
            pe.transpose(bank[3][0:R, 128:256], dsth[:, 0:R], ident[:]).then_inc(S["T1"], 1)

        def softmax_pe_1(pe, S, q, heads):
            R = heads * SG
            pe.wait_ge(S["f1"], q + 1)
            pe.sem_inc(S["pe"], 1)
            pe.transpose(bank[3][0:1, 256:256 + R], f1[0:R, 127:128], ident[0:R, 0:R]).then_inc(S["ml"], 1)

        def softmax_pe_2(pe, S, q, heads):
            R = heads * SG
            pe.wait_ge(S["cr"], q + 1)
            pe.sem_inc(S["pe"], 1)
            pe.transpose(bank[3][0:R, 384:385], flat(cshift, heads), ident[0:1, 0:1]).then_inc(S["cc"], 1)

        def softmax_pe_3(pe, S, q, heads):
            R = heads * SG
            pe.wait_ge(S["mx"], q + 1)
            pe.sem_inc(S["pe"], 1)
            pe.transpose(bank[3][:, 128:128 + R], mx[0:R, :], ident[0:R, 0:R]).then_inc(S["me"], 1)

        def softmax_pe_4(pe, S, q, fb, heads, selm, nr):
            R = heads * SG
            pe.wait_ge(S["fd"], q + 1)
            pe.sem_inc(S["pe"], 1)
            for r in range(nr):
                last = pe.matmul(fb[:, r * SG:(r + 1) * SG], selm[0:R, r, :], fdiag[0:R, :], start=True, stop=True)
            last.then_inc(S["fac"], 1)

        def softmax_act_1(act, S, q, heads):
            act.wait_ge(S["T1"], q + 1)
            act.activation(dT[0:heads * SG, 0:128], bank[3][0:heads * SG, 128:256], ACT.Copy).then_inc(S["dT"], 1)

        def softmax_act_3(act, S, q, heads):
            act.wait_ge(S["mx"], q + 1)
            act.activation(cm[0:heads * SG, :], cm[0:heads * SG, :], ACT.Exp).then_inc(S["cm"], 1)

        def softmax_act_4(act, S, q, s, heads, nex):
            act.wait_ge(S["sub"], q + 1)
            act.activation(ex[:, s, 0:nex, 0:heads * SG], ex[:, s, 0:nex, 0:heads * SG], ACT.Exp).then_inc(S["ex"], 1)

        def softmax_act_5(act, S, q, s, fb, nr):
            act.wait_ge(S["fac"], q + 1)
            act.activation(fac[:, s, 0:nr, :], fb[:, 0:nr * SG].rearrange("p (r t) -> p r t", r=nr), ACT.Copy).then_inc(S["ex"], 1)

        def split_steps(dve, S, q, s, fill):
            c = LoopChain(dve, S["xc"], q, 5 + fill(None))
            dve.wait_ge(S["ex"], q * 2 + 1)
            fill(c)
            c.link(dve.tensor_copy(exb[:, s, 0, :], exf[:]))
            for part in (1, 2):
                c.link(dve.tensor_tensor(exf[:], exf[:], exb[:, s, part - 1, :], ALU.subtract))
                c.link(dve.tensor_copy(exb[:, s, part, :], exf[:]))
            c.done()
            dve.sem_inc(S["xb"], 1)

        def bf16_operands(act, S, i, k, Dw, ob, one, s_one, s_done):
            s, kk = k // KG, k % KG
            act.wait_ge(S["xb"], i * 2 + (s + 1))
            for part in range(3):
                act.activation(Dw[:, k % 2, :, part * 8:(part + 1) * 8],
                               exb[:, s, part, :].rearrange("p (x t) -> p t x", x=8)[:, kk * GT:(kk + 1) * GT, :],
                               ACT.Copy).then_inc(s_done, 1)
            act.wait_ge(s_one, i * UG + (k + 1))
            act.activation(ob[:, k % 2, :], one[:, k * GT:(k + 1) * GT, :].rearrange("p t n -> p (t n)"), ACT.Copy).then_inc(s_done, 1)

        LATE = KG + 2

        def pending(i, k, half):
            if k % KG != half or not back(i, k, half + 1):
                return None
            a, b = back(i, k, half + 1)
            return a, b // KG

        k_i, k_d, k_l, k_p = sem("k_i"), sem("k_d"), sem("k_l"), sem("k_p")
        dprev = sb("dprev", [128, NT], I32)
        lastr = sb("lastr", [1, NT + 1], I32)
        with nc.Block() as block:
            @block.sync
            def _(sp):
                sp.dma_start(dprev[:], A["dst_before"]).then_inc(k_l, 16)
                sp.wait_ge(k_d, 1)
                sp.dma_start(lastr[:, 1:NT + 1], A["dst"][W - 1:W, :]).then_inc(k_l, 16)

            @block.gpsimd
            def _(pool):
                for m in (sel, sel8, delta_t):
                    pool.memset(m[:], 0.0).then_inc(k_i, 1)
                pool.wait_ge(k_i, 3)
                n = 3
                for h in range(8):
                    pool.affine_select(out=delta_t[:], in_=delta_t[:], compare_op=ALU.not_equal, fill=1.0, base=-h * SG,
                                       pattern=[[-1, SG]], channel_multiplier=1).then_inc(k_i, 1)
                    n += 1
                    pool.wait_ge(k_i, n)
                for m, heads, cw in ((sel, 4, 64), (sel8, 8, 16)):
                    nr = 2 if heads == 4 else 1
                    for r in range(nr):
                        v = m[:, r, :]
                        pool.memset(v, 1.0).then_inc(k_i, 1)
                        n += 1
                        pool.wait_ge(k_i, n)
                        per = 128 // cw
                        vv = v.rearrange("p (a c) -> p a c", a=per)
                        pool.affine_select(out=vv, in_=vv, compare_op=ALU.is_ge, fill=0.0, base=-SG * per * r,
                                           pattern=[[-SG, per], [0, cw]], channel_multiplier=1).then_inc(k_i, 1)
                        n += 1
                        pool.wait_ge(k_i, n)
                        pool.affine_select(out=vv, in_=vv, compare_op=ALU.is_ge, fill=0.0, base=SG * per * r + SG - 1,
                                           pattern=[[SG, per], [0, cw]], channel_multiplier=-1).then_inc(k_i, 1)
                        n += 1
                        pool.wait_ge(k_i, n)
                    reps = 24 // heads
                    v = m[:, nr, 0:24]
                    pool.memset(v, 1.0).then_inc(k_i, 1)
                    n += 1
                    pool.wait_ge(k_i, n)
                    vv = v.rearrange("p (b h) -> p b h", b=reps)
                    pool.affine_select(out=vv, in_=vv, compare_op=ALU.is_ge, fill=0.0, base=0,
                                       pattern=[[0, reps], [-SG, heads]], channel_multiplier=1).then_inc(k_i, 1)
                    n += 1
                    pool.wait_ge(k_i, n)
                    pool.affine_select(out=vv, in_=vv, compare_op=ALU.is_ge, fill=0.0, base=SG - 1,
                                       pattern=[[0, reps], [SG, heads]], channel_multiplier=-1).then_inc(k_i, 1)
                    n += 1
                    pool.wait_ge(k_i, n)

            @block.vector
            def _(dve):
                c = Chain(dve, k_d)
                c.mark(dve.memset(lastr[:, 0:1], -2))
                c.mark(dve.memset(pen[:], 0.0))
                c.mark(dve.memset(prow[:], -BIG))
                c.mark(dve.tensor_reduce(parts8[:], ident[0:24, 0:24].rearrange("p (a x) -> p x a", a=3), AX.X, ALU.add))
                c.mark(dve.tensor_copy(dst_f[:], dst_i[:]))
                dve.wait_ge(k_l, 32)
                c.mark(dve.tensor_tensor(first[:], dst_i[:], dprev[:], ALU.not_equal))
                c.mark(dve.tensor_tensor(pl[:], lastr[:, 1:NT + 1], lastr[:, 0:NT], ALU.is_equal))
                c.link(dve.tensor_tensor(ql[:], base_i[0:1, :], lastr[:, 0:NT], ALU.is_equal))
                c.mark(dve.tensor_scalar(pl[:], pl[:], -1.0, BIG, ALU.add, ALU.mult))
                c.mark(dve.tensor_scalar(ql[:], ql[:], -1.0, BIG, ALU.add, ALU.mult))

        WD = 4 * 64
        wsd = sb("wsd", [D, 2, 4])
        ww0 = sb("ww0", [D, 4, D])
        wwbd = sb("wwbd", [128, 2, 2, D])
        biasc = sb("biasc", [128, 2])
        biasb = sb("biasb", [128, 2, PN])
        cb = sb("cb", [PN, D])
        bpb = sb("bpb", [PN, D])
        gamma = sb("gamma", [PN, D])
        beta = sb("beta", [PN, D])
        w_att = tmp("w_att", [D, 4, 64])
        att = tmp("att", [D, 2, 4, 64])
        gw = tmp("gw", [D, WD])
        wp = tmp("wp", [128, 2, D])
        wT = tmp("wT", [128, 2, D])
        asd = tmp("asd", [PN, NJ, 8])
        dw = tmp("dw", [PN, NJ, 8])
        T1 = dram("T1", [N, D + 4])
        T1W = dram("T1W", [NW, 8])
        n1_l, n1_dve, n1_var, n1_std, n1_t, n1_tc, n1_pw, n1_aw, n1_m, n1_o, n1_pp = [sem("n1_" + x) for x in
            ("l", "dve", "var", "std", "t", "tc", "pw", "aw", "m", "o", "pp")]
        XC, yn, tab = node_buffers("n1")
        with nc.Block() as block:
            @block.sync
            def _(sp):
                sp.dma_start(gw[:], A["L1_gnn_W"]).then_inc(n1_l, 16)
                sp.dma_start(att[:, 0], A["L1_gnn_att_src"].rearrange("h c -> (h c)").unsqueeze(0).partition_broadcast(D)).then_inc(n1_l, 16)
                sp.dma_start(att[:, 1], A["L1_gnn_att_dst"].rearrange("h c -> (h c)").unsqueeze(0).partition_broadcast(D)).then_inc(n1_l, 16)
                sp.dma_start(wp[:], A["L1_gnn_Wp"].rearrange("(g p) o -> p g o", g=2)).then_inc(n1_l, 16)
                sp.dma_start(bpb[:], A["L1_gnn_bp"].partition_broadcast(PN)).then_inc(n1_l, 16)
                sp.dma_start(gamma[:], A["L1_gnn_gamma"].partition_broadcast(PN)).then_inc(n1_l, 16)
                sp.dma_start(beta[:], A["L1_gnn_beta"].partition_broadcast(PN)).then_inc(n1_l, 16)
                with nc.allow_non_contiguous_dma(reason="256 floats, a column for each pair of heads"):
                    sp.dma_start(biasc[:], A["L1_gnn_bias"].rearrange("a (g p) -> (a p) g", g=2)).then_inc(n1_l, 16)
                sp.dma_start(T1W[N:NW, :], zero[:, 0:8]).then_inc(n1_o, 16)
                sp.wait_ge(n1_dve, 24)
                sp.dma_start(T1.rearrange("(j p) f -> p j f", p=PN)[:, :, 0:D], H[:]).then_inc(n1_o, 16)
                sp.dma_start(T1.rearrange("(j p) f -> p j f", p=PN)[:, :, D:D + 4], asd[:, :, 0:4]).then_inc(n1_o, 16)
                sp.dma_start(T1W[0:N, :].rearrange("(j p) f -> p j f", p=PN), dw[:]).then_inc(n1_o, 16)
                sp.wait_ge(n1_o, 64)

            @block.vector
            def _(dve):
                c = Chain(dve, n1_dve)
                ln_relu_steps(c, n1_var, n1_std, 1, XC=XC)
                c.mark(dve.memset(acc[:], 0.0))
                c.mark(dve.memset(wwbd[:], 0.0))
                dve.wait_ge(n1_l, 8 * 16)
                for a in range(2):
                    c.link(dve.tensor_tensor(w_att[:], gw[:].rearrange("k (h c) -> k h c", h=4), att[:, a], ALU.mult))
                    c.link(dve.tensor_reduce(wsd[:, a, :], w_att[:], AX.X, ALU.add))
                for g in range(2):
                    c.mark(dve.tensor_scalar(biasb[:, g, :], zero[:, 0:PN], biasc[:, g:g + 1], None, ALU.add))
                dve.wait_ge(n1_pw, 1)
                c.mark(dve.tensor_copy(wT[:], bank[4][:, 0:128].rearrange("p (g k) -> p g k", g=2)))
                dve.wait_ge(n1_pw, 2)
                c.mark(dve.tensor_copy(ww0[:], bank[5][0:D, 0:WD].rearrange("p (h o) -> p h o", h=4)))
                for g in range(2):
                    for hh in range(2):
                        P = slice(64 * hh, 64 * hh + 64)
                        dve.tensor_copy(wwbd[P, g, hh, :], bank[6][P, g * D:(g + 1) * D])
                c.link(dve.tensor_tensor(cb[:], bpb[:], bank[7][0:PN, 0:D], ALU.add))
                dve.wait_ge(n1_m, 1)
                c.link(dve.tensor_copy(asd[:], bank[2][0:PN, 0:NJ * 8].rearrange("p (j f) -> p j f", j=NJ)))
                c.link(dve.tensor_scalar(st[:, 6, :], cnt[:], 1.0, None, ALU.max))
                c.link(dve.reciprocal(st[:, 7, :], st[:, 6, :]))
                c.link(dve.tensor_tensor(loop_a[:], loop_a[:], st[:, 7, :].unsqueeze(2).to_broadcast([PN, NJ, 4]), ALU.mult))
                dve.tensor_copy(dw[:, :, 0:4], asd[:, :, 4:8]).then_inc(n1_aw, 1)
                dve.tensor_tensor(loop_a[:], loop_a[:], asd[:, :, 0:4], ALU.add).then_inc(n1_aw, 1)
                dve.wait_ge(n1_aw, 2)
                dve.tensor_tensor(loop_a[:], loop_a[:], asd[:, :, 4:8], ALU.add).then_inc(n1_aw, 1)
                dve.wait_ge(n1_aw, 3)
                c.mark(dve.scalar_tensor_tensor(dw[:, :, 4:8], loop_a[:], SLOPE, loop_a[:], ALU.mult, ALU.max))

            @block.scalar
            def _(act):
                ln_std_step(act, n1_var, n1_std, 1)
                transposed_copy_steps(act, n1_t, n1_tc)

            @block.tensor
            def _(pe):
                pe.wait_ge(n1_l, 8 * 16)
                for g in range(2):
                    last = pe.transpose(bank[4][:, g * D:(g + 1) * D], gw[:, g * 128:(g + 1) * 128], ident[0:D, 0:D])
                last.then_inc(n1_pw, 1)
                pe.wait_ge(n1_dve, 17)
                c = Chain(pe, n1_pp)
                for h in range(4):
                    P = slice(64 * (h % 2), 64 * (h % 2) + 64)
                    c.link(pe.matmul(bank[5][0:D, h * D:(h + 1) * D], wT[P, h // 2, :], wp[P, h // 2, :], start=True, stop=True))
                    c.link(pe.matmul(bank[6][P, (h // 2) * D:(h // 2 + 1) * D], wT[P, h // 2, :], wp[P, h // 2, :],
                                     start=True, stop=True))
                for g in range(2):
                    last = pe.matmul(bank[7][0:PN, 0:D], biasb[:, g, :], wp[:, g, :], start=(g == 0), stop=(g == 1))
                last.then_inc(n1_pw, 1)
                transpose_steps(pe, n1_t, n1_tc)
                pe.wait_ge(n1_tc, len(rounds(NJ, 4)))
                for j in range(NJ):
                    last = pe.matmul(bank[2][0:PN, j * 8:(j + 1) * 8], HT[:, j * PN:(j + 1) * PN],
                                     wsd[:].rearrange("k a h -> k (a h)"), start=True, stop=True)
                last.then_inc(n1_m, 1)

        layer.close()

        e1_g = [sem(f"e1_g{k}") for k in range(UG)]
        e1_w = [sem(f"e1_w{k}") for k in range(UG)]
        e1_dl = [sem(f"e1_dl{k}") for k in range(DR)]
        e1_idx, e1_step, e1_one, e1_oT, e1_P, e1_M, e1_Mx, e1_S, e1_acc, e1_z2, e1_sp = [sem("e1_" + x) for x in
            ("idx", "step", "one", "oT", "P", "M", "Mx", "S", "acc", "z2", "sp")]
        S1 = softmax_sems("b1")
        ga = tmp("ga1", [128, UT, D + 4])
        win = tmp("win1", [128, UT, 8])
        one = tmp("one1", [128, UT, 128])
        oneT = tmp("oneT1", [128, 2, GT * W])
        dl = tmp("dl1", [128, DR, GT * W], BF16)
        M1 = tmp("M1", [128, 2, GT, 2, 128])
        D1 = tmp("D1", [128, 2, GT, 128], BF16)
        ob = tmp("ob1", [128, 2, GT * W], BF16)
        with nc.Block() as block:
            @block.gpsimd
            def _(pool):
                gather_program(ga, pool, T1, D + 4, e1_g, e1_M, e1_idx, e1_step)

            @block.sync
            def _(sp):
                def body(i, k):
                    place_load(dl, sp, i, k, e1_dl, e1_oT, e1_sp)
                    window_loads(win, sp, i, k, T1W, 8, e1_w, e1_P, e1_sp)
                each_group(sp, body)

            @block.scalar
            def _(act):
                def weights(i, k):
                    g = i * UG + k
                    s, kk = k // KG, k % KG
                    wait(act, e1_S, (g - 1) * GT)
                    bf16_operands(act, S1, i, k, D1, ob, one, e1_one, e1_Mx)

                def softmax_2(i, s):
                    q = i * 2 + s
                    softmax_act_3(act, S1, q, 4)
                    softmax_act_4(act, S1, q, s, 4, 2)
                    softmax_act_5(act, S1, q, s, bank[1 + s][:, 128:176], 3)

                def body(i, k):
                    if pending(i, k, 0):
                        a, s = pending(i, k, 0)
                        softmax_act_1(act, S1, a * 2 + s, 4)
                    if pending(i, k, 1):
                        softmax_2(*pending(i, k, 1))
                    if back(i, k, LATE - 1):
                        weights(*back(i, k, LATE - 1))
                each_group(act, body)
                softmax_act_1(act, S1, NI * 2 - 1, 4)
                weights(NI - 1, KG - 1)
                softmax_2(NI - 1, 1)
                for k in range(KG, UG):
                    weights(NI - 1, k)

            @block.tensor
            def _(pe):
                def sums(i, k, t):
                    g = i * UG + k
                    if t == 0:
                        pe.wait_ge(e1_M, g + 1)
                        pe.wait_ge(e1_Mx, g * 4 + 4)
                    wait(pe, e1_acc, (g - 1) * 2 * GT + 2 * t + 2)
                    for r in range(2):
                        pe.matmul(bank[4 + t][:, r * 128:(r + 1) * 128], M1[:, k % 2, t, r, :], one[:, k * GT + t, :],
                                  start=True, stop=True)
                    last = pe.matmul(bank[4 + t][:, 256:384], D1[:, k % 2, t, :], ob[:, k % 2, t * W:(t + 1) * W],
                                     start=True, stop=True)
                    last.then_inc(e1_S, 1)

                def all_sums(old, after):
                    for t in range(GT):
                        if old:
                            sums(*old, t)
                        if t in after:
                            after[t]()

                def softmax_1(i, s, old):
                    q = i * 2 + s
                    all_sums(old, {0: lambda: softmax_pe_0(pe, S1, q, 4), 2: lambda: softmax_pe_1(pe, S1, q, 4),
                                   3: lambda: softmax_pe_2(pe, S1, q, 4)})

                def softmax_2(i, s, old):
                    q = i * 2 + s
                    all_sums(old, {0: lambda: softmax_pe_3(pe, S1, q, 4),
                                   2: lambda: softmax_pe_4(pe, S1, q, bank[1 + s][:, 128:176], 4, sel, 3)})

                def body(i, k):
                    g = i * UG + k
                    s, kk = k // KG, k % KG
                    old = back(i, k, LATE)
                    if pending(i, k, 0):
                        softmax_1(*pending(i, k, 0), old)
                    elif pending(i, k, 1):
                        softmax_2(*pending(i, k, 1), old)
                    else:
                        all_sums(old, {})
                    pe.wait_ge(e1_oT, g + 1)
                    pe.wait_ge(e1_w[k], i * 64 + 64)
                    if kk == 0:
                        wait(pe, S1["ex"], i * 4 + (s * 2 - 2))
                    for t in range(GT):
                        o = (kk * GT + t) * 8
                        last = pe.matmul(bank[1 + s][:, o:o + 8], oneT[:, k % 2, t * W:(t + 1) * W], win[:, k * GT + t, 0:8],
                                         start=True, stop=True)
                    last.then_inc(e1_P, 1)
                each_group(pe, body)
                softmax_1(NI - 1, 1, (NI - 1, KG - 2))
                softmax_2(NI - 1, 1, (NI - 1, KG - 1))
                for k in range(KG, UG):
                    all_sums((NI - 1, k), {})

            @block.vector
            def _(dve):
                c = Chain(dve, e1_z2)
                c.mark(dve.memset(D1[:], 0.0))
                c.link(dve.memset(crow[:], -BIG))

                def weighted(i, k):
                    g = i * UG + k
                    s, kk = k // KG, k % KG
                    wait(dve, e1_S, (g - 1) * GT)
                    dve.wait_ge(S1["ex"], (i * 2 + s) * 2 + 2)
                    w = lambda x: ex[:, s, x, 0:64].rearrange("p (h t) -> p t h", h=4)[:, kk * GT:(kk + 1) * GT, :]
                    dve.tensor_tensor(M1[:, k % 2].rearrange("p t r (b c) -> p t (r b) c", b=2),
                                      ga[:, k * GT:(k + 1) * GT, 0:D].unsqueeze(2).to_broadcast([128, GT, 4, D]),
                                      w(0).unsqueeze(3).to_broadcast([128, GT, 4, D]), ALU.mult).then_inc(e1_M, 1)

                def add_sums(i, k, t, b):
                    g = i * UG + k
                    s, kk = k // KG, k % KG
                    wait(dve, e1_acc, g * 2 * GT + 2 * t)
                    a = acc[:, :, bass.ds(b, 1)]
                    dve.tensor_tensor(a, a, fac[:, s, :, kk * GT + t:kk * GT + t + 1], ALU.mult).then_inc(e1_acc, 1)
                    dve.wait_ge(e1_acc, g * 2 * GT + (2 * t + 1))
                    dve.wait_ge(e1_S, g * GT + (t + 1))
                    a = acc[:, :, bass.ds(b, W)]
                    dve.tensor_tensor(a, a, bank[4 + t][:, 0:384].rearrange("p (r n) -> p r n", r=3), ALU.add).then_inc(e1_acc, 1)

                def scores(c, i, s):
                    q = i * 2 + s
                    for kk in range(KG):
                        dve.wait_ge(e1_g[s * KG + kk], i * 64 + 64)
                    dve.wait_ge(e1_P, i * UG + (s + 1) * KG)
                    P = bank[1 + s][:, 0:128].rearrange("p (t f) -> p f t", f=8)
                    v = lambda x: x.rearrange("p (h t) -> p h t", h=4)
                    c.mark(dve.tensor_copy(v(lp[:]), P[:, 4:8, :]))
                    c.link(dve.tensor_tensor(v(al[:, 0, 0:64]), ga[:, s * SG:(s + 1) * SG, D:D + 4].rearrange("p t f -> p f t"),
                                             P[:, 0:4, :], ALU.add))
                    c.link(dve.tensor_tensor(v(al[:, 0, 0:64]), v(al[:, 0, 0:64]),
                                             edge_a[:, bass.ds(i * UT + s * SG, SG), :].rearrange("p t f -> p f t"), ALU.add))
                    c.link(dve.scalar_tensor_tensor(al[:, 0, 0:64], al[:, 0, 0:64], SLOPE, al[:, 0, 0:64], ALU.mult, ALU.max))
                    c.mark(dve.tensor_tensor(am[:, 0:64], al[:, 0, 0:64], lp[:], ALU.max))
                    softmax_dve_0(dve, S1, c, i * UT + s * SG, 4)

                def softmax_1(i, s, old):
                    q = i * 2 + s
                    c = LoopChain(dve, S1["bd"], q, 5 + SOFT)
                    if old:
                        starts = bases_of(dve, *old)
                    scores(c, i, s)
                    if old:
                        add_sums(*old, 0, starts[0])
                    softmax_dve_1(dve, S1, c, q, 4)
                    if old:
                        add_sums(*old, 1, starts[1])
                        add_sums(*old, 2, starts[2])
                    softmax_dve_2(dve, S1, c, q, i * UT + s * SG, 4)
                    if old:
                        add_sums(*old, 3, starts[3])

                def softmax_2(i, s, old):
                    q = i * 2 + s
                    c = LoopChain(dve, S1["bd"], q, 5 + SOFT, 5 + SOFT_1)
                    if old:
                        starts = bases_of(dve, *old)
                    softmax_dve_3(dve, S1, c, q, 4)
                    if old:
                        add_sums(*old, 0, starts[0])
                    m = softmax_dve_4(dve, S1, c, q, 4)
                    dve.tensor_tensor(ex[:, s, 0, 0:64], al[:, 0, 0:64], m, ALU.subtract).then_inc(S1["pen2"], 1)
                    dve.tensor_tensor(ex[:, s, 1, 0:64], lp[:], m, ALU.subtract).then_inc(S1["pen2"], 1)
                    dve.wait_ge(S1["pen2"], q * 2 + 2)
                    dve.sem_inc(S1["sub"], 1)
                    if old:
                        for t in range(1, GT):
                            add_sums(*old, t, starts[t])

                    def fill(c):
                        if c is None:
                            return 2
                        c.mark(dve.tensor_copy(exf[:, 0:64], ex[:, s, 0, 0:64]))
                        c.link(dve.tensor_tensor(exf[:, 64:128].rearrange("p (h t) -> p h t", h=4),
                                                 ex[:, s, 1, 0:64].rearrange("p (h t) -> p h t", h=4),
                                                 first[:, bass.ds(i * UT + s * SG, SG)].unsqueeze(1).to_broadcast([128, 4, SG]),
                                                 ALU.mult))
                    split_steps(dve, S1, q, s, fill)

                def body(i, k):
                    g = i * UG + k
                    wait(dve, e1_P, g - 1)
                    transposed_one_hot_step(oneT[:, k % 2, :], dl, dve, i, k, e1_dl, e1_oT)
                    wait(dve, e1_S, (g - 7) * GT)
                    one_hot_ring_step(one, dve, i, k, e1_one)
                    old = back(i, k, LATE)
                    if pending(i, k, 0):
                        softmax_1(*pending(i, k, 0), old)
                    elif pending(i, k, 1):
                        softmax_2(*pending(i, k, 1), old)
                    elif old:
                        starts = bases_of(dve, *old)
                        for t in range(GT):
                            add_sums(*old, t, starts[t])
                    if back(i, k, LATE - 1):
                        weighted(*back(i, k, LATE - 1))
                each_group(dve, body)
                softmax_1(NI - 1, 1, (NI - 1, KG - 2))
                weighted(NI - 1, KG - 1)
                softmax_2(NI - 1, 1, (NI - 1, KG - 1))
                weighted(NI - 1, KG)
                for k in range(KG, UG):
                    starts = bases_of(dve, NI - 1, k)
                    if k + 1 < UG:
                        weighted(NI - 1, k + 1)
                    for t in range(GT):
                        add_sums(NI - 1, k, t, starts[t])

        layer.close()
        den = tmp("den", [PN, NJ, 8])
        yl = tmp("yl", [PN, 2, 4, D])
        m1_d, m1_dve, m1_m, m1_act = [sem("m1_" + x) for x in ("d", "dve", "m", "act")]
        m1_var, m1_std = sem("m1_var"), sem("m1_std")
        XC, yn, tab = node_buffers("m1")
        with nc.Block() as block:
            @block.tensor
            def _(pe):
                for j in range(NJ):
                    last = pe.matmul(bank[0][0:PN, j * 8:(j + 1) * 8], acc[0:24, 2, j * PN:(j + 1) * PN], parts8[:], start=True, stop=True)
                last.then_inc(m1_d, 1)
                for j in range(NJ):
                    if j >= 2:
                        pe.wait_ge(m1_dve, 5 + 4 * (j - 1))
                    b = bank[1 + j % 2]
                    for g in range(2):
                        pe.matmul(b[0:PN, g * 128:(g + 1) * 128], acc[:, g, j * PN:(j + 1) * PN],
                                  wwbd[:, g].rearrange("p a o -> p (a o)"), start=True, stop=True)
                    pe.matmul(b[0:PN, 256:512], HT[:, j * PN:(j + 1) * PN], ww0[:].rearrange("p h o -> p (h o)"),
                              start=True, stop=True).then_inc(m1_m, 1)

            @block.vector
            def _(dve):
                c = Chain(dve, m1_dve)
                dve.wait_ge(m1_d, 1)
                c.link(dve.tensor_copy(den[:], bank[0][0:PN, 0:NJ * 8].rearrange("p (j f) -> p j f", j=NJ)))
                c.link(dve.tensor_scalar(st[:, 6, :], cnt[:], 0.0, None, ALU.is_equal))
                c.link(dve.tensor_tensor(den[:, :, 4:8], den[:, :, 4:8], st[:, 6, :].unsqueeze(2).to_broadcast([PN, NJ, 4]), ALU.add))
                c.link(dve.tensor_tensor(den[:, :, 0:4], den[:, :, 0:4], den[:, :, 4:8], ALU.add))
                c.link(dve.reciprocal(den[:, :, 0:4], den[:, :, 0:4]))
                for j in range(NJ):
                    dve.wait_ge(m1_m, j + 1)
                    b = bank[1 + j % 2]
                    y = yl[:, j % 2]
                    wl = den[:, j, 4:8].unsqueeze(2).to_broadcast([PN, 4, D])
                    rd = den[:, j, 0:4].unsqueeze(2).to_broadcast([PN, 4, D])
                    c.link(dve.tensor_tensor(y, b[0:PN, 256:512].rearrange("p (h o) -> p h o", h=4), wl, ALU.mult))
                    c.link(dve.tensor_tensor(y, b[0:PN, 0:256].rearrange("p (h o) -> p h o", h=4), y, ALU.add))
                    c.link(dve.tensor_tensor(y, y, rd, ALU.mult))
                    c.mark(dve.tensor_reduce(XC[:, j, :], y.rearrange("p h o -> p o h"), AX.X, ALU.add))
                dve.wait_ge(m1_dve, c.n)
                bc = lambda v: v[:].unsqueeze(1).to_broadcast([PN, NJ, D])
                c.link(dve.tensor_tensor(XC[:], XC[:], bc(cb), ALU.add))
                c.link(dve.tensor_scalar(tab[:, :, 0:D], XC[:], 0.0, None, ALU.min))
                m1_min = c.n
                c.link(dve.tensor_scalar(XC[:], XC[:], 0.0, -1.0, ALU.max, ALU.add))
                s_done["m1_min"] = m1_min
                c.link(dve.tensor_tensor(H[:], H[:], XC[:], ALU.add))
                dve.wait_ge(m1_act, 1)
                c.link(dve.tensor_tensor(H[:], H[:], tab[:, :, D:2 * D], ALU.add))
                ln_relu_steps(c, m1_var, m1_std, 1, dst=yn, src=H, relu=False, XC=XC)
                c.link(dve.tensor_tensor(yn[:], yn[:], bc(gamma), ALU.mult))
                c.link(dve.tensor_tensor(yn[:], yn[:], bc(beta), ALU.add))
                c.link(dve.tensor_tensor(X[:], X[:], yn[:], ALU.add))

            @block.scalar
            def _(act):
                act.wait_ge(m1_dve, 5 + 4 * NJ + 2)
                act.activation(tab[:, :, D:2 * D], tab[:, :, 0:D], ACT.Exp).then_inc(m1_act, 1)
                ln_std_step(act, m1_var, m1_std, 1)
        end_of_layer()
        if finish("L1"):
            return

        w2t = sb("w2t", [D, D])
        b2b = sb("b2b", [PN, D])
        dis = sb("dis", [PN, NJ])
        F = 128
        w1kv = sb("w1kv", [D, F])
        b1kv = sb("b1kv", [F, 1])
        w2v = sb("w2v", [F, F])
        w2k = sb("w2k", [F, F])
        b2v = sb("b2v", [128, F])
        b2k = sb("b2k", [F, 1])
        T2 = dram("T2", [N, D])
        WK = dram("WK", [F, EP])
        WV = dram("WV", [W, NT * F])
        n2_l, n2_z, n2_dve, n2_var, n2_std, n2_deg, n2_t, n2_tc, n2_o = [sem("n2_" + x) for x in
            ("l", "z", "dve", "var", "std", "deg", "t", "tc", "o")]
        XC, yn, tab = node_buffers("n2")
        with nc.Block() as block:
            @block.gpsimd
            def _(pool):
                pool.memset(w2v[:], 0.0).then_inc(n2_z, 1)
                pool.memset(w2k[:], 0.0).then_inc(n2_z, 1)

            @block.vector
            def _(dve):
                c = Chain(dve, n2_dve)
                c.link(dve.tensor_scalar(st[:, 6, :], cnt[:], 1.0, None, ALU.add))
                dve.wait_ge(n2_deg, 1)
                c.link(dve.reciprocal(dis[:], st[:, 7, :]))
                c.mark(dve.memset(acc[:], 0.0))
                ln_relu_steps(c, n2_var, n2_std, 1, XC=XC)
                c.mark(dve.tensor_tensor(yn[:], H[:], dis[:].unsqueeze(2).to_broadcast([PN, NJ, D]), ALU.mult))

            @block.scalar
            def _(act):
                act.wait_ge(n2_dve, 1)
                act.activation(st[:, 7, :], st[:, 6, :], ACT.Sqrt).then_inc(n2_deg, 1)
                ln_std_step(act, n2_var, n2_std, 1)
                transposed_copy_steps(act, n2_t, n2_tc)

            @block.tensor
            def _(pe):
                pe.wait_ge(n2_dve, 12)
                transpose_steps(pe, n2_t, n2_tc, src=yn)

            @block.sync
            def _(sp):
                sp.dma_start(w2t[:], A["L2_gnn_WT"]).then_inc(n2_l, 16)
                sp.dma_start(b2b[:], A["L2_gnn_b"].partition_broadcast(PN)).then_inc(n2_l, 16)
                L = lambda o, i: sp.dma_start(o, i).then_inc(n2_l, 16)
                L(w1kv[:, 0:D], A["L3_gnn_v_w1"])
                L(w1kv[:, D:F], A["L3_gnn_k_w1"])
                sp.wait_ge(n2_z, 2)
                L(w2v[0:D, :], A["L3_gnn_v_w2"])
                L(w2k[D:F, :], A["L3_gnn_k_w2"])
                L(b2v[:], A["L3_gnn_v_b2"].partition_broadcast(128))
                with nc.allow_non_contiguous_dma(reason="biases as columns"):
                    L(b1kv[0:D, :], A["L3_gnn_v_b1"].rearrange("a f -> f a"))
                    L(b1kv[D:F, :], A["L3_gnn_k_b1"].rearrange("a f -> f a"))
                    L(b2k[:], A["L3_gnn_k_b2"].rearrange("a f -> f a"))
                sp.wait_ge(n2_dve, 12)
                sp.dma_start(T2.rearrange("(j p) f -> p j f", p=PN), yn[:]).then_inc(n2_o, 16)
                sp.wait_ge(n2_o, 16)
                sp.wait_ge(n2_l, 10 * 16)
        layer.close()

        e2_g = [sem(f"e2_g{k}") for k in range(UG)]
        e2_e = [sem(f"e2_e{k}") for k in range(2)]
        e2_o = [sem(f"e2_o{k}") for k in range(2)]
        e2_idx, e2_step, e2_one, e2_S, e2_acc, e2_H, e2_h, e2_W, e2_w, e2_v, e2_sp = [sem("e2_" + x) for x in
            ("idx", "step", "one", "S", "acc", "H", "h", "W", "w", "v", "sp")]
        ga = tmp("ga2", [128, UT, D])
        one = tmp("one2", [128, UT, 128])
        ef = tmp("ef", [D, 2, GT * W])
        hid = tmp("hid", [F, 2, GT * W])
        wko = tmp("wko", [128, 2, GT * W])
        wvo = tmp("wvo", [128, 2, GT * W])
        with nc.Block() as block:
            @block.gpsimd
            def _(pool):
                gather_program(ga, pool, T2, D, e2_g, e2_S, e2_idx, e2_step)

            @block.sync
            def _(sp):
                def store(i, k):
                    g = i * UG + k
                    cols = bass.ds(g * GT * W, GT * W)
                    sp.wait_ge(e2_w, g + 1)
                    sp.sem_inc(e2_sp, 1)
                    sp.dma_start(WK[:, cols], wko[:, k % 2, :]).then_inc(e2_o[k % 2], 16)
                    sp.wait_ge(e2_v, g + 1)
                    sp.sem_inc(e2_sp, 1)
                    sp.dma_start(WV[:, cols], wvo[:, k % 2, :]).then_inc(e2_o[k % 2], 16)

                def body(i, k):
                    g = i * UG + k
                    wait(sp, e2_H, g - 1)
                    sp.sem_inc(e2_sp, 1)
                    sp.dma_start(ef[:, k % 2, :], A["ea64"][:, bass.ds(g * GT * W, GT * W)]).then_inc(e2_e[k % 2], 16)
                    if back(i, k, 2):
                        store(*back(i, k, 2))
                each_group(sp, body)
                store(NI - 1, UG - 2)
                store(NI - 1, UG - 1)
                for slot in range(2):
                    sp.wait_ge(e2_o[slot], NI * UG // 2 * 32)

            @block.tensor
            def _(pe):
                def networks(i, k):
                    g = i * UG + k
                    pe.wait_ge(e2_h, g + 1)
                    wait(pe, e2_w, g - 1)
                    wait(pe, e2_v, g - 1)
                    pe.matmul(bank[4 + k % 2][:], w2k[:], hid[:, k % 2, :], start=True, stop=True)
                    for t in range(GT):
                        last = pe.matmul(bank[6 + k % 2][:, t * 128:(t + 1) * 128], hid[:, k % 2, t * 128:(t + 1) * 128], w2v[:],
                                         start=True, stop=True)
                    last.then_inc(e2_W, 1)

                def body(i, k):
                    g = i * UG + k
                    pe.wait_ge(e2_e[k % 2], i * (UG // 2 * 16) + (k // 2 + 1) * 16)
                    wait(pe, e2_h, g - 1)
                    pe.matmul(bank[2 + k % 2][:], w1kv[:], ef[:, k % 2, :], start=True, stop=True).then_inc(e2_H, 1)
                    if before(i, k):
                        networks(*before(i, k))
                    pe.wait_ge(e2_one, g + 1)
                    pe.wait_ge(e2_g[k], i * 64 + 64)
                    wait(pe, e2_acc, (g - 1) * GT)
                    for t in range(GT):
                        last = pe.matmul(bank[k % 2][0:D, t * 128:(t + 1) * 128], ga[:, k * GT + t, :], one[:, k * GT + t, :],
                                         start=True, stop=True)
                    last.then_inc(e2_S, 1)
                each_group(pe, body)
                networks(NI - 1, UG - 1)

            @block.scalar
            def _(act):
                def outputs(i, k):
                    g = i * UG + k
                    act.wait_ge(e2_W, g + 1)
                    if back(i, k, 2):
                        act.wait_ge(e2_o[k % 2], i * (UG // 2 * 32) + (k // 2) * 32)
                    act.activation(wko[:, k % 2, :], bank[4 + k % 2][:], ACT.Identity, bias=b2k[:, 0:1]).then_inc(e2_w, 1)

                def body(i, k):
                    g = i * UG + k
                    act.wait_ge(e2_H, g + 1)
                    wait(act, e2_W, g - 1)
                    act.activation(hid[:, k % 2, :], bank[2 + k % 2][:], ACT.Relu, bias=b1kv[:, 0:1]).then_inc(e2_h, 1)
                    if before(i, k):
                        outputs(*before(i, k))
                each_group(act, body)
                outputs(NI - 1, UG - 1)

            @block.vector
            def _(dve):
                def with_bias(i, k):
                    g = i * UG + k
                    dve.wait_ge(e2_W, g + 1)
                    if back(i, k, 2):
                        dve.wait_ge(e2_o[k % 2], i * (UG // 2 * 32) + (k // 2) * 32)
                    dve.tensor_tensor(wvo[:, k % 2, :].rearrange("p (t f) -> p t f", t=GT),
                                      bank[6 + k % 2][:].rearrange("p (t f) -> p t f", t=GT),
                                      b2v[:].unsqueeze(1).to_broadcast([128, GT, F]), ALU.add).then_inc(e2_v, 1)

                def add_sums(i, k):
                    g = i * UG + k
                    starts = bases_of(dve, i, k)
                    dve.wait_ge(e2_S, g + 1)
                    for t, b in enumerate(starts):
                        wait(dve, e2_acc, g * GT + t)
                        a = acc[0:D, 0, bass.ds(b, W)]
                        dve.tensor_tensor(a, a, bank[k % 2][0:D, t * 128:(t + 1) * 128], ALU.add).then_inc(e2_acc, 1)

                def body(i, k):
                    g = i * UG + k
                    wait(dve, e2_S, g - 7)
                    one_hot_ring_step(one, dve, i, k, e2_one)
                    if before(i, k):
                        add_sums(*before(i, k))
                        with_bias(*before(i, k))
                each_group(dve, body)
                add_sums(NI - 1, UG - 1)
                with_bias(NI - 1, UG - 1)
        layer.close()

        m2_m, m2_dve = sem("m2_m"), sem("m2_dve")
        XC, yn, tab = node_buffers("m2")
        with nc.Block() as block:
            @block.tensor
            def _(pe):
                for r, (j0, n) in enumerate(rounds(NJ, 4)):
                    if r >= 2:
                        pe.wait_ge(m2_dve, r - 1)
                    for j in range(n):
                        cols = slice((j0 + j) * PN, (j0 + j + 1) * PN)
                        o = bank[r % 2][0:PN, j * D:(j + 1) * D]
                        pe.matmul(o, acc[0:D, 0, cols], w2t[:], start=True, stop=False)
                        last = pe.matmul(o, HT[:, cols], w2t[:], start=False, stop=True)
                    last.then_inc(m2_m, 1)

            @block.vector
            def _(dve):
                c = Chain(dve, m2_dve)
                for r, (j0, n) in enumerate(rounds(NJ, 4)):
                    dve.wait_ge(m2_m, r + 1)
                    c.mark(dve.tensor_tensor(yn[:, j0:j0 + n, :], bank[r % 2][0:PN, 0:n * D].rearrange("p (j f) -> p j f", j=n),
                                             dis[:, j0:j0 + n].unsqueeze(2).to_broadcast([PN, n, D]), ALU.mult))
                dve.wait_ge(m2_dve, c.n)
                c.link(dve.tensor_tensor(yn[:], yn[:], b2b[:].unsqueeze(1).to_broadcast([PN, NJ, D]), ALU.add))
                c.link(dve.scalar_tensor_tensor(X[:], yn[:], 0.0, X[:], ALU.max, ALU.add))
        end_of_layer()
        if finish("L2"):
            return

        NS = 9
        NZ = 5
        wq = sb("wq", [D, F])
        ck = sb("ck", [128, NZ, F])
        cv = sb("cv", [128, NZ, F])
        w_out = sb("w_out", [F, D])
        w_self = sb("w_self", [D, D])
        gcol = sb("gcol", [D, 1])
        bcol = sb("bcol", [D, 1])
        shsel = sb("shsel", [3 * NS, NZ, 128], BF16)
        sel_b = sb("sel_b", [24, 128])
        XX = dram("XX", [N, 2 * D])
        QW = dram("QW", [NW, F])
        SH = dram("SH", [3, NS * EP], BF16)
        n3_l, n3_s, n3_sd, n3_p, n3_dve, n3_var, n3_std, n3_t, n3_tc, n3_q, n3_qc, n3_o, n3_c = [sem("n3_" + x) for x in
            ("l", "s", "sd", "p", "dve", "var", "std", "t", "tc", "q", "qc", "o", "c")]
        NL3 = 9
        SF = NS * EP // 128
        XC, yn, tab = node_buffers("n3")
        shf = tmp("shf", [128, SF])
        shp = tmp("shp", [128, 3, SF], BF16)
        shsel_f = tmp("shsel_f", [3 * NS, NZ, 128])
        with nc.Block() as block:
            @block.sync
            def _(sp):
                sp.dma_start(shf[:], A["ea9"].rearrange("s (a f) -> (s a) f", a=1).rearrange("s f -> (s f)")
                             .rearrange("(p f) -> p f", p=128)).then_inc(n3_s, 16)
                L = lambda o, i: sp.dma_start(o, i).then_inc(n3_l, 16)
                L(wq[:], A["L3_gnn_Wq"])
                L(w_out[:], A["L3_gnn_W_out"])
                L(w_self[:], A["L3_gnn_W_self"])
                with nc.allow_non_contiguous_dma(reason="biases as columns"):
                    L(gcol[:], A["L3_gnn_gamma"].rearrange("a f -> f a"))
                    L(bcol[:], A["L3_gnn_beta"].rearrange("a f -> f a"))
                for m, w in ((ck, "Cqk"), (cv, "Cv")):
                    L(m[0:D, :, :], A["L3_gnn_" + w][:, 0:NS:2, :])
                    L(m[D:128, 0:NZ - 1, :], A["L3_gnn_" + w][:, 1:NS:2, :])
                for part in range(3):
                    sp.wait_ge(n3_sd, 2 * part + 1)
                    sp.dma_start(SH[part].rearrange("(p f) -> p f", p=128), shp[:, part, :]).then_inc(n3_o, 16)
                sp.dma_start(QW[N:NW, :], zero[:, 0:F]).then_inc(n3_o, 16)
                sp.wait_ge(n3_dve, 9)
                for a in range(2):
                    sp.dma_start(XX.rearrange("(j p) f -> p j f", p=PN)[:, :, a * D:(a + 1) * D], H[:]).then_inc(n3_o, 16)
                sp.wait_ge(n3_qc, len(rounds(NJ, 4)))
                sp.dma_start(QW[0:N, :].rearrange("(j p) f -> p j f", p=PN), tab[:]).then_inc(n3_o, 16)
                sp.wait_ge(n3_o, 7 * 16)
                sp.wait_ge(n3_l, NL3 * 16)

            @block.gpsimd
            def _(pool):
                pool.memset(shsel_f[:], 0.0).then_inc(n3_p, 1)
                n = 1
                for part in range(3):
                    pool.wait_ge(n3_p, n)
                    pool.affine_select(out=shsel_f[:].rearrange("p j (a c) -> p j a c", a=2),
                                       in_=shsel_f[:].rearrange("p j (a c) -> p j a c", a=2),
                                       compare_op=ALU.not_equal, fill=1.0, base=-NS * part,
                                       pattern=[[-2, NZ], [-1, 2], [0, D]], channel_multiplier=1).then_inc(n3_p, 1)
                    n += 1
                pool.memset(sel_b[0:8, :], 1.0).then_inc(n3_p, 1)
                n += 1
                pool.wait_ge(n3_p, n)
                pool.affine_select(out=sel_b[0:8, :], in_=sel_b[0:8, :], compare_op=ALU.is_ge, fill=0.0, base=0,
                                   pattern=[[1, 128]], channel_multiplier=-16).then_inc(n3_p, 1)
                n += 1
                pool.wait_ge(n3_p, n)
                pool.affine_select(out=sel_b[0:8, :], in_=sel_b[0:8, :], compare_op=ALU.is_ge, fill=0.0, base=15,
                                   pattern=[[-1, 128]], channel_multiplier=16).then_inc(n3_p, 1)

            @block.vector
            def _(dve):
                c = Chain(dve, n3_dve)
                ln_relu_steps(c, n3_var, n3_std, 1, XC=XC)
                c.mark(dve.memset(acc[:, 0:2, :], 0.0))
                s = Chain(dve, n3_sd)
                dve.wait_ge(n3_s, 16)
                s.link(dve.tensor_copy(shp[:, 0, :], shf[:]))
                for part in range(1, 3):
                    s.link(dve.tensor_tensor(shf[:], shf[:], shp[:, part - 1, :], ALU.subtract))
                    s.link(dve.tensor_copy(shp[:, part, :], shf[:]))
                dve.wait_ge(n3_p, 4)
                dve.tensor_copy(shsel[:], shsel_f[:]).then_inc(n3_c, 1)

            @block.scalar
            def _(act):
                ln_std_step(act, n3_var, n3_std, 1)
                transposed_copy_steps(act, n3_t, n3_tc)
                for r, (j0, n) in enumerate(rounds(NJ, 4)):
                    act.wait_ge(n3_q, r + 1)
                    act.activation(tab[:, j0:j0 + n, :], bank[2 + r % 2][0:PN, 0:n * 128].rearrange("p (j f) -> p j f", j=n),
                                   ACT.Copy).then_inc(n3_qc, 1)

            @block.tensor
            def _(pe):
                pe.wait_ge(n3_dve, 8)
                transpose_steps(pe, n3_t, n3_tc)
                pe.wait_ge(n3_l, NL3 * 16)
                for r, (j0, n) in enumerate(rounds(NJ, 4)):
                    pe.wait_ge(n3_tc, r + 1)
                    if r >= 2:
                        pe.wait_ge(n3_qc, r - 1)
                    for j in range(n):
                        last = pe.matmul(bank[2 + r % 2][0:PN, j * 128:(j + 1) * 128], HT[:, (j0 + j) * PN:(j0 + j + 1) * PN],
                                         wq[:], start=True, stop=True)
                    last.then_inc(n3_q, 1)
        layer.close()

        e3_g = [sem(f"e3_g{k}") for k in range(UG)]
        WR = 2
        e3_w = [sem(f"e3_w{k}") for k in range(WR)]
        e3_e = [sem(f"e3_e{k}") for k in range(2)]
        e3_n = [sem(f"e3_n{k}") for k in range(2)]
        e3_dl = [sem(f"e3_dl{k}") for k in range(2)]
        (e3_idx, e3_step, e3_one, e3_oT, e3_X, e3_xT, e3_sh, e3_z, e3_Q, e3_q, e3_K, e3_kt, e3_pr,
         e3_V, e3_vw, e3_P, e3_S, e3_acc, e3_M, e3_Mx, e3_i, e3_sp) = [sem("e3_" + x) for x in
            ("idx", "step", "one", "oT", "X", "xT", "sh", "z", "Q", "q", "K", "kt", "pr",
             "V", "vw", "P", "S", "acc", "M", "Mx", "i", "sp")]
        S3 = softmax_sems("b3")
        GR = 4
        ga = tmp("ga3", [128, GR * GT, F])
        win = tmp("win3", [128, WR * GT, F])
        one = tmp("one3", [128, UT, 128])
        oneT = acc[:, 2, 0 * 512:1 * 512]
        xT = acc[:, 2, 1 * 512:2 * 512]
        dl = tmp("dl3", [128, 2, GT * W], BF16)
        wks = tmp("wks", [128, 2, GT * W])
        shl = tmp("shl", [3 * NS, 2, GT * W], BF16)
        spare = edge_a[:].rearrange("p t h -> p (t h)")
        wvs = spare[:, 0:2 * GT * W].rearrange("p (a e) -> p a e", a=2)
        z = tmp("z", [128, 2, NZ, GT * W])
        qs = acc[:, 2, 2 * 512:3 * 512]
        kt = acc[:, 2, 4 * 512:5 * 512]
        vw = tmp("vw", [128, UT, F])
        M3 = tmp("M3", [128, 2, GT, F])
        D3 = tmp("D3", [128, 2, GT, 128], BF16)
        ob = tmp("ob3", [128, 2, GT * W], BF16)
        hsel = tmp("hsel", [128, 8])
        with nc.Block() as block:
            @block.gpsimd
            def _(pool):
                gather_program(ga, pool, XX, F, e3_g, e3_X, e3_idx, e3_step, ring=GR)

            @block.sync
            def _(sp):
                def body(i, k):
                    g = i * UG + k
                    cols = bass.ds(g * GT * W, GT * W)
                    wait(sp, e3_oT, g - 1)
                    sp.sem_inc(e3_sp, 1)
                    sp.dma_start(dl[:, k % 2, :], DL[:, cols].partition_broadcast(128)).then_inc(e3_dl[k % 2], 16)
                    wait(sp, e3_sh, (g - 1) * NZ)
                    sp.sem_inc(e3_sp, 1)
                    for part in range(3):
                        sp.dma_start(shl[part * NS:(part + 1) * NS, k % 2, :],
                                     SH[part].rearrange("(s e) -> s e", s=NS)[:, cols]).then_inc(e3_e[k % 2], 16)
                    window_loads(win, sp, i, k, QW, F, e3_w, e3_Q, e3_sp, ring=WR)
                    wait(sp, e3_vw, g - 1)
                    sp.sem_inc(e3_sp, 1)
                    sp.dma_start(wks[:, k % 2, :], WK[:, cols]).then_inc(e3_n[k % 2], 16)
                    sp.dma_start(wvs[:, k % 2, :], WV[:, cols]).then_inc(e3_n[k % 2], 16)
                each_group(sp, body)

            @block.scalar
            def _(act):
                def weights(i, k):
                    g = i * UG + k
                    s, kk = k // KG, k % KG
                    wait(act, e3_S, (g - 1) * 2)
                    bf16_operands(act, S3, i, k, D3, ob, one, e3_one, e3_Mx)

                def softmax_2(i, s):
                    q = i * 2 + s
                    softmax_act_3(act, S3, q, 8)
                    softmax_act_4(act, S3, q, s, 8, 1)
                    softmax_act_5(act, S3, q, s, bank[4][:, 128:160], 2)

                def body(i, k):
                    g = i * UG + k
                    act.wait_ge(e3_X, g + 1)
                    wait(act, e3_z, g * NZ)
                    act.activation(xT[:], bank[0][:], ACT.Copy).then_inc(e3_xT, 1)
                    if pending(i, k, 0):
                        a, s = pending(i, k, 0)
                        softmax_act_1(act, S3, a * 2 + s, 8)
                    act.wait_ge(e3_Q, g + 1)
                    wait(act, e3_pr, g)
                    act.activation(qs[:], bank[7][:], ACT.Copy).then_inc(e3_q, 1)
                    if pending(i, k, 1):
                        softmax_2(*pending(i, k, 1))
                    if back(i, k, LATE - 1):
                        weights(*back(i, k, LATE - 1))
                act.wait_ge(e3_i, 3)
                each_group(act, body)
                weights(NI - 1, KG - 1)
                softmax_act_1(act, S3, NI * 2 - 1, 8)
                softmax_2(NI - 1, 1)
                for k in range(KG, UG):
                    weights(NI - 1, k)

            @block.tensor
            def _(pe):
                def sums(i, k, half):
                    g = i * UG + k
                    if half == 0:
                        pe.wait_ge(e3_M, g + 1)
                        pe.wait_ge(e3_Mx, g * 4 + 4)
                    for t in range(2 * half, 2 * half + 2):
                        o = (t % 2) * 256
                        pe.matmul(bank[7 - half][:, o:o + 128], M3[:, k % 2, t, :], one[:, k * GT + t, :], start=True, stop=True)
                        last = pe.matmul(bank[7 - half][:, o + 128:o + 256], D3[:, k % 2, t, :], ob[:, k % 2, t * W:(t + 1) * W],
                                         start=True, stop=True)
                    last.then_inc(e3_S, 1)

                def harmonics(i, k, j):
                    u = (i * UG + k) * NZ + j
                    m = 128 if j < NZ - 1 else D
                    wait(pe, e3_z, u - 1)
                    pe.matmul(bank[1 + (k * NZ + j) % 2][0:m, :], shsel[:, j, 0:m], shl[:, k % 2, :], start=True, stop=True)\
                      .then_inc(e3_sh, 1)

                def body(i, k):
                    g = i * UG + k
                    s, kk = k // KG, k % KG
                    old = back(i, k, LATE)
                    p1, p2 = pending(i, k, 0), pending(i, k, 1)
                    if p1 or p2:
                        a, b = p1 or p2
                        q = a * 2 + b
                    pe.wait_ge(e3_g[k], i * 64 + 64)
                    wait(pe, e3_xT, g)
                    for t in range(GT):
                        last = pe.transpose(bank[0][:, t * 128:(t + 1) * 128], ga[:, (k % GR) * GT + t, :], ident[:])
                    last.then_inc(e3_X, 1)
                    wait(pe, e3_q, g)
                    if old:
                        sums(*old, 0)
                    pe.wait_ge(e3_e[k % 2], i * (UG // 2 * 48) + (k // 2 + 1) * 48)
                    for j in range(2):
                        harmonics(i, k, j)
                    if p1:
                        softmax_pe_0(pe, S3, q, 8)
                    wait(pe, e3_vw, g)
                    if old:
                        sums(*old, 1)
                    wait(pe, e3_kt, g)
                    for j in range(NZ):
                        if j == 2:
                            if old:
                                pe.wait_ge(e3_acc, (old[0] * UG + old[1]) * 8 + 4)
                            pe.wait_ge(e3_w[k % WR], i * (UG // WR * 64) + (k // WR + 1) * 64)
                            pe.wait_ge(e3_oT, g + 1)
                            for t in range(GT):
                                last = pe.matmul(bank[7][:, t * 128:(t + 1) * 128], win[:, (k % WR) * GT + t, :],
                                                 oneT[:, t * 128:(t + 1) * 128], start=True, stop=True)
                            last.then_inc(e3_Q, 1)
                        m = 128 if j < NZ - 1 else D
                        pe.wait_ge(e3_z, g * NZ + (j + 1))
                        last = pe.matmul(bank[5][:], ck[0:m, j, :], z[0:m, k % 2, j, :], start=(j == 0), stop=(j == NZ - 1))
                        if j + 2 < NZ:
                            harmonics(i, k, j + 2)
                        if j == NZ - 1:
                            last.then_inc(e3_K, 1)
                        if p1 and j == 2:
                            softmax_pe_1(pe, S3, q, 8)
                        if p2 and j == 3:
                            softmax_pe_3(pe, S3, q, 8)
                    if old:
                        pe.wait_ge(e3_acc, (old[0] * UG + old[1]) * 8 + 8)
                    else:
                        wait(pe, e3_vw, g)
                    for t in range(GT):
                        for j in range(NZ):
                            m = 128 if j < NZ - 1 else D
                            last = pe.matmul(bank[6][:, t * 128:(t + 1) * 128], z[0:m, k % 2, j, t * 128:(t + 1) * 128], cv[0:m, j, :],
                                             start=(j == 0), stop=(j == NZ - 1))
                        if t == GT - 1:
                            last.then_inc(e3_V, 1)
                        if p1 and t == 2:
                            softmax_pe_2(pe, S3, q, 8)
                        if p2 and t == 2:
                            softmax_pe_4(pe, S3, q, bank[4][:, 128:160], 8, sel8, 2)
                    pe.wait_ge(e3_pr, g + 1)
                    if kk == 1:
                        wait(pe, S3["ex"], i * 4 + s * 2)
                    for t in range(GT):
                        o = (kk * GT + t) * 8
                        last = pe.matmul(bank[4][:, o:o + 8], kt[:, t * 128:(t + 1) * 128], hsel[:], start=True, stop=True)
                    last.then_inc(e3_P, 1)
                each_group(pe, body)
                for k in range(UG - LATE, KG):
                    if k > UG - LATE:
                        pe.wait_ge(e3_acc, ((NI - 1) * UG + k) * 8)
                    sums(NI - 1, k, 0)
                    pe.wait_ge(e3_vw, NI * UG)
                    sums(NI - 1, k, 1)
                q = NI * 2 - 1
                softmax_pe_0(pe, S3, q, 8)
                softmax_pe_1(pe, S3, q, 8)
                softmax_pe_2(pe, S3, q, 8)
                softmax_pe_3(pe, S3, q, 8)
                softmax_pe_4(pe, S3, q, bank[4][:, 128:160], 8, sel8, 2)
                for k in range(KG, UG):
                    pe.wait_ge(e3_acc, ((NI - 1) * UG + k) * 8)
                    sums(NI - 1, k, 0)
                    sums(NI - 1, k, 1)

            @block.vector
            def _(dve):
                dve.memset(D3[:], 0.0).then_inc(e3_i, 1)
                dve.memset(crow[:], -BIG).then_inc(e3_i, 1)
                dve.tensor_reduce(hsel[:], ident[:].rearrange("p (h c) -> p h c", h=8), AX.X, ALU.add).then_inc(e3_i, 1)
                dve.wait_ge(e3_i, 3)

                def values(i, k):
                    g = i * UG + k
                    s, kk = k // KG, k % KG
                    wait(dve, e3_S, (g - 1) * 2)
                    dve.wait_ge(S3["ex"], (i * 2 + s) * 2 + 1)
                    w = ex[:, s, 0, :].rearrange("p (h t) -> p t h", h=8)[:, kk * GT:(kk + 1) * GT, :]
                    dve.tensor_tensor(M3[:, k % 2].rearrange("p t (h c) -> p t h c", h=8),
                                      vw[:, k * GT:(k + 1) * GT, :].rearrange("p t (h c) -> p t h c", h=8),
                                      w.unsqueeze(3).to_broadcast([128, GT, 8, 16]), ALU.mult).then_inc(e3_M, 1)

                def add_sums(i, k, half, starts):
                    g = i * UG + k
                    s, kk = k // KG, k % KG
                    dve.wait_ge(S3["ex"], (i * 2 + s) * 2 + 2)
                    for t in range(2 * half, 2 * half + 2):
                        b = starts[t]
                        wait(dve, e3_acc, g * 8 + 2 * t)
                        a = acc[:, 0:2, bass.ds(b, 1)]
                        dve.tensor_tensor(a, a, fac[:, s, 0:2, kk * GT + t:kk * GT + t + 1], ALU.mult).then_inc(e3_acc, 1)
                        dve.wait_ge(e3_acc, g * 8 + (2 * t + 1))
                        if t == 2 * half:
                            dve.wait_ge(e3_S, g * 2 + (half + 1))
                        a = acc[:, 0:2, bass.ds(b, W)]
                        dve.tensor_tensor(a, a, bank[7 - half][:, (t % 2) * 256:(t % 2 + 1) * 256].rearrange("p (r n) -> p r n", r=2),
                                          ALU.add).then_inc(e3_acc, 1)

                def scores(c, q, s):
                    dve.wait_ge(e3_P, (q + 1) * KG)
                    c.link(dve.tensor_copy(am[:].rearrange("p (h t) -> p h t", h=8),
                                           bank[4][:, 0:128].rearrange("p (t h) -> p h t", h=8)))

                def exponents(c, q, s):
                    m = softmax_dve_4(dve, S3, c, q, 8)
                    dve.tensor_tensor(ex[:, s, 0, :], am[:], m, ALU.subtract).then_inc(S3["pen"], 1)
                    dve.wait_ge(S3["pen"], q + 1)
                    dve.sem_inc(S3["sub"], 1)

                def fill(c, s):
                    if c is None:
                        return 1
                    c.link(dve.tensor_copy(exf[:], ex[:, s, 0, :]))

                def body(i, k):
                    g = i * UG + k
                    old = back(i, k, LATE)
                    p1, p2 = pending(i, k, 0), pending(i, k, 1)
                    wait(dve, e3_Q, g)
                    dve.wait_ge(e3_dl[k % 2], i * (UG // 2 * 16) + (k // 2 + 1) * 16)
                    dve.tensor_scalar(oneT[:], dl[:, k % 2, :], iota_p[:, 0:1], None, ALU.is_equal).then_inc(e3_oT, 1)
                    if old:
                        starts = bases_of(dve, *old)
                    if p2:
                        q, s = p2[0] * 2 + p2[1], p2[1]
                        c = LoopChain(dve, S3["bd"], q, 1 + SOFT, 1 + SOFT_1)
                    if p1:
                        q, s = p1[0] * 2 + p1[1], p1[1]
                        c0 = p1[0] * UT + s * SG
                        c = LoopChain(dve, S3["bd"], q, 1 + SOFT)
                        scores(c, q, s)
                        softmax_dve_0(dve, S3, c, c0, 8)
                    dve.wait_ge(e3_xT, g + 1)
                    for j in range(NZ):
                        m = 128 if j < NZ - 1 else D
                        dve.wait_ge(e3_sh, g * NZ + (j + 1))
                        dve.tensor_tensor(z[0:m, k % 2, j, :], bank[1 + (k * NZ + j) % 2][0:m, :], xT[0:m, :], ALU.mult).then_inc(e3_z, 1)
                        if old and j == 1:
                            add_sums(*old, 0, starts)
                        if old and j == NZ - 1:
                            add_sums(*old, 1, starts)
                        if p1 and j == 2:
                            softmax_dve_1(dve, S3, c, q, 8)
                        if p2 and j == 2:
                            softmax_dve_3(dve, S3, c, q, 8)
                    if p1:
                        softmax_dve_2(dve, S3, c, q, c0, 8)
                    dve.wait_ge(e3_K, g + 1)
                    dve.wait_ge(e3_n[k % 2], i * (UG // 2 * 32) + (k // 2 + 1) * 32)
                    dve.tensor_tensor(kt[:], bank[5][:], wks[:, k % 2, :], ALU.mult).then_inc(e3_kt, 1)
                    dve.wait_ge(e3_kt, g + 1)
                    dve.wait_ge(e3_q, g + 1)
                    dve.tensor_tensor(kt[:], kt[:], qs[:], ALU.mult).then_inc(e3_pr, 1)
                    if p2:
                        exponents(c, q, s)
                    one_hot_ring_step(one, dve, i, k, e3_one)
                    if p2:
                        split_steps(dve, S3, q, s, lambda c: fill(c, s))
                    if back(i, k, LATE - 1):
                        values(*back(i, k, LATE - 1))
                    dve.wait_ge(e3_V, g + 1)
                    dve.tensor_tensor(vw[:, k * GT:(k + 1) * GT, :].rearrange("p t f -> p (t f)"), bank[6][:], wvs[:, k % 2, :],
                                      ALU.mult).then_inc(e3_vw, 1)
                each_group(dve, body)
                values(NI - 1, KG - 1)
                for k in range(UG - LATE, KG):
                    starts = bases_of(dve, NI - 1, k)
                    for half in range(2):
                        add_sums(NI - 1, k, half, starts)
                q, c0 = NI * 2 - 1, NT - SG
                c = LoopChain(dve, S3["bd"], q, 1 + SOFT)
                scores(c, q, 1)
                softmax_dve_0(dve, S3, c, c0, 8)
                softmax_dve_1(dve, S3, c, q, 8)
                softmax_dve_2(dve, S3, c, q, c0, 8)
                softmax_dve_3(dve, S3, c, q, 8)
                exponents(c, q, 1)
                split_steps(dve, S3, q, 1, lambda c: fill(c, 1))
                for k in range(KG, UG):
                    starts = bases_of(dve, NI - 1, k)
                    values(NI - 1, k)
                    for half in range(2):
                        add_sums(NI - 1, k, half, starts)
        layer.close()

        m3_r, m3_b, m3_u, m3_m, m3_c, m3_dve, m3_sd, m3_t, m3_x, m3_o, m3_s = [sem("m3_" + x) for x in
            ("r", "b", "u", "m", "c", "dve", "sd", "t", "x", "o", "s")]
        OT = tmp("OT", [D, N])
        sq = tmp("sq", [D, N])
        rden = tmp("rden", [128, 2, 512])
        bn = tmp("bn", [D, 8])
        CH = rounds(N, 512)
        with nc.Block() as block:
            @block.vector
            def _(dve):
                c = Chain(dve, m3_r)
                for n, (a, w) in enumerate(CH):
                    dve.wait_ge(m3_b, n + 1)
                    r = rden[:, n % 2, 0:w]
                    c.link(dve.tensor_scalar(r, bank[n % 2][:, 0:w], 1e-16, None, ALU.add))
                    c.link(dve.reciprocal(r, r))
                    dve.tensor_tensor(acc[:, 0, a:a + w], acc[:, 0, a:a + w], r, ALU.mult).then_inc(m3_u, 1)
                dve.wait_ge(m3_c, len(CH))
                c = Chain(dve, m3_dve)
                c.link(dve.tensor_reduce(bn[:, 0:1], OT[:], AX.X, ALU.add))
                c.link(dve.tensor_scalar(bn[:, 1:2], bn[:, 0:1], -1.0 / N, None, ALU.mult))
                c.link(dve.tensor_scalar(OT[:], OT[:], bn[:, 1:2], None, ALU.add))
                c.link(dve.tensor_tensor(sq[:], OT[:], OT[:], ALU.mult))
                c.link(dve.tensor_reduce(bn[:, 2:3], sq[:], AX.X, ALU.add))
                c.link(dve.tensor_scalar(bn[:, 3:4], bn[:, 2:3], 1.0 / N, EPS, ALU.mult, ALU.add))
                dve.wait_ge(m3_sd, 1)
                c.link(dve.reciprocal(bn[:, 5:6], bn[:, 4:5]))
                c.link(dve.tensor_tensor(bn[:, 6:7], bn[:, 5:6], gcol[:], ALU.mult))
                c.link(dve.tensor_scalar(OT[:], OT[:], bn[:, 6:7], bcol[:, 0:1], ALU.mult, ALU.add))
                for r, (j0, n) in enumerate(rounds(NJ, 4)):
                    dve.wait_ge(m3_t, r + 1)
                    dve.tensor_tensor(X[:, j0:j0 + n, :], X[:, j0:j0 + n, :],
                                      bank[4 + r % 2][0:PN, 0:n * D].rearrange("p (j f) -> p j f", j=n), ALU.add).then_inc(m3_x, 1)

            @block.tensor
            def _(pe):
                pe.wait_ge(m3_s, 32)
                for n, (a, w) in enumerate(CH):
                    if n >= 2:
                        pe.wait_ge(m3_u, n - 1)
                    pe.matmul(bank[n % 2][:, 0:w], sel_b[:], acc[0:24, 1, a:a + w], start=True, stop=True).then_inc(m3_b, 1)
                    pe.wait_ge(m3_u, n + 1)
                    if n >= 2:
                        pe.wait_ge(m3_c, n - 1)
                    pe.matmul(bank[2 + n % 2][0:D, 0:w], w_self[:], HT[:, a:a + w], start=True, stop=False)
                    pe.matmul(bank[2 + n % 2][0:D, 0:w], w_out[:], acc[:, 0, a:a + w], start=False, stop=True).then_inc(m3_m, 1)
                pe.wait_ge(m3_dve, 9)
                for r, (j0, n) in enumerate(rounds(NJ, 4)):
                    if r >= 2:
                        pe.wait_ge(m3_x, r - 1)
                    for j in range(n):
                        last = pe.transpose(bank[4 + r % 2][0:PN, j * D:(j + 1) * D], OT[:, (j0 + j) * PN:(j0 + j + 1) * PN],
                                            ident[0:D, 0:D])
                    last.then_inc(m3_t, 1)

            @block.scalar
            def _(act):
                for n, (a, w) in enumerate(CH):
                    act.wait_ge(m3_m, n + 1)
                    act.activation(OT[:, a:a + w], bank[2 + n % 2][0:D, 0:w], ACT.Copy).then_inc(m3_c, 1)
                act.wait_ge(m3_dve, 6)
                act.activation(bn[:, 4:5], bn[:, 3:4], ACT.Sqrt).then_inc(m3_sd, 1)

            @block.sync
            def _(sp):
                for part in (1, 2):
                    sp.dma_start(sel_b[8 * part:8 * part + 8, :], sel_b[0:8, :]).then_inc(m3_s, 16)
                o = out.rearrange("(j p) f -> p j f", p=PN)
                for r, (j0, n) in enumerate(rounds(NJ, 4)):
                    sp.wait_ge(m3_x, r + 1)
                    sp.dma_start(o[:, j0:j0 + n, :], X[:, j0:j0 + n, :]).then_inc(m3_o, 16)
                sp.wait_ge(m3_o, 16 * len(rounds(NJ, 4)))
        end_of_layer()


def kernel(**inputs):
    import numpy as np
    import concourse.bacc as bacc
    from concourse.bass_utils import run_bass_kernel_spmd as run

    nc = bacc.Bacc("TRN2", target_bir_lowering=False, num_devices=1)
    a = {k: np.asarray(v) for k, v in inputs.items()}
    fill = EP - E

    def rows(v, value):
        return np.pad(v, (0, fill), constant_values=value)

    a["src"] = rows(a["src"], 0).reshape(NT, W).T
    a["dst"] = rows(a["dst"], -1).reshape(NT, W).T
    dst = a["dst"].T.reshape(-1)
    a["dst_rows"] = dst.reshape(NT, W)
    a["dst_before"] = np.concatenate([np.full(1, -2, dst.dtype), dst[:-1]]).reshape(NT, W).T
    a["rel"] = rows(a.pop("edge_type_8"), 0).reshape(1, EP)
    a["ea16"] = np.pad(a.pop("edge_attr_16"), ((0, fill), (0, 0))).T
    a["ea64"] = np.pad(a.pop("edge_attr_64"), ((0, fill), (0, 0))).T
    a["ea9"] = np.pad(a.pop("edge_attr_9"), ((0, fill), (0, 0))).T
    a["L2_gnn_WT"] = a.pop("L2_gnn_W").T
    for k, v in a.items():
        a[k] = np.ascontiguousarray(v.reshape(1, -1) if v.ndim == 1 else v)
    arrays = {f"in_{k}": v for k, v in a.items()}
    aps = {k: nc.dram_tensor(f"in_{k}", v.shape, mybir.dt.from_np(v.dtype), kind="ExternalInput").ap() for k, v in a.items()}
    out = nc.dram_tensor("out_x", (N, D), F32, kind="ExternalOutput").ap()
    build(nc, aps, out)
    return run(nc, [arrays], core_ids=[0]).results[0]["out_x"]
```
